# Optimizing a Trainium2 kernel written in Bass

```python
import numpy as np
import jax
import jax.numpy as jnp

def _softmax(x, axis=-1):
    return jax.nn.softmax(x, axis=axis)

def _gelu(x):
    return jax.nn.gelu(x, approximate=True)

def _silu(x):
    return jax.nn.silu(x)

def _sigmoid(x):
    return jax.nn.sigmoid(x)

def _layernorm(x, axis=-1, eps=1e-05):
    m = jnp.mean(x, axis=axis, keepdims=True)
    v = jnp.var(x, axis=axis, keepdims=True)
    return (x - m) / jnp.sqrt(v + eps)

def _scatter_add(tgt, idx, src, axis=0):
    return tgt.at[idx].add(src)

def _segment_sum(src, seg, n):
    return jax.ops.segment_sum(src, seg, n)
kernel_name = 'mk_macaron_d1_jaxref_r4_0c7779'

def setup_inputs(seed: int=0):
    np.random.seed(seed)
    _w = jnp.asarray

    def _L0_attn_setup():
        import math
        import jax, jax.numpy as jnp
        import numpy as np
        D_MODEL = 256
        N_HEADS = 16
        D_K = D_MODEL // N_HEADS
        D_C = 64
        B, S = (2, 512)
        key = jax.random.key(seed)
        ks = jax.random.split(key, 7)
        sd = lambda fan_in: 1.0 / math.sqrt(fan_in)
        return {'x': jax.random.normal(ks[0], (B, S, D_MODEL), dtype=jnp.float32), 'W_dq': jax.random.uniform(ks[1], (D_MODEL, D_C), minval=-sd(D_MODEL), maxval=sd(D_MODEL), dtype=jnp.float32), 'W_uq': jax.random.uniform(ks[2], (D_C, N_HEADS * D_K), minval=-sd(D_C), maxval=sd(D_C), dtype=jnp.float32), 'W_dkv': jax.random.uniform(ks[3], (D_MODEL, D_C), minval=-sd(D_MODEL), maxval=sd(D_MODEL), dtype=jnp.float32), 'W_uk': jax.random.uniform(ks[4], (D_C, N_HEADS * D_K), minval=-sd(D_C), maxval=sd(D_C), dtype=jnp.float32), 'W_uv': jax.random.uniform(ks[5], (D_C, N_HEADS * D_K), minval=-sd(D_C), maxval=sd(D_C), dtype=jnp.float32), 'W_o': jax.random.uniform(ks[6], (N_HEADS * D_K, D_MODEL), minval=-sd(N_HEADS * D_K), maxval=sd(N_HEADS * D_K), dtype=jnp.float32)}
    _L0_attn_in = _L0_attn_setup()

    def _L0_ffn_setup():
        import jax, jax.numpy as jnp
        import numpy as np
        E = 8
        K = 2
        S = 1
        THRESHOLD = 0.7
        NORM_TOPK = True
        H = 256
        F = 256
        B, SEQ = (2, 256)
        key = jax.random.key(seed)
        k1, k2, k3, k4, k5 = jax.random.split(key, 5)
        hidden_states = jax.random.normal(k1, (B, SEQ, H), jnp.float32)
        gate_weight = jax.random.normal(k2, (E, H), jnp.float32) * 0.02
        gate_up_proj = jax.random.normal(k3, (E, 2 * F, H), jnp.float32) * 0.02
        down_proj = jax.random.normal(k4, (E, H, F), jnp.float32) * 0.02
        sim = jax.random.uniform(k5, (E, E), jnp.float32)
        sim = (sim + sim.T) / 2.0
        sim = sim.at[jnp.arange(E), jnp.arange(E)].set(1.0)
        return {'hidden_states': hidden_states, 'gate_weight': gate_weight, 'gate_up_proj': gate_up_proj, 'down_proj': down_proj, 'similarity_matrix': sim}
    _L0_ffn_in = _L0_ffn_setup()
    _d = {'L0_attn_x': _L0_attn_in['x'], 'L0_attn_W_dq': _L0_attn_in['W_dq'], 'L0_attn_W_uq': _L0_attn_in['W_uq'], 'L0_attn_W_dkv': _L0_attn_in['W_dkv'], 'L0_attn_W_uk': _L0_attn_in['W_uk'], 'L0_attn_W_uv': _L0_attn_in['W_uv'], 'L0_attn_W_o': _L0_attn_in['W_o'], 'L0_ffn_gate_weight': _L0_ffn_in['gate_weight'], 'L0_ffn_gate_up_proj': _L0_ffn_in['gate_up_proj'], 'L0_ffn_down_proj': _L0_ffn_in['down_proj'], 'L0_ffn_similarity_matrix': _L0_ffn_in['similarity_matrix']}
    _x0 = _d['L0_attn_x']
    _d['L0_attn_x'] = jax.random.normal(jax.random.fold_in(jax.random.key(seed), 1), (4, 1024, 256), dtype=_x0.dtype)
    del _x0
    return _d

def reference(L0_attn_x, L0_attn_W_dq, L0_attn_W_uq, L0_attn_W_dkv, L0_attn_W_uk, L0_attn_W_uv, L0_attn_W_o, L0_ffn_gate_weight, L0_ffn_gate_up_proj, L0_ffn_down_proj, L0_ffn_similarity_matrix):

    def _L0_attn_ref(x, W_dq, W_uq, W_dkv, W_uk, W_uv, W_o):
        import math
        import jax, jax.numpy as jnp
        import numpy as np
        D_MODEL = 256
        N_HEADS = 16
        D_K = D_MODEL // N_HEADS
        D_C = 64
        B, S = (2, 512)
        Bx, Sx, _ = x.shape
        c_q = x @ W_dq
        Q = (c_q @ W_uq).reshape(Bx, Sx, N_HEADS, D_K)
        c_kv = x @ W_dkv
        K = (c_kv @ W_uk).reshape(Bx, Sx, N_HEADS, D_K)
        V = (c_kv @ W_uv).reshape(Bx, Sx, N_HEADS, D_K)
        scores = jnp.einsum('bqhd,bkhd->bhqk', Q, K) / math.sqrt(D_K)
        causal = jnp.tril(jnp.ones((Sx, Sx), dtype=bool))
        scores = jnp.where(causal, scores, -jnp.inf)
        attn = jax.nn.softmax(scores, axis=-1)
        out = jnp.einsum('bhqk,bkhd->bqhd', attn, V).reshape(Bx, Sx, N_HEADS * D_K)
        return out @ W_o

    def _L0_ffn_ref(hidden_states, gate_weight, gate_up_proj, down_proj, similarity_matrix):
        import jax, jax.numpy as jnp
        import numpy as np
        E = 8
        K = 2
        S = 1
        THRESHOLD = 0.7
        NORM_TOPK = True
        H = 256
        F = 256
        B, SEQ = (2, 256)
        b, s, h = hidden_states.shape
        x = hidden_states.reshape(-1, h)
        N = x.shape[0]
        logits = x @ gate_weight.T
        probs = jax.nn.softmax(logits.astype(jnp.float32), axis=-1)
        top_w, top_i = jax.lax.top_k(probs, K)
        if NORM_TOPK:
            top_w = top_w / jnp.clip(jnp.sum(top_w, -1, keepdims=True), 1e-12)
        primary_mask = jnp.zeros((E,), bool).at[top_i[:, :S].reshape(-1)].set(True)
        sim = jnp.where(primary_mask[None, :], similarity_matrix.astype(jnp.float32), -jnp.inf)
        best_j = jnp.argmax(sim, axis=-1)
        best_sim = jnp.max(sim, axis=-1)
        ids = jnp.arange(E)
        expert_map = jnp.where(~primary_mask & (best_sim >= THRESHOLD), best_j, ids)
        rerouted = expert_map[top_i]
        rows = jnp.arange(N)[:, None]
        dense = jnp.zeros((N, E), top_w.dtype).at[rows, rerouted].add(top_w)
        fw, fi = jax.lax.top_k(dense, K)
        combine = jnp.zeros((N, E), fw.dtype).at[rows, fi].add(jnp.where(fw > 0, fw, 0.0))
        gu = jnp.einsum('nh,efh->enf', x, gate_up_proj)
        g, u = jnp.split(gu, 2, axis=-1)
        hmid = jax.nn.silu(g) * u
        y = jnp.einsum('enf,ehf->enh', hmid, down_proj)
        out = jnp.einsum('ne,enh->nh', combine, y)
        return out.reshape(b, s, h)
    x = L0_attn_x
    x = x + 0.5 * _L0_ffn_ref(_layernorm(x, axis=-1), L0_ffn_gate_weight, L0_ffn_gate_up_proj, L0_ffn_down_proj, L0_ffn_similarity_matrix)
    x = x + _L0_attn_ref(_layernorm(x, axis=-1), L0_attn_W_dq, L0_attn_W_uq, L0_attn_W_dkv, L0_attn_W_uk, L0_attn_W_uv, L0_attn_W_o)
    x = x + 0.5 * _L0_ffn_ref(_layernorm(x, axis=-1), L0_ffn_gate_weight, L0_ffn_gate_up_proj, L0_ffn_down_proj, L0_ffn_similarity_matrix)
    return x

_drawn_inputs = setup_inputs


def setup_inputs(seed=0):
    import zlib

    import numpy as np

    out = dict(_drawn_inputs(seed))
    spreads = {}
    factors = {'L0_attn_W_dq': 8.0,
     'L0_attn_W_uq': 8.0,
     'L0_attn_W_dkv': 3.416,
     'L0_attn_W_uk': 8.0,
     'L0_attn_W_uv': 3.472,
     'L0_attn_W_o': 3.519,
     'L0_ffn_gate_weight': 5.39,
     'L0_ffn_gate_up_proj': 4.695,
     'L0_ffn_down_proj': 4.695}
    for name, (base, spread) in spreads.items():
        noise = np.random.default_rng([zlib.crc32(name.encode()), seed]).standard_normal(out[name].shape)
        drawn = base * np.exp(spread * noise) if base else spread * noise
        out[name] = jnp.asarray(drawn.astype(out[name].dtype))
    for name, factor in factors.items():
        out[name] = (out[name] * factor).astype(out[name].dtype)
    return out
```

```python
from contextlib import ExitStack

import concourse.bass as bass
from concourse import mybir

F32 = mybir.dt.float32
BF16 = mybir.dt.bfloat16
F16 = mybir.dt.float16
I32 = mybir.dt.int32
ALU = mybir.AluOpType
ACT = mybir.ActivationFunctionType
AX_X = mybir.AxisListType.X

P = 128
B, S, D = 4, 1024, 256
N = B * S
NT = N // P
DC = D // P
E = 8
F = 256
TOPK = 2
SLOTC = TOPK * NT
U = 4
MT = TOPK * N // P + E
H, DK, DL = 16, 16, 64
HG = 4
NG = B * H // HG
QT = S // P
BIG = 3.0e38
NEG = -1.0e30
EPS = 1e-5
THRESHOLD = 0.7
HALF = 0.5
PARTS = 3
Q_PARTS = (0, 0, 0, 1, 1, 2)
K_PARTS = (0, 1, 2, 0, 1, 0)
KROWS = len(Q_PARTS) * DK
MROWS = KROWS + PARTS
VW = 32
SLOTS = 3


def wait(eng, sem, value):
    if not isinstance(value, int) or value > 0:
        eng.wait_ge(sem, value)


def hold(eng, sem, value, T):
    wait(eng, sem, value)
    if not isinstance(value, int):
        eng.sem_inc(T.holds_passed[eng.engine], 1)


class Chain:

    def __init__(self, eng, sem):
        self.eng, self.sem, self.n = eng, sem, 0

    def link(self, ins):
        self.n += 1
        ins.then_inc(self.sem, 1)
        self.eng.wait_ge(self.sem, self.n)


class Mem:

    def __init__(self, nc, ctx, tag):
        self.nc, self.ctx, self.tag = nc, ctx, tag

    def sb(self, name, shape, dt=F32):
        return self.ctx.enter_context(self.nc.sbuf_tensor(f"{self.tag}_{name}", shape, dt))

    def ps(self, name, shape, dt=F32):
        return self.ctx.enter_context(self.nc.psum_tensor(f"{self.tag}_{name}", shape, dt))

    def sem(self, name):
        return self.ctx.enter_context(self.nc.semaphore(f"{self.tag}_{name}"))


def bc(ap, axis, shape):
    return ap.unsqueeze(axis).to_broadcast(shape)


def layernorm_stats(nc, dve, act, M):
    stats = M.sb("stats", [P, NT, 6])
    mean, rstd = M.sb("mean", [P, NT]), M.sb("rstd", [P, NT])
    tmp = M.sb("lntmp", [P, 4, NT])
    stats_sem, var_ready, std_ready, chain_sem = (M.sem(n) for n in ("stats", "var_ready", "std_ready", "lnchain"))
    return stats, mean, rstd, tmp, stats_sem, var_ready, std_ready, chain_sem


def dve_stats(nc, dve, x, ln):
    stats, mean, rstd, tmp, stats_sem, var_ready, std_ready, chain_sem = ln
    with dve.Fori(0, NT // U) as it:
        for s in range(U):
            nc.vector.bn_stats(stats[:, bass.ds(it * U + s, 1), :], x[:, bass.ds(it * U + s, 1), :]).then_inc(stats_sem, 1)
    dve.wait_ge(stats_sem, NT)
    c = Chain(dve, chain_sem)
    even_mean, odd_mean, even_m2, odd_m2 = (stats[:, :, k] for k in (1, 4, 2, 5))
    nc.vector.tensor_tensor(tmp[:, 0], even_mean, odd_mean, ALU.add)
    nc.vector.tensor_tensor(tmp[:, 1], even_mean, odd_mean, ALU.subtract)
    c.link(nc.vector.tensor_tensor(tmp[:, 2], even_m2, odd_m2, ALU.add))
    nc.vector.tensor_scalar(mean[:], tmp[:, 0], 0.5, None, ALU.mult)
    c.link(nc.vector.tensor_tensor(tmp[:, 3], tmp[:, 1], tmp[:, 1], ALU.mult))
    c.link(nc.vector.tensor_scalar(tmp[:, 0], tmp[:, 2], 1.0 / D, EPS, ALU.mult, ALU.add))
    nc.vector.scalar_tensor_tensor(tmp[:, 1], tmp[:, 3], 0.25, tmp[:, 0], ALU.mult, ALU.add).then_inc(var_ready, 1)
    dve.wait_ge(std_ready, 1)
    c.link(nc.vector.reciprocal(rstd[:], tmp[:, 2]))


def act_std(nc, act, ln):
    tmp, var_ready, std_ready = ln[3], ln[5], ln[6]
    act.wait_ge(var_ready, 1)
    nc.scalar.activation(tmp[:, 2], tmp[:, 1], ACT.Sqrt).then_inc(std_ready, 1)


def phase_logits(nc, T, tag, x, xn_dram, logits, loads=None):
    with ExitStack() as ctx:
        M = Mem(nc, ctx, tag)
        ln = layernorm_stats(nc, None, None, M)
        mean, rstd = ln[1], ln[2]
        xn = M.sb("xn", [P, U, D])
        xT = M.sb("xT", [P, 2, DC, P])
        psT = [M.ps(f"psT{i}", [P, 512]) for i in range(2)]
        psL = M.ps("psL", [P, 512])
        xn_ready, xn_stored, t_done, xT_ready, l_done, l_copied = (
            M.sem(n) for n in ("xn_ready", "xn_stored", "t_done", "xT_ready", "l_done", "l_copied"))
        xn_view = xn_dram.rearrange("(n p) d -> p n d", p=P)
        block = ctx.enter_context(nc.Block())

        @block.sync
        def _(sp):
            if loads:
                loads(sp)

            def store(it):
                hold(sp, xn_ready, it * U + U, T)
                sp.dma_start(xn_view[:, bass.ds(it * U, U), :], xn[:]).then_inc(xn_stored, 16)

            with sp.Fori(0, NT // U) as it:
                store(it)
            hold(sp, xn_stored, 16 * (NT // U), T)

        @block.vector
        def _(dve):
            if loads:
                dve.wait_ge(T.x_loaded, 64)
            dve_stats(nc, dve, x, ln)

            def normalise(it, first):
                if not first:
                    dve.wait_ge(xn_stored, it * 16)
                for s in range(U):
                    if not first:
                        dve.wait_ge(t_done, it * U + s + 1 - U)
                    nc.vector.tensor_scalar(xn[:, s, :], x[:, bass.ds(it * U + s, 1), :],
                                            mean[:, bass.ds(it * U + s, 1)], rstd[:, bass.ds(it * U + s, 1)],
                                            ALU.subtract, ALU.mult).then_inc(xn_ready, 1)

            normalise(0, True)
            with dve.Fori(1, NT // U) as it:
                normalise(it, False)

        @block.tensor
        def _(pe):
            pe.wait_ge(T.const_ready, T.N_CONST)
            if loads:
                pe.wait_ge(T.w_loaded, T.N_W)

            def transposes(it, s):
                n = it * U + s
                pe.wait_ge(xn_ready, n + 1)
                wait(pe, xT_ready, n - 1)
                for c in range(DC):
                    ins = nc.tensor.transpose(psT[s % 2][:, c * P:(c + 1) * P], xn[:, s, c * P:(c + 1) * P], T.ident[:])
                ins.then_inc(t_done, 1)

            def scores(it, s):
                n = it * U + s
                pe.wait_ge(xT_ready, n + 1)
                if s == 0:
                    wait(pe, l_copied, it)
                for c in range(DC):
                    ins = nc.tensor.matmul(psL[:, s * E:(s + 1) * E], xT[:, s % 2, c, :], T.gateT[:, c, :],
                                           start=(c == 0), stop=(c == DC - 1))
                ins.then_inc(l_done, 1)

            def body(it):
                transposes(it, 0)
                for s in range(U):
                    if s + 1 < U:
                        transposes(it, s + 1)
                    scores(it, s)

            body(0)
            with pe.Fori(1, NT // U) as it:
                body(it)

        @block.scalar
        def _(act):
            act_std(nc, act, ln)

            def body(it):
                for s in range(U):
                    n = it * U + s
                    act.wait_ge(t_done, n + 1)
                    wait(act, l_done, n - 1)
                    nc.scalar.copy(xT[:, s % 2, :, :], psT[s % 2][:, 0:D].rearrange("p (c t) -> p c t", c=DC)).then_inc(xT_ready, 1)
                act.wait_ge(l_done, it * U + U)
                nc.scalar.copy(logits[:, bass.ds(it * U, U), :],
                               psL[:, 0:U * E].rearrange("p (s e) -> p s e", s=U)).then_inc(l_copied, 1)

            body(0)
            with act.Fori(1, NT // U) as it:
                body(it)


def phase_route(nc, T, tag, logits, R):
    with ExitStack() as ctx:
        M = Mem(nc, ctx, tag)
        shape = [P, NT, E]
        top = [M.sb(f"top{k}", [P, NT]) for k in range(TOPK)]
        choice = [M.sb(f"choice{k}", [P, NT]) for k in range(TOPK)]
        picked = M.sb("picked", [P, TOPK, NT, E])
        work = M.sb("work", [P, NT, E])
        rest = M.sb("rest", [P, NT, E])
        gap, expgap, den = (M.sb(n, [P, NT]) for n in ("gap", "expgap", "den"))
        primary, masked, unmasked = (M.sb(n, [P, E]) for n in ("primary", "masked", "unmasked"))
        sim, simw = M.sb("sim", [P, E, E]), M.sb("simw", [P, E, E])
        best, best_j, moved, emap = (M.sb(n, [P, E]) for n in ("best", "best_j", "moved", "emap"))
        target = M.sb("target", [P, SLOTC])
        routed, routed_bf = M.sb("routed", [P, SLOTC, E]), M.sb("routed_bf", [P, SLOTC, E], BF16)
        big = M.sb("big", [P, SLOTC, E])
        upto = M.sb("upto", [P, SLOTC, E])
        ones = M.sb("ones", [P, SLOTC])
        zeros = M.sb("zeros", [P, MT], F16)
        counts_i, tiles_i = M.sb("counts_i", [P, E], I32), M.sb("tiles_i", [P, E], I32)
        tiles, tiles_end, row0 = (M.sb(n, [P, E]) for n in ("tiles", "tiles_end", "row0"))
        place = M.sb("place", [P, SLOTC])
        lane_i, tile_i = M.sb("lane_i", [P, SLOTC], I32), M.sb("tile_i", [P, SLOTC], I32)
        lane, tile = M.sb("lane", [P, SLOTC]), M.sb("tile", [P, SLOTC])
        ended = M.sb("ended", [P, MT, E])
        expert_f = M.sb("expert_f", [P, MT])
        lane_hot = M.sb("lane_hot", [P, U, P], F16)
        tile_tok = M.sb("tile_tok", [P, U, MT], F16)
        ps_count, ps_before, ps_total, ps_table = (M.ps(n, [P, 512]) for n in ("ps_count", "ps_before", "ps_total", "ps_table"))
        chain_sem, gap_ready, exp_ready, first_ready, counted, routed_ready, ranked, hot_ready, hot_used, table_done = (
            M.sem(n) for n in ("chain", "gap_ready", "exp_ready", "first_ready", "counted", "routed_ready", "ranked",
                               "hot_ready", "hot_used", "table_done"))
        block = ctx.enter_context(nc.Block())
        iota_e = T.iota[:, 0:E]

        @block.scalar
        def _(act):
            act.wait_ge(gap_ready, 1)
            nc.scalar.activation(expgap[:], gap[:], ACT.Exp).then_inc(exp_ready, 1)

        @block.vector
        def _(dve):
            c = Chain(dve, chain_sem)
            v = nc.vector
            c.link(v.memset(ones[:], 1.0))
            c.link(v.memset(zeros[:], 0.0))
            src = logits
            for k in range(TOPK):
                c.link(v.tensor_reduce(top[k][:], src[:], AX_X, ALU.max))
                c.link(v.tensor_tensor(work[:], src[:], bc(top[k][:], 2, shape), ALU.not_equal))
                c.link(v.scalar_tensor_tensor(work[:], work[:], float(E), bc(iota_e, 1, shape), ALU.mult, ALU.add))
                c.link(v.tensor_reduce(choice[k][:], work[:], AX_X, ALU.min))
                ins = v.tensor_tensor(picked[:, k], bc(iota_e, 1, shape), bc(choice[k][:], 2, shape), ALU.is_equal)
                ins.then_inc(chain_sem, 1)
                c.n += 1
                dve.wait_ge(chain_sem, c.n)
                if k == 0:
                    c.link(v.scalar_tensor_tensor(rest[:], picked[:, 0], -BIG, logits[:], ALU.mult, ALU.add))
                    v.tensor_copy(work[:], picked[:, 0]).then_inc(first_ready, 1)
                    dve.wait_ge(first_ready, 1)
                    dve.wait_ge(counted, 1)
                    src = rest
            v.tensor_tensor(gap[:], top[1][:], top[0][:], ALU.subtract).then_inc(gap_ready, 1)
            dve.wait_ge(exp_ready, 1)
            c.link(v.tensor_scalar(den[:], expgap[:], 1.0, None, ALU.add))
            c.link(v.reciprocal(gap[:], den[:]))
            v.tensor_scalar(R.weight[:, 0], gap[:], HALF, None, ALU.mult)
            c.link(v.scalar_tensor_tensor(R.weight[:, 1], expgap[:], HALF, gap[:], ALU.mult, ALU.mult))
            c.link(v.tensor_reduce(primary[:], ps_count[:, 0:NT * E].rearrange("p (n e) -> p e n", e=E), AX_X, ALU.add))
            c.link(v.tensor_scalar(primary[:], primary[:], 1.0, None, ALU.min))
            v.tensor_scalar(unmasked[:], primary[:], -1.0, 1.0, ALU.mult, ALU.add)
            c.link(v.tensor_scalar(masked[:], primary[:], BIG, -BIG, ALU.mult, ALU.add))
            ee = [P, E, E]
            c.link(v.tensor_tensor(sim[:], T.simb[:], bc(primary[:], 1, ee), ALU.mult))
            c.link(v.tensor_tensor(sim[:], sim[:], bc(masked[:], 1, ee), ALU.add))
            c.link(v.tensor_reduce(best[:], sim[:], AX_X, ALU.max))
            c.link(v.tensor_tensor(simw[:], sim[:], bc(best[:], 2, ee), ALU.not_equal))
            c.link(v.scalar_tensor_tensor(simw[:], simw[:], float(E), bc(iota_e, 1, ee), ALU.mult, ALU.add))
            c.link(v.tensor_reduce(best_j[:], simw[:], AX_X, ALU.min))
            c.link(v.scalar_tensor_tensor(moved[:], best[:], THRESHOLD, unmasked[:], ALU.is_ge, ALU.mult))
            c.link(v.tensor_tensor(best_j[:], best_j[:], iota_e, ALU.subtract))
            c.link(v.tensor_tensor(best_j[:], best_j[:], moved[:], ALU.mult))
            c.link(v.tensor_tensor(emap[:], best_j[:], iota_e, ALU.add))
            full = [P, SLOTC, E]
            c.link(v.tensor_tensor(big[:], picked[:].rearrange("p k n e -> p (k n) e"), bc(emap[:], 1, full), ALU.mult))
            c.link(v.tensor_reduce(target[:], big[:], AX_X, ALU.add))
            c.link(v.tensor_tensor(routed[:], bc(iota_e, 1, full), bc(target[:], 2, full), ALU.is_equal))
            v.tensor_copy(routed_bf[:], routed[:]).then_inc(routed_ready, 1)
            dve.wait_ge(ranked, 1)
            before = ps_before[:].rearrange("p (c e) -> p c e", e=E)
            total = ps_total[:].rearrange("p (c e) -> p c e", e=E)
            for e in range(E):
                ins = v.tensor_tensor_scan(upto[:, :, e], ones[:], total[:, :, e], 0.0, ALU.mult, ALU.add)
                c.n += 1
                ins.then_inc(chain_sem, 1)
            dve.wait_ge(chain_sem, c.n)
            c.link(v.tensor_scalar(counts_i[:], upto[:, SLOTC - 1, :], float(P - 1), None, ALU.add))
            c.link(v.tensor_scalar(tiles_i[:], counts_i[:], P.bit_length() - 1, None, ALU.logical_shift_right))
            c.link(v.tensor_copy(tiles[:], tiles_i[:]))
            c.link(v.tensor_tensor_scan(tiles_end[:], ones[:, 0:E], tiles[:], 0.0, ALU.mult, ALU.add))
            c.link(v.tensor_tensor(row0[:], tiles_end[:], tiles[:], ALU.subtract))
            c.link(v.tensor_scalar(row0[:], row0[:], float(P), None, ALU.mult))
            c.link(v.tensor_tensor(big[:], upto[:], total, ALU.subtract))
            c.link(v.tensor_tensor(big[:], big[:], before, ALU.add))
            c.link(v.tensor_tensor(big[:], big[:], bc(row0[:], 1, full), ALU.add))
            c.link(v.tensor_tensor(big[:], big[:], routed[:], ALU.mult))
            c.link(v.tensor_reduce(place[:], big[:], AX_X, ALU.add))
            c.link(v.tensor_copy(R.place[:], place[:]))
            v.tensor_scalar(lane_i[:], R.place[:], P - 1, None, ALU.bitwise_and)
            c.link(v.tensor_scalar(tile_i[:], R.place[:], P.bit_length() - 1, None, ALU.logical_shift_right))
            v.tensor_copy(lane[:], lane_i[:])
            c.link(v.tensor_copy(tile[:], tile_i[:]))
            te = [P, MT, E]
            c.link(v.tensor_tensor(ended[:], bc(T.iota[:, 0:MT], 2, te), bc(tiles_end[:], 1, te), ALU.is_ge))
            c.link(v.tensor_reduce(expert_f[:], ended[:], AX_X, ALU.add))
            c.link(v.tensor_scalar(R.expert[:], expert_f[0:1, :], float(E - 1), None, ALU.min))

            def hot(it):
                for s in range(U):
                    col = bass.ds(it * U + s, 1)
                    wait(dve, hot_used, it * U + s + 1 - U)
                    v.tensor_scalar(lane_hot[:, s, :], T.iota_h[:, 0:P], lane[:, col], None, ALU.is_equal).then_inc(hot_ready, 1)
                    v.tensor_scalar(tile_tok[:, s, :], T.iota_h[:, 0:MT], tile[:, col], T.token[:, col],
                                    ALU.is_equal, ALU.mult).then_inc(hot_ready, 1)

            hot(0)
            with dve.Fori(1, SLOTC // U) as it:
                hot(it)
            dve.wait_ge(table_done, 1)
            c.link(v.tensor_scalar(R.table[:], ps_table[:, 0:MT], float(N // 2), None, ALU.add))

        @block.tensor
        def _(pe):
            pe.wait_ge(first_ready, 1)
            nc.tensor.matmul(ps_count[:, 0:NT * E], T.ones_f[:], work[:].rearrange("p n e -> p (n e)"),
                             start=True, stop=True).then_inc(counted, 1)
            pe.wait_ge(routed_ready, 1)
            rhs = routed_bf[:].rearrange("p c e -> p (c e)")
            nc.tensor.matmul(ps_before[:], T.lower_bf[:], rhs, start=True, stop=True)
            nc.tensor.matmul(ps_total[:], T.ones_bf[:], rhs, start=True, stop=True).then_inc(ranked, 1)
            pe.wait_ge(hot_ready, 1)
            nc.tensor.matmul(ps_table[:, 0:MT], lane_hot[:, 0, :], zeros[:], start=True, stop=False)

            def add(it):
                for s in range(U):
                    pe.wait_ge(hot_ready, it * (2 * U) + (2 * s + 2))
                    ins = nc.tensor.matmul(ps_table[:, 0:MT], lane_hot[:, s, :], tile_tok[:, s, :], start=False, stop=False)
                    ins.then_inc(hot_used, 1)
            add(0)
            with pe.Fori(1, SLOTC // U) as it:
                add(it)
            nc.tensor.matmul(ps_table[:, 0:MT], lane_hot[:, U - 1, :], zeros[:], start=False, stop=True).then_inc(table_done, 1)


def phase_experts(nc, T, tag, R, xn_dram, y_dram):
    with ExitStack() as ctx:
        M = Mem(nc, ctx, tag)
        index = M.sb("index", [P, U], I32)
        xg = M.sb("xg", [P, U, D])
        xT = M.sb("xT", [P, 2, DC, P])
        sg = M.sb("sg", [P, 2, F])
        hid = M.sb("hid", [P, 2, F])
        hT = M.sb("hT", [P, 2, DC, P])
        y = M.sb("y", [P, U, D])
        psX, psH = M.ps("psX", [P, 512]), M.ps("psH", [P, 512])
        psG = [M.ps(f"psG{i}", [P, 512]) for i in range(2)]
        psY = [M.ps(f"psY{i}", [P, 512]) for i in range(2)]
        x_loaded = [M.sem(f"x_loaded{s}") for s in range(U)]
        y_stored = [M.sem(f"y_stored{s}") for s in range(U)]
        index_ready, xt_done, xT_ready, gu_done, sg_ready, hid_ready, ht_done, hT_ready, y_done, y_ready = (
            M.sem(n) for n in ("index_ready", "xt_done", "xT_ready", "gu_done", "sg_ready", "hid_ready", "ht_done",
                               "hT_ready", "y_done", "y_ready"))
        ITS = MT // U
        y_view = y_dram.rearrange("(t p) d -> p t d", p=P)
        block = ctx.enter_context(nc.Block())

        def steps(eng, body):
            body(0, False)
            with eng.Fori(1, ITS - 1) as it:
                body(it, False)
            body(ITS - 1, True)

        @block.gpsimd
        def _(pool):
            def body(it, last):
                for s in range(U):
                    t = it * U + s
                    hold(pool, xt_done, t + 1 - U, T)
                    nc.gpsimd.tensor_copy(index[:, s:s + 1], R.table[:, bass.ds(t, 1)]).then_inc(index_ready, 1)
                    hold(pool, index_ready, t + 1, T)
                    nc.gpsimd.indirect_dma_start(xg[:, s, :], None, xn_dram,
                                                 bass.IndirectOffsetOnAxis(ap=index[:, s:s + 1], axis=0)).then_inc(x_loaded[s], 16)
            steps(pool, body)

        @block.tensor
        def _(pe):
            def transpose_x(it, s):
                t = it * U + s
                pe.wait_ge(x_loaded[s], it * 16 + 16)
                wait(pe, xT_ready, t)
                for c in range(DC):
                    ins = nc.tensor.transpose(psX[:, c * P:(c + 1) * P], xg[:, s, c * P:(c + 1) * P], T.ident[:])
                ins.then_inc(xt_done, 1)

            def transpose_h(t, s):
                pe.wait_ge(hid_ready, t + 1)
                wait(pe, hT_ready, t)
                for c in range(DC):
                    ins = nc.tensor.transpose(psH[:, c * P:(c + 1) * P], hid[:, s % 2, c * P:(c + 1) * P], T.ident[:])
                ins.then_inc(ht_done, 1)

            def gate_up(t, s, e):
                pe.wait_ge(xT_ready, t + 1)
                wait(pe, hid_ready, t - 1)
                for c in range(DC):
                    ins = nc.tensor.matmul(psG[s % 2][:], xT[:, s % 2, c, :], T.wgu[:, c, bass.ds(e, 1), :].rearrange("p a f -> p (a f)"),
                                           start=(c == 0), stop=(c == DC - 1))
                ins.then_inc(gu_done, 1)

            def down(t, s, e):
                pe.wait_ge(hT_ready, t + 1)
                wait(pe, y_ready, t - 1)
                for c in range(DC):
                    ins = nc.tensor.matmul(psY[s % 2][:, 0:D], hT[:, s % 2, c, :], T.wd[:, c, bass.ds(e, 1), :].rearrange("p a f -> p (a f)"),
                                           start=(c == 0), stop=(c == DC - 1))
                ins.then_inc(y_done, 1)

            def expert(t):
                return pe.value_load(R.expert[0:1, bass.ds(t, 1)], min_val=0, max_val=E - 1)

            def body(it, last):
                for s in range(U):
                    t = it * U + s
                    if not (last and s == U - 1):
                        transpose_x(it + (s + 1) // U, (s + 1) % U)
                    if not (isinstance(t, int) and t == 0):
                        transpose_h(t - 1, s + 1)
                    gate_up(t, s, expert(t))
                    if not (isinstance(t, int) and t == 0):
                        down(t - 1, s + 1, expert(t - 1))

            transpose_x(0, 0)
            steps(pe, body)
            transpose_h(MT - 1, MT - 1)
            down(MT - 1, MT - 1, expert(MT - 1))

        @block.scalar
        def _(act):
            def copy_x(t, s):
                act.wait_ge(xt_done, t + 1)
                wait(act, gu_done, t - 1)
                nc.scalar.copy(xT[:, s % 2, :, :], psX[:, 0:D].rearrange("p (c t) -> p c t", c=DC)).then_inc(xT_ready, 1)

            def copy_y(it, s, t):
                act.wait_ge(y_done, t + 1)
                wait(act, y_stored[s], it * 16)
                nc.scalar.copy(y[:, s, :], psY[s % 2][:, 0:D]).then_inc(y_ready, 1)

            def body(it, last):
                for s in range(U):
                    t = it * U + s
                    if not (last and s == U - 1):
                        copy_x(t + 1, s + 1)
                    act.wait_ge(gu_done, t + 1)
                    wait(act, hid_ready, t - 1)
                    nc.scalar.activation(sg[:, s % 2, :], psG[s % 2][:, 0:F], ACT.Silu).then_inc(sg_ready, 1)
                    if not (isinstance(t, int) and t == 0):
                        copy_y(it - (s == 0), (s - 1) % U, t - 1)

            copy_x(0, 0)
            steps(act, body)
            copy_y(ITS - 1, U - 1, MT - 1)

        @block.vector
        def _(dve):
            def copy_h(t, s):
                dve.wait_ge(ht_done, t + 1)
                wait(dve, y_done, t - 1)
                nc.vector.tensor_copy(hT[:, s % 2, :, :], psH[:, 0:D].rearrange("p (c t) -> p c t", c=DC)).then_inc(hT_ready, 1)

            def body(it, last):
                for s in range(U):
                    t = it * U + s
                    if not (isinstance(t, int) and t == 0):
                        copy_h(t - 1, s + 1)
                    dve.wait_ge(sg_ready, t + 1)
                    wait(dve, ht_done, t - 1)
                    nc.vector.tensor_tensor(hid[:, s % 2, :], sg[:, s % 2, :], psG[s % 2][:, F:2 * F], ALU.mult).then_inc(hid_ready, 1)

            steps(dve, body)
            copy_h(MT - 1, MT - 1)

        @block.sync
        def _(sp):
            def body(it, last):
                for s in range(U):
                    t = it * U + s
                    hold(sp, y_ready, t + 1, T)
                    sp.dma_start(y_view[:, bass.ds(t, 1), :], y[:, s:s + 1, :]).then_inc(y_stored[s], 16)
            steps(sp, body)
            for s in range(U):
                hold(sp, y_stored[s], 16 * ITS, T)


def phase_combine(nc, T, tag, R, x, y_dram, out=None):
    with ExitStack() as ctx:
        M = Mem(nc, ctx, tag)
        index = M.sb("index", [P, U, TOPK], I32)
        yg = M.sb("yg", [P, U, TOPK, D])
        y_loaded = [M.sem(f"y_loaded{s}") for s in range(U)]
        index_ready, first_added, added, stored = (M.sem(n) for n in ("index_ready", "first_added", "added", "stored"))
        ITS = NT // U
        block = ctx.enter_context(nc.Block())

        @block.gpsimd
        def _(pool):
            def body(it):
                for s in range(U):
                    n = it * U + s
                    hold(pool, added, n + 1 - U, T)
                    for k in range(TOPK):
                            nc.gpsimd.tensor_copy(index[:, s, k:k + 1], R.place[:, bass.ds(n + k * NT, 1)]).then_inc(index_ready, 1)
                    hold(pool, index_ready, n * TOPK + TOPK, T)
                    for k in range(TOPK):
                            nc.gpsimd.indirect_dma_start(yg[:, s, k, :], None, y_dram,
                                                     bass.IndirectOffsetOnAxis(ap=index[:, s, k:k + 1], axis=0)).then_inc(y_loaded[s], 16)
            body(0)
            with pool.Fori(1, ITS) as it:
                body(it)

        @block.vector
        def _(dve):
            with dve.Fori(0, ITS) as it:
                for s in range(U):
                    n = it * U + s
                    row = x[:, bass.ds(n, 1), :].rearrange("p a d -> p (a d)")
                    dve.wait_ge(y_loaded[s], it * (16 * TOPK) + 16 * TOPK)
                    nc.vector.scalar_tensor_tensor(row, yg[:, s, 0, :], R.weight[:, 0, bass.ds(n, 1)], row,
                                                   ALU.mult, ALU.add).then_inc(first_added, 1)
                    dve.wait_ge(first_added, n + 1)
                    nc.vector.scalar_tensor_tensor(row, yg[:, s, 1, :], R.weight[:, 1, bass.ds(n, 1)], row,
                                                   ALU.mult, ALU.add).then_inc(added, 1)

        if out is not None:
            out_view = out.rearrange("(n p) d -> p n d", p=P)

            @block.sync
            def _(sp):
                with sp.Fori(0, ITS) as it:
                    hold(sp, added, it * U + U, T)
                    sp.dma_start(out_view[:, bass.ds(it * U, U), :], x[:, bass.ds(it * U, U), :]).then_inc(stored, 16)
                hold(sp, stored, 16 * ITS, T)


def phase_qkv(nc, T, tag, x, qk_dram, v_dram):
    with ExitStack() as ctx:
        M = Mem(nc, ctx, tag)
        ln = layernorm_stats(nc, None, None, M)
        mean, rstd = ln[1], ln[2]
        W = U * P
        CH = N // W
        NU = 4
        xn = M.sb("xn", [P, U, D])
        xT = M.sb("xT", [P, DC, W])
        cT = M.sb("cT", [P, W])
        parts = M.sb("parts", [P, NU, PARTS, W], BF16)
        left = M.sb("left", [P, 2, W])
        vx = M.sb("vx", [P, U, H, VW])
        psT = [M.ps(f"psT{i}", [P, 512]) for i in range(DC)]
        psC = M.ps("psC", [P, 512])
        psU = [M.ps(f"psU{i}", [P, 512]) for i in range(2)]
        psV = [M.ps(f"psV{i}", [P, 512]) for i in range(2)]
        wset, wl = M.sem("vset"), M.sem("w_loaded")
        xn_ready, t_done, xT_ready, c_done, cT_ready, u_done, high_ready, left_ready, mid_ready, low_ready, v_done, v_ready, v_stored = (
            M.sem(n) for n in ("xn_ready", "t_done", "xT_ready", "c_done", "cT_ready", "u_done", "high_ready", "left_ready",
                               "mid_ready", "low_ready", "v_done", "v_ready", "v_stored"))
        parts_stored = [M.sem(f"parts_stored{u}") for u in range(NU)]
        v_view = v_dram.rearrange("(n p) w -> p n w", p=P)
        block = ctx.enter_context(nc.Block())

        @block.sync
        def _(sp):
            def body(it):
                for u in range(NU):
                    hold(sp, low_ready, it * NU + u + 1, T)
                    rows = slice((u % 2) * P, (u % 2) * P + P)
                    sp.dma_start(qk_dram[u // 2, :, rows, bass.ds(it * W, W)].rearrange("a p t -> p a t"),
                                 parts[:, u]).then_inc(parts_stored[u], 16)
                hold(sp, v_ready, it * 2 + 2, T)
                sp.dma_start(v_view[:, bass.ds(it * U, U), :], vx[:].rearrange("p n h w -> p n (h w)")).then_inc(v_stored, 16)
            with sp.Fori(0, CH) as it:
                body(it)
            for u in range(NU):
                hold(sp, parts_stored[u], 16 * CH, T)
            hold(sp, v_stored, 16 * CH, T)

        @block.gpsimd
        def _(pool):
            nc.gpsimd.memset(vx[:], 0.0).then_inc(wset, 1)
            hold(pool, wset, 1, T)
            nc.gpsimd.memset(vx[:, :, :, DK:DK + 1], 1.0).then_inc(wset, 1)

            def body(it):
                for u in range(NU):
                    r = it * NU + u
                    hold(pool, left_ready, r + 1, T)
                    hold(pool, parts_stored[u], it * 16, T)
                    nc.gpsimd.tensor_copy(parts[:, u, 1, :], left[:, u % 2, :]).then_inc(mid_ready, 1)
                    hold(pool, mid_ready, r + 1, T)
                    nc.gpsimd.tensor_tensor(parts[:, u, 2, :], left[:, u % 2, :], parts[:, u, 1, :],
                                            ALU.subtract).then_inc(low_ready, 1)
            body(0)
            with pool.Fori(1, CH) as it:
                body(it)

        @block.vector
        def _(dve):
            dve_stats(nc, dve, x, ln)

            def normalise(it):
                for s in range(U):
                    n = bass.ds(it * U + s, 1)
                    wait(dve, t_done, it)
                    nc.vector.tensor_scalar(xn[:, s, :], x[:, n, :], mean[:, n], rstd[:, n],
                                            ALU.subtract, ALU.mult).then_inc(xn_ready, 1)

            def body(it, last):
                if not last:
                    normalise(it + 1)
                for u in range(NU):
                    r = it * NU + u
                    dve.wait_ge(high_ready, r + 1)
                    wait(dve, low_ready, r - 1)
                    nc.vector.tensor_tensor(left[:, u % 2, :], psU[u % 2][:], parts[:, u, 0, :], ALU.subtract).then_inc(left_ready, 1)

            normalise(0)
            body(0, False)
            with dve.Fori(1, CH - 1) as it:
                body(it, False)
            body(CH - 1, True)

        @block.tensor
        def _(pe):
            def body(it):
                pe.wait_ge(xn_ready, it * U + U)
                wait(pe, xT_ready, it * DC)
                for c in range(DC):
                    for s in range(U):
                        ins = nc.tensor.transpose(psT[c][:, s * P:(s + 1) * P], xn[:, s, c * P:(c + 1) * P], T.ident[:])
                ins.then_inc(t_done, 1)
                pe.wait_ge(xT_ready, it * DC + DC)
                for c in range(DC):
                    ins = nc.tensor.matmul(psC[:], T.wdown[:, c, :], xT[:, c, :], start=(c == 0), stop=(c == DC - 1))
                ins.then_inc(c_done, 1)
                pe.wait_ge(cT_ready, it + 1)
                for u in range(NU):
                    wait(pe, left_ready, it * NU + u - 1)
                    rows = slice(0, DL) if u < 2 else slice(DL, 2 * DL)
                    nc.tensor.matmul(psU[u % 2][:], T.wup[rows, (u % 2) * P:(u % 2 + 1) * P], cT[rows, :],
                                     start=True, stop=True).then_inc(u_done, 1)
                for a in range(2):
                    wait(pe, v_ready, it * 2 + a - 1)
                    for s in range(2):
                        ins = nc.tensor.matmul(psV[a][:, s * D:(s + 1) * D], cT[DL:2 * DL, (2 * a + s) * P:(2 * a + s + 1) * P],
                                               T.wuv[DL:2 * DL, :], start=True, stop=True)
                    ins.then_inc(v_done, 1)
            body(0)
            with pe.Fori(1, CH) as it:
                body(it)

        @block.scalar
        def _(act):
            act_std(nc, act, ln)
            act.wait_ge(wset, 2)

            def body(it):
                act.wait_ge(t_done, it + 1)
                wait(act, c_done, it)
                for c in range(DC):
                    nc.scalar.copy(xT[:, c, :], psT[c][:]).then_inc(xT_ready, 1)
                act.wait_ge(c_done, it + 1)
                wait(act, v_done, it * 2)
                nc.scalar.copy(cT[:], psC[:]).then_inc(cT_ready, 1)
                for u in range(NU):
                    act.wait_ge(u_done, it * NU + u + 1)
                    wait(act, parts_stored[u], it * 16)
                    nc.scalar.copy(parts[:, u, 0, :], psU[u % 2][:]).then_inc(high_ready, 1)
                for a in range(2):
                    act.wait_ge(v_done, it * 2 + a + 1)
                    wait(act, v_stored, it * 16)
                    nc.scalar.copy(vx[:, 2 * a:2 * a + 2, :, 0:DK],
                                   psV[a][:].rearrange("p (s h d) -> p s h d", s=2, h=H)).then_inc(v_ready, 1)
            body(0)
            with act.Fori(1, CH) as it:
                body(it)


def score_units():
    units = []
    for h in range(HG):
        for i in range(QT):
            end = (i + 1) * P
            units.append((h, i, 0, min(end, 512), i))
            if end > 512:
                units.append((h, i, 512, end - 512, i + QT // 2))
    return units


def step_plan(units, with_next, with_before):
    order = []
    work = [w + P * (k0 + w == (i + 1) * P) for _, i, k0, w, _ in units]
    total_st = sum(HG * (S - j * P) for j in range(QT))
    u, lag, done_s, done_st = 0, 2, 0, 0
    for n in range(QT * HG):
        j, h = n // HG, n % HG
        order.append(("st", j, h))
        done_st += S - j * P
        if n >= HG + lag and (n - lag) % HG == HG - 1:
            order.append(("pv", (n - lag) // HG - 1))
        if with_before and n == 1:
            order += [("o", c) for c in range(2)]
        if with_next:
            while u < len(units) and done_s * total_st * 0.9 < done_st * sum(work):
                done_s += work[u]
                order.append(("s", u))
                u += 1
            if u == len(units):
                order += [("m", a) for a in range(2)]
                u += 1
    order = [x for x in order if x[0] != "pv"]
    out = []
    for x in order:
        out.append(x)
        if x[0] == "st" and x[1] > 0 and x[2] == lag - 1:
            out.append(("pv", x[1] - 1))
    out.append(("pv", QT - 1))
    return out, [x for x in out if x[0] in "smo"]


def phase_attention(nc, T, tag, qk_dram, v_dram, o_dram):
    with ExitStack() as ctx:
        M = Mem(nc, ctx, tag)
        units = score_units()
        NS = len(units)
        QHALF = QT // 2
        GB = H // HG
        MROW = HG * QT // 2
        qst = [M.sb(f"qst{s}", [P, HG, S], BF16) for s in range(SLOTS)]
        kst = [M.sb(f"kst{s}", [P, HG, S], BF16) for s in range(SLOTS)]
        vst = [M.sb(f"vst{s}", [P, QT, HG * VW]) for s in range(SLOTS)]
        prob = [M.sb(f"prob{i}", [P, HG, S]) for i in range(2)]
        maxp = M.sb("maxp", [P, HG, QT + QHALF])
        maxq = M.sb("maxq", [P, HG, QT])
        neg, mid = M.sb("neg", [MROW, 2, P]), M.sb("mid", [MROW, 2, P])
        mparts = M.sb("mparts", [MROW, 2, PARTS, P], BF16)
        oT = M.sb("oT", [P, 2, 512])
        orow = M.sb("orow", [P, 2, 512])
        psR = [M.ps(f"psR{i}", [P, 512]) for i in range(2)]
        psS = [M.ps(f"psS{i}", [P, S]) for i in range(2)]
        psO = [M.ps(f"psO{i}", [P, 512]) for i in range(2)]
        loaded = [M.sem(f"loaded{s}") for s in range(SLOTS)]
        o_stored = [M.sem(f"o_stored{c}") for c in range(2)]
        m_loaded, filled, drained, max_ready, m_ready, st_done, exp_done, pv_done, o_copied, ones_set, chain = (
            M.sem(n) for n in ("m_loaded", "filled", "drained", "max_ready", "m_ready", "st_done", "exp_done", "pv_done",
                               "o_copied", "ones_set", "chain"))
        N_LOADS = 2 * len(Q_PARTS) + 1
        RING0 = NS + 2
        RING = NS + 4
        CHAIN = 7
        block = ctx.enter_context(nc.Block())

        def steps(step):
            def run(eng):
                last = (NG - 1) // SLOTS - 1
                for k in range(SLOTS):
                    step(k, k, True, k > 0)
                with eng.Fori(1, last) as it:
                    for k in range(SLOTS):
                        step(it * SLOTS + k, k, True, True)
                for g in range(last * SLOTS, NG):
                    step(g, g % SLOTS, g + 1 < NG, True)
            return run

        def ring_base(g):
            return RING0 if isinstance(g, int) and g == 0 else g * RING + (RING0 - 2)

        def out_at(g, c):
            plan = step_plan(units, not (isinstance(g, int) and g + 2 >= NG), True)[1]
            if isinstance(g, int) and g == NG - 1:
                return (NG - 1) * RING + (RING0 - 2) + 2 + c + 1
            return (g + 1) * RING + (RING0 - 2 + plan.index(("o", c)) + 1)

        @block.sync
        def _(sp):
            sp.wait_ge(ones_set, 2 * SLOTS)

            def load(g, slot):
                b, hg = g // GB, g % GB
                for kind, st, which in ((0, qst, Q_PARTS), (1, kst, K_PARTS)):
                    for r, part in enumerate(which):
                        src = qk_dram[kind, part, bass.ds(hg * (HG * DK), HG * DK), bass.ds(b * S, S)]
                        sp.dma_start(st[slot][r * DK:(r + 1) * DK, :, :],
                                     src.rearrange("(h d) t -> d h t", d=DK)).then_inc(loaded[slot], 16)
                src = v_dram[bass.ds(b * S, S), bass.ds(hg * (HG * VW), HG * VW)]
                sp.dma_start(vst[slot][:], src.rearrange("(j p) w -> p j w", p=P)).then_inc(loaded[slot], 16)

            def store_out(g):
                b, hg = g // GB, g % GB
                for c in range(2):
                    hold(sp, drained, out_at(g, c), T)
                    dst = o_dram[bass.ds(b * S + c * 512, 512), bass.ds(hg * (HG * VW), HG * VW)]
                    sp.dma_start(dst.rearrange("(i p) w -> p i w", p=P),
                                 orow[:, c, :].rearrange("p (i w) -> p i w", w=HG * VW)).then_inc(o_stored[c], 16)

            def load_max(g, slot):
                hold(sp, m_ready, g * 2 + 2, T)
                for part in range(PARTS):
                    row = qst[slot][KROWS + part:KROWS + part + 1, :, :]
                    for a in range(2):
                        sp.dma_start(row[:, 2 * a:2 * a + 2, :], mparts[:, a, part, :]).then_inc(m_loaded, 16)

            def step(g, k, with_next, with_before):
                if with_before:
                    store_out(g - 1)
                if with_next:
                    load_max(g + 1, (k + 1) % SLOTS)
                if not isinstance(g, int) or g + SLOTS < NG:
                    hold(sp, pv_done, g * QT + QT, T)
                    load(g + SLOTS, k)

            for g in range(SLOTS):
                load(g, g)
            load_max(0, 0)
            steps(step)(sp)
            store_out(NG - 1)
            for c in range(2):
                sp.wait_ge(o_stored[c], 16 * NG)

        @block.gpsimd
        def _(pool):
            for s in range(SLOTS):
                nc.gpsimd.memset(kst[s][KROWS:P, :, :], 1.0).then_inc(ones_set, 1)
                nc.gpsimd.memset(qst[s][KROWS:P, :, :], 0.0).then_inc(ones_set, 1)

        @block.tensor
        def _(pe):
            def score(u, slot, r, bank):
                h, i, k0, w, _ = units[u]
                wait(pe, drained, r - 1)
                diag = k0 + w == (i + 1) * P
                ins = nc.tensor.matmul(psR[bank][:, 0:w], qst[slot][0:KROWS, h, i * P:(i + 1) * P],
                                       kst[slot][0:KROWS, h, k0:k0 + w], start=True, stop=not diag)
                if diag:
                    ins = nc.tensor.matmul(psR[bank][:, w - P:w], T.ident_bf[:], T.causal[:], start=False, stop=True)
                ins.then_inc(filled, 1)

            def turn_max(g, a, r, bank):
                wait(pe, drained, r - 1)
                pe.wait_ge(max_ready, g + 1)
                nc.tensor.transpose(psR[bank][0:MROW, 0:P], maxq[:, 2 * a:2 * a + 2, :].rearrange("p h i -> p (h i)"),
                                    T.ident[:]).then_inc(filled, 1)

            def turn_out(g, c, r, bank):
                wait(pe, drained, r - 1)
                pe.wait_ge(o_copied, g * 2 + c + 1)
                for i in range(512 // P):
                    ins = nc.tensor.transpose(psR[bank][:, i * P:(i + 1) * P], oT[:, c, i * P:(i + 1) * P], T.ident[:])
                ins.then_inc(filled, 1)

            def score_t(g, k, j, h):
                n = j * HG + h
                wait(pe, exp_done, g * (QT * HG) + n - 1)
                for q0 in range(j * P // 512 * 512, S, 512):
                    a = max(q0, j * P)
                    ins = nc.tensor.matmul(psS[n % 2][:, a:q0 + 512], kst[k][0:MROWS, h, j * P:(j + 1) * P],
                                           qst[k][0:MROWS, h, a:q0 + 512], start=True, stop=a > j * P)
                    if a == j * P:
                        ins = nc.tensor.matmul(psS[n % 2][:, a:a + P], T.ident_bf[:], T.causal_t[:], start=False, stop=True)
                ins.then_inc(st_done, 1)

            def pv(g, k, j):
                pe.wait_ge(exp_done, g * (QT * HG) + (j + 1) * HG)
                if j == 0:
                    wait(pe, o_copied, g * 2)
                for c in range(j // QHALF, 2):
                    a = max(c * 512, j * P)
                    for h in range(HG):
                        ins = nc.tensor.matmul(psO[c][h * VW:(h + 1) * VW, a - c * 512:512],
                                               vst[k][:, j, h * VW:(h + 1) * VW], prob[j % 2][:, h, a:(c + 1) * 512],
                                               start=(j == 0), stop=(j == QHALF * (c + 1) - 1))
                ins.then_inc(pv_done, 1)

            def step(g, k, with_next, with_before):
                base, slot, idx = ring_base(g), (k + 1) % SLOTS, 0
                pe.wait_ge(m_loaded, g * (32 * PARTS) + 32 * PARTS)
                if with_next:
                    pe.wait_ge(loaded[slot], ((g - k) // SLOTS) * (16 * N_LOADS) + 16 * N_LOADS * ((k + 1) // SLOTS + 1))
                for what, *at in step_plan(units, with_next, with_before)[0]:
                    if what == "st":
                        score_t(g, k, *at)
                        continue
                    if what == "pv":
                        pv(g, k, *at)
                        continue
                    if what == "s":
                        score(at[0], slot, base + idx, idx % 2)
                    elif what == "m":
                        turn_max(g + 1, at[0], base + idx, idx % 2)
                    else:
                        turn_out(g - 1, at[0], base + idx, idx % 2)
                    idx += 1

            pe.wait_ge(loaded[0], 16 * N_LOADS)
            for u in range(NS):
                score(u, 0, u, u % 2)
            for a in range(2):
                turn_max(0, a, NS + a, a)
            steps(step)(pe)
            for c in range(2):
                turn_out(NG - 1, c, out_at(NG - 1, c) - 1, c)

        @block.scalar
        def _(act):
            def copy_out(g, c):
                act.wait_ge(pv_done, g * QT + QHALF * (c + 1))
                nc.scalar.copy(oT[:, c, :], psO[c][:]).then_inc(o_copied, 1)

            def step(g, k, with_next, with_before):
                for j in range(QT):
                    wait(act, pv_done, g * QT + j - 1)
                    for h in range(HG):
                        n = j * HG + h
                        act.wait_ge(st_done, g * (QT * HG) + n + 1)
                        nc.scalar.activation(prob[j % 2][:, h, j * P:S], psS[n % 2][:, j * P:S], ACT.Exp,
                                             scale=DK ** -0.5).then_inc(exp_done, 1)
                    if j == QHALF + 1:
                        copy_out(g, 0)
                copy_out(g, 1)
            steps(step)(act)

        @block.vector
        def _(dve):
            def link(ins, g, n):
                ins.then_inc(chain, 1)
                dve.wait_ge(chain, g * CHAIN + n)

            def row_max(u, r, bank):
                h, _, _, w, col = units[u]
                dve.wait_ge(filled, r + 1)
                nc.vector.tensor_reduce(maxp[:, h, col:col + 1], psR[bank][:, 0:w], AX_X, ALU.max).then_inc(drained, 1)

            def join_max(g, r):
                dve.wait_ge(drained, r)
                link(nc.vector.tensor_copy(maxq[:, :, 0:QHALF], maxp[:, :, 0:QHALF]), g, 1)
                nc.vector.tensor_tensor(maxq[:, :, QHALF:QT], maxp[:, :, QHALF:QT], maxp[:, :, QT:QT + QHALF],
                                        ALU.max).then_inc(max_ready, 1)

            def split_max(g, a, r, bank):
                n = 1 + 3 * a
                dve.wait_ge(filled, r + 1)
                wait(dve, m_loaded, g * (32 * PARTS))
                nc.vector.tensor_scalar(neg[:, a], psR[bank][0:MROW, 0:P], -1.0, None, ALU.mult).then_inc(drained, 1)
                dve.wait_ge(drained, r + 1)
                link(nc.vector.tensor_copy(mparts[:, a, 0], neg[:, a]), g, n + 1)
                link(nc.vector.tensor_tensor(mid[:, a], neg[:, a], mparts[:, a, 0], ALU.subtract), g, n + 2)
                link(nc.vector.tensor_copy(mparts[:, a, 1], mid[:, a]), g, n + 3)
                nc.vector.tensor_tensor(mparts[:, a, 2], mid[:, a], mparts[:, a, 1], ALU.subtract).then_inc(m_ready, 1)

            def copy_rows(g, c, r, bank):
                dve.wait_ge(filled, r + 1)
                wait(dve, o_stored[c], g * 16)
                nc.vector.tensor_copy(orow[:, c, :], psR[bank][:]).then_inc(drained, 1)

            def step(g, k, with_next, with_before):
                base = ring_base(g)
                for idx, (what, at) in enumerate(step_plan(units, with_next, with_before)[1]):
                    if what == "s":
                        row_max(at, base + idx, idx % 2)
                    elif what == "m":
                        if at == 0:
                            join_max(g + 1, base + idx)
                        split_max(g + 1, at, base + idx, idx % 2)
                    else:
                        copy_rows(g - 1, at, base + idx, idx % 2)

            for u in range(NS):
                row_max(u, u, u % 2)
            join_max(0, NS)
            for a in range(2):
                split_max(0, a, NS + a, a)
            steps(step)(dve)
            for c in range(2):
                copy_rows(NG - 1, c, out_at(NG - 1, c) - 1, c)


def phase_output(nc, T, tag, x, o_dram):
    with ExitStack() as ctx:
        M = Mem(nc, ctx, tag)
        ITS = NT // U
        raw = M.sb("raw", [P, U, H, VW])
        inv = M.sb("inv", [P, U, H])
        att = M.sb("att", [P, U, H, DK])
        aT = M.sb("aT", [P, 2, DC, P])
        psT = [M.ps(f"psT{i}", [P, 512]) for i in range(2)]
        psW = [M.ps(f"psW{i}", [P, 512]) for i in range(2)]
        raw_loaded, inv_ready, att_ready, t_done, aT_ready, w_done, added = (
            M.sem(n) for n in ("raw_loaded", "inv_ready", "att_ready", "t_done", "aT_ready", "w_done", "added"))
        o_view = o_dram.rearrange("(n p) w -> p n w", p=P)
        block = ctx.enter_context(nc.Block())

        @block.sync
        def _(sp):
            def body(it):
                hold(sp, att_ready, it * U, T)
                sp.dma_start(raw[:].rearrange("p n h w -> p n (h w)"), o_view[:, bass.ds(it * U, U), :]).then_inc(raw_loaded, 16)
            body(0)
            with sp.Fori(1, ITS) as it:
                body(it)

        @block.vector
        def _(dve):
            def scaled(it):
                dve.wait_ge(raw_loaded, it * 16 + 16)
                wait(dve, att_ready, it * U)
                nc.vector.reciprocal(inv[:], raw[:, :, :, DK]).then_inc(inv_ready, 1)
                dve.wait_ge(inv_ready, it + 1)
                for s in range(U):
                    wait(dve, t_done, it * U + s + 1 - U)
                    nc.vector.tensor_tensor(att[:, s], raw[:, s, :, 0:DK], bc(inv[:, s, :], 2, [P, H, DK]), ALU.mult).then_inc(att_ready, 1)

            def add(it):
                for s in range(U):
                    n = it * U + s
                    row = x[:, bass.ds(n, 1), :].rearrange("p a d -> p (a d)")
                    dve.wait_ge(w_done, n + 1)
                    nc.vector.tensor_tensor(row, row, psW[s % 2][:, 0:D], ALU.add).then_inc(added, 1)

            scaled(0)
            with dve.Fori(0, ITS - 1) as it:
                scaled(it + 1)
                add(it)
            add(ITS - 1)

        @block.tensor
        def _(pe):
            def turn(it, s):
                n = it * U + s
                pe.wait_ge(att_ready, n + 1)
                wait(pe, aT_ready, n - 1)
                for c in range(DC):
                    ins = nc.tensor.transpose(psT[s % 2][:, c * P:(c + 1) * P],
                                              att[:, s].rearrange("p h d -> p (h d)")[:, c * P:(c + 1) * P], T.ident[:])
                ins.then_inc(t_done, 1)

            def project(it, s):
                n = it * U + s
                pe.wait_ge(aT_ready, n + 1)
                wait(pe, added, n - 1)
                for c in range(DC):
                    ins = nc.tensor.matmul(psW[s % 2][:, 0:D], aT[:, s % 2, c, :], T.wo[:, c, :], start=(c == 0), stop=(c == DC - 1))
                ins.then_inc(w_done, 1)

            def body(it):
                turn(it, 0)
                for s in range(U):
                    if s + 1 < U:
                        turn(it, s + 1)
                    project(it, s)
            body(0)
            with pe.Fori(1, ITS) as it:
                body(it)

        @block.scalar
        def _(act):
            def body(it):
                for s in range(U):
                    n = it * U + s
                    act.wait_ge(t_done, n + 1)
                    wait(act, w_done, n - 1)
                    nc.scalar.copy(aT[:, s % 2, :, :], psT[s % 2][:, 0:D].rearrange("p (c t) -> p c t", c=DC)).then_inc(aT_ready, 1)
            body(0)
            with act.Fori(1, ITS) as it:
                body(it)


class Tables:
    pass


def phase_constants(nc, T, M):
    T.ident, T.ident_bf = M.sb("ident", [P, P]), M.sb("ident_bf", [P, P], BF16)
    T.causal, T.causal_t = M.sb("causal", [P, P], BF16), M.sb("causal_t", [P, P], BF16)
    T.lower_bf, T.ones_bf, T.ones_f = M.sb("lower_bf", [P, P], BF16), M.sb("ones_bf", [P, P], BF16), M.sb("ones_f", [P, P])
    iota_i, token_i = M.sb("iota_i", [P, P], I32), M.sb("token_i", [P, SLOTC], I32)
    T.iota, T.iota_h = M.sb("iota", [P, P]), M.sb("iota_h", [P, P], F16)
    T.token = M.sb("token", [P, SLOTC])
    made = M.sem("made")
    T.const_ready = M.sem("const_ready")
    T.N_CONST = 1
    with nc.Block() as block:
        @block.gpsimd
        def _(pool):
            g = nc.gpsimd
            c = Chain(pool, made)
            c.link(g.memset(T.ones_f[:], 1.0))
            c.link(g.memset(T.ones_bf[:], 1.0))
            c.link(g.memset(T.causal[:], 0.0))
            c.link(g.memset(T.causal_t[:], 0.0))
            square = [[1, P]]
            c.link(g.affine_select(out=T.ident[:], in_=T.ones_f[:], compare_op=ALU.is_equal, fill=0.0, base=0,
                                   pattern=square, channel_multiplier=-1))
            c.link(g.affine_select(out=T.ident_bf[:], in_=T.ones_bf[:], compare_op=ALU.is_equal, fill=0.0, base=0,
                                   pattern=square, channel_multiplier=-1))
            c.link(g.affine_select(out=T.lower_bf[:], in_=T.ones_bf[:], compare_op=ALU.is_gt, fill=0.0, base=0,
                                   pattern=square, channel_multiplier=-1))
            c.link(g.affine_select(out=T.causal[:], in_=T.causal[:], compare_op=ALU.is_ge, fill=NEG, base=0,
                                   pattern=[[-1, P]], channel_multiplier=1))
            c.link(g.affine_select(out=T.causal_t[:], in_=T.causal_t[:], compare_op=ALU.is_ge, fill=NEG, base=0,
                                   pattern=square, channel_multiplier=-1))
            c.link(g.iota(iota_i[:], [[1, P]], base=0, channel_multiplier=0))
            c.link(g.iota(token_i[:], [[0, TOPK], [P, NT]], base=-(N // 2), channel_multiplier=1))
            c.link(g.tensor_copy(T.iota[:], iota_i[:]))
            c.link(g.tensor_copy(T.iota_h[:], iota_i[:]))
            g.tensor_copy(T.token[:], token_i[:]).then_inc(T.const_ready, 1)


class Routing:

    def __init__(self, M, k):
        self.weight = M.sb(f"weight{k}", [P, TOPK, NT])
        self.place = M.sb(f"place{k}", [P, SLOTC], I32)
        self.table = M.sb(f"table{k}", [P, MT], I32)
        self.expert = M.sb(f"expert{k}", [1, MT], I32)


def program(nc, x, W_dq, W_uq, W_dkv, W_uk, W_uv, W_o, gate, gate_up, down, similarity, out):
    with ExitStack() as ctx:
        M = Mem(nc, ctx, "all")
        T = Tables()
        xs = M.sb("x", [P, NT, D])
        logits = M.sb("logits", [P, NT, E])
        R = Routing(M, 0)
        T.gateT, T.simb = M.sb("gateT", [P, DC, E]), M.sb("simb", [P, E, E])
        T.wgu, T.wd = M.sb("wgu", [P, DC, E, 2 * F]), M.sb("wd", [P, DC, E, D])
        T.wdown = M.sb("wdown", [P, DC, 2 * DL])
        T.wup, T.wuv = M.sb("wup", [P, D]), M.sb("wuv", [P, D])
        T.wo = M.sb("wo", [P, DC, D])
        T.x_loaded, T.w_loaded = M.sem("x_loaded"), M.sem("w_loaded")
        T.holds_passed = {e.engine: M.sem(n) for e, n in ((nc.gpsimd, "pool_holds"), (nc.sync, "sp_holds"))}
        xn_dram = nc.dram_tensor("xn_rows", (N, D), F32).ap()
        y_dram = nc.dram_tensor("y_rows", (MT * P, D), F32).ap()
        qk_dram = nc.dram_tensor("qk_parts", (2, PARTS, D, N), BF16).ap()
        v_dram = nc.dram_tensor("v_rows", (N, H * VW), F32).ap()
        o_dram = nc.dram_tensor("o_rows", (N, H * VW), F32).ap()
        phase_constants(nc, T, M)
        x_view = x.rearrange("(n p) d -> p n d", p=P)
        split = lambda w: w.rearrange("(c p) n -> p c n", p=P)
        weights = [(T.gateT[:], split(gate)), (T.simb[:].rearrange("p a b -> p (a b)"), similarity.partition_broadcast(P)),
                   (T.wdown[:, :, 0:DL], split(W_dq)), (T.wdown[:, :, DL:2 * DL], split(W_dkv)),
                   (T.wup[0:DL, :], W_uq), (T.wup[DL:2 * DL, :], W_uk), (T.wuv[DL:2 * DL, :], W_uv), (T.wo[:], split(W_o))]
        weights += [(T.wgu[:, c], gate_up[:, c * P:(c + 1) * P, :].rearrange("e p f -> p e f")) for c in range(DC)]
        weights += [(T.wd[:, c], down[:, c * P:(c + 1) * P, :].rearrange("e p f -> p e f")) for c in range(DC)]
        T.N_W = 16 * len(weights)

        def loads(sp):
            for q in range(4):
                n = slice(q * NT // 4, (q + 1) * NT // 4)
                sp.dma_start(xs[:, n, :], x_view[:, n, :]).then_inc(T.x_loaded, 16)
            for dst, src in weights:
                sp.dma_start(dst, src).then_inc(T.w_loaded, 16)

        def moe(tag, first, result):
            phase_logits(nc, T, tag + "l", xs, xn_dram, logits, loads if first else None)
            phase_route(nc, T, tag + "r", logits, R)
            phase_experts(nc, T, tag + "e", R, xn_dram, y_dram)
            phase_combine(nc, T, tag + "c", R, xs, y_dram, result)

        moe("a", True, None)
        phase_qkv(nc, T, "q", xs, qk_dram, v_dram)
        phase_attention(nc, T, "t", qk_dram, v_dram, o_dram)
        phase_output(nc, T, "o", xs, o_dram)
        moe("b", False, out)


def kernel(L0_attn_x, L0_attn_W_dq, L0_attn_W_uq, L0_attn_W_dkv, L0_attn_W_uk, L0_attn_W_uv, L0_attn_W_o, L0_ffn_gate_weight,
           L0_ffn_gate_up_proj, L0_ffn_down_proj, L0_ffn_similarity_matrix):
    import concourse.bacc as bacc
    import numpy as np
    from concourse.bass_utils import run_bass_kernel_spmd

    rows = np.ascontiguousarray
    arrays = {
        "x": rows(L0_attn_x).reshape(N, D),
        "w_dq": rows(L0_attn_W_dq), "w_uq": rows(L0_attn_W_uq), "w_dkv": rows(L0_attn_W_dkv),
        "w_uk": rows(L0_attn_W_uk), "w_uv": rows(L0_attn_W_uv), "w_o": rows(L0_attn_W_o),
        "gate": rows(np.transpose(L0_ffn_gate_weight)),
        "gate_up": rows(np.transpose(L0_ffn_gate_up_proj, (0, 2, 1))),
        "down": rows(np.transpose(L0_ffn_down_proj, (0, 2, 1))),
        "similarity": rows(L0_ffn_similarity_matrix).reshape(E * E),
    }
    nc = bacc.Bacc("TRN2", target_bir_lowering=False, num_devices=1)
    args = [nc.dram_tensor(f"in_{k}", a.shape, mybir.dt.from_np(a.dtype), kind="ExternalInput").ap() for k, a in arrays.items()]
    out = nc.dram_tensor("out_rows", (N, D), F32, kind="ExternalOutput").ap()
    program(nc, *args, out)
    result = run_bass_kernel_spmd(nc, [{f"in_{k}": a for k, a in arrays.items()}], core_ids=[0])
    return result.results[0]["out_rows"].reshape(B, S, D)
```

```python
from contextlib import ExitStack

import concourse.bass as bass
from concourse import mybir

F32 = mybir.dt.float32
BF16 = mybir.dt.bfloat16
F16 = mybir.dt.float16
I32 = mybir.dt.int32
ALU = mybir.AluOpType
ACT = mybir.ActivationFunctionType
AX_X = mybir.AxisListType.X

P = 128
B, S, D = 4, 1024, 256
N = B * S
NT = N // P
DC = D // P
E = 8
F = 256
TOPK = 2
SLOTC = TOPK * NT
U = 4
MT = TOPK * N // P + E
H, DK, DL = 16, 16, 64
HG = 4
NG = B * H // HG
QT = S // P
BIG = 3.0e38
NEG = -1.0e30
EPS = 1e-5
THRESHOLD = 0.7
HALF = 0.5
PARTS = 3
Q_PARTS = (0, 0, 0, 1, 1, 2)
K_PARTS = (0, 1, 2, 0, 1, 0)
KROWS = len(Q_PARTS) * DK
MROWS = KROWS + PARTS
VW = 32
SLOTS = 3
RING_BANKS = 3
ST_BANKS = 3
AHEAD = 17


def wait(eng, sem, value):
    if not isinstance(value, int) or value > 0:
        eng.wait_ge(sem, value)


def hold(eng, sem, value, T):
    wait(eng, sem, value)
    if not isinstance(value, int):
        eng.sem_inc(T.holds_passed[eng.engine], 1)


class Chain:

    def __init__(self, eng, sem):
        self.eng, self.sem, self.n = eng, sem, 0

    def link(self, ins):
        self.n += 1
        ins.then_inc(self.sem, 1)
        self.eng.wait_ge(self.sem, self.n)


class Mem:

    def __init__(self, nc, ctx, tag):
        self.nc, self.ctx, self.tag = nc, ctx, tag

    def sb(self, name, shape, dt=F32):
        return self.ctx.enter_context(self.nc.sbuf_tensor(f"{self.tag}_{name}", shape, dt))

    def ps(self, name, shape, dt=F32):
        return self.ctx.enter_context(self.nc.psum_tensor(f"{self.tag}_{name}", shape, dt))

    def sem(self, name):
        return self.ctx.enter_context(self.nc.semaphore(f"{self.tag}_{name}"))


def bc(ap, axis, shape):
    return ap.unsqueeze(axis).to_broadcast(shape)


def phase_logits(nc, T, tag, x, xn_dram, logits, o_dram=None, loads=None):
    with ExitStack() as ctx:
        M = Mem(nc, ctx, tag)
        ln = LayerNorm(nc, T, M)
        CH = NT // U
        raw, inv = M.sb("raw", [P, 2, U, H, VW]), M.sb("inv", [P, 2, U, H])
        att = M.sb("att", [P, 2, U, H, DK])
        aT = M.sb("aT", [P, U, DC, P])
        xn = M.sb("xn", [P, 2, U, D])
        xT = M.sb("xT", [P, 2, DC, P])
        psA, psW, psT, psL = ([M.ps(f"{n}{i}", [P, 512]) for i in range(2)] for n in ("psA", "psW", "psT", "psL"))
        xn_stored = [M.sem(f"xn_stored{b}") for b in range(2)]
        xn_ready, t_done, xT_ready, l_done, l_copied = (M.sem(n) for n in ("xn_ready", "t_done", "xT_ready", "l_done", "l_copied"))
        xn_view = xn_dram.rearrange("(n p) d -> p n d", p=P)
        attended = o_dram is not None
        if attended:
            raw_loaded = [M.sem(f"raw_loaded{b}") for b in range(2)]
            inv_ready, att_ready, at_done, aT_ready, w_done, added = (
                M.sem(n) for n in ("inv_ready", "att_ready", "at_done", "aT_ready", "w_done", "added"))
            o_view = o_dram.rearrange("(n p) w -> p n w", p=P)
        block = ctx.enter_context(nc.Block())

        def row(c, s):
            return x[:, bass.ds(c * U + s, 1), :].rearrange("p a d -> p (a d)")

        def steps(eng, step):
            def has(c):
                return lambda d: not isinstance(c, int) or 0 <= c + d < CH
            for c in range(-2, 2):
                step(c, c % 2, has(c))
            with eng.Fori(1, CH // 2 - 1) as it:
                for b in range(2):
                    step(it * 2 + b, b, has(it))
            for c in range(CH - 2, CH + 1):
                step(c, c % 2, has(c))

        @block.sync
        def _(sp):
            def load(c, b):
                sp.dma_start(raw[:, b].rearrange("p n h w -> p n (h w)"), o_view[:, bass.ds(c * U, U), :]).then_inc(raw_loaded[b], 16)

            def step(c, b, has):
                if attended and has(4):
                    hold(sp, att_ready, c * U + (2 * U + U), T)
                    load(c + 4, b)
                if has(0):
                    hold(sp, xn_ready, c * U + U, T)
                    sp.dma_start(xn_view[:, bass.ds(c * U, U), :], xn[:, b]).then_inc(xn_stored[b], 16)
                    if loads:
                        loads[1](sp, c)

            if loads:
                loads[0](sp)
            if attended:
                for b in range(2):
                    load(b, b)
            for c in range(-2, 2):
                step(c, c % 2, lambda d: 0 <= c + d < CH)
            with sp.Fori(1, CH // 2 - 2) as it:
                for b in range(2):
                    step(it * 2 + b, b, lambda d: True)
            for c in range(CH - 4, CH):
                step(c, c % 2, lambda d: 0 <= c + d < CH)
            for b in range(2):
                sp.wait_ge(xn_stored[b], 16 * (CH // 2))

        if attended:
            @block.gpsimd
            def _(pool):
                def step(c, b, has):
                    if has(2):
                        a = c + 2
                        hold(pool, inv_ready, a + 1, T)
                        hold(pool, at_done, c * U + U, T)
                        for s in range(U):
                            nc.gpsimd.tensor_tensor(att[:, b, s], raw[:, b, s, :, 0:DK], bc(inv[:, b, s, :], 2, [P, H, DK]),
                                                    ALU.mult).then_inc(att_ready, 1)
                steps(pool, step)

        @block.vector
        def _(dve):
            def step(c, b, has):
                if attended and has(2):
                    dve.wait_ge(raw_loaded[b], (c // 2) * 16 + 32)
                    wait(dve, att_ready, c * U + U)
                    nc.vector.reciprocal(inv[:, b], raw[:, b, :, :, DK]).then_inc(inv_ready, 1)
                if not has(0):
                    return
                for s in range(U):
                    if attended:
                        n = c * U + s
                        dve.wait_ge(w_done, n + 1)
                        nc.vector.tensor_tensor(row(c, s), row(c, s), psW[s % 2][:, 0:D], ALU.add).then_inc(added, 1)
                        if s:
                            hold(dve, added, n, T)
                            ln.tile_stats(s - 1, x[:, bass.ds(n - 1, 1), :])
                    else:
                        if s == 0:
                            i = c if isinstance(c, int) and c < 2 else 2
                            dve.wait_ge(T.x_loaded[i], 32 if i == 2 else 16)
                        ln.tile_stats(s, x[:, bass.ds(c * U + s, 1), :])
                if attended:
                    hold(dve, added, c * U + U, T)
                    ln.tile_stats(U - 1, x[:, bass.ds(c * U + U - 1, 1), :])
                ln.variance(dve, c)
                ln.reciprocal(dve, c)
                for s in range(U):
                    if s == 0 and (not isinstance(c, int) or c > 1):
                        dve.wait_ge(xn_stored[b], (c // 2) * 16)
                        dve.wait_ge(t_done, c * U - U)
                    ln.normalised(s, xn[:, b, s, :], row(c, s)).then_inc(xn_ready, 1)
            steps(dve, step)

        @block.tensor
        def _(pe):
            pe.wait_ge(T.const_ready, T.N_CONST)
            if loads:
                pe.wait_ge(T.gate_loaded, 16)

            def project(c, s):
                n = c * U + s
                pe.wait_ge(aT_ready, n + 1)
                wait(pe, added, n - 1)
                for k in range(DC):
                    ins = nc.tensor.matmul(psW[s % 2][:, 0:D], aT[:, s, k, :], T.wo[:, k, :], start=(k == 0), stop=(k == DC - 1))
                ins.then_inc(w_done, 1)

            def turn_att(c, b, s):
                n = c * U + s
                pe.wait_ge(att_ready, n + 1)
                wait(pe, aT_ready, n - 1)
                for k in range(DC):
                    ins = nc.tensor.transpose(psA[s % 2][:, k * P:(k + 1) * P],
                                              att[:, b, s].rearrange("p h d -> p (h d)")[:, k * P:(k + 1) * P], T.ident[:])
                ins.then_inc(at_done, 1)

            def turn(c, b, s):
                n = c * U + s
                pe.wait_ge(xn_ready, n + 1)
                wait(pe, xT_ready, n - 1)
                for k in range(DC):
                    ins = nc.tensor.transpose(psT[s % 2][:, k * P:(k + 1) * P], xn[:, b, s, k * P:(k + 1) * P], T.ident[:])
                ins.then_inc(t_done, 1)

            def scores(c, b, s):
                n = c * U + s
                pe.wait_ge(xT_ready, n + 1)
                if s == 0:
                    wait(pe, l_copied, c - 1)
                for k in range(DC):
                    ins = nc.tensor.matmul(psL[b][:, s * E:(s + 1) * E], xT[:, s % 2, k, :], T.gateT[:, k, :],
                                           start=(k == 0), stop=(k == DC - 1))
                ins.then_inc(l_done, 1)

            def step(c, b, has):
                for s in range(U):
                    if attended and has(0):
                        project(c, s)
                    if attended and has(1):
                        turn_att(c + 1, 1 - b, s)
                    if has(-1):
                        turn(c - 1, 1 - b, s)
                        if s:
                            scores(c - 1, 1 - b, s - 1)
                if has(-1):
                    scores(c - 1, 1 - b, U - 1)
            steps(pe, step)

        @block.scalar
        def _(act):
            def step(c, b, has):
                for s in range(U):
                    if attended and has(1):
                        n = (c + 1) * U + s
                        act.wait_ge(at_done, n + 1)
                        wait(act, w_done, n + 1 - U)
                        nc.scalar.copy(aT[:, s], psA[s % 2][:, 0:D].rearrange("p (k t) -> p k t", k=DC)).then_inc(aT_ready, 1)
                    if has(-1):
                        n = (c - 1) * U + s
                        act.wait_ge(t_done, n + 1)
                        wait(act, l_done, n - 1)
                        nc.scalar.copy(xT[:, s % 2], psT[s % 2][:, 0:D].rearrange("p (k t) -> p k t", k=DC)).then_inc(xT_ready, 1)
                if has(0):
                    ln.deviation(act, c)
                if has(-1):
                    act.wait_ge(l_done, c * U)
                    nc.scalar.copy(logits[:, bass.ds((c - 1) * U, U), :],
                                   psL[1 - b][:, 0:U * E].rearrange("p (s e) -> p s e", s=U)).then_inc(l_copied, 1)
            steps(act, step)


def phase_route(nc, T, tag, logits, R):
    with ExitStack() as ctx:
        M = Mem(nc, ctx, tag)
        shape = [P, NT, E]
        top = [M.sb(f"top{k}", [P, NT]) for k in range(TOPK)]
        choice = [M.sb(f"choice{k}", [P, NT]) for k in range(TOPK)]
        picked = M.sb("picked", [P, TOPK, NT, E])
        work = M.sb("work", [P, NT, E])
        rest = M.sb("rest", [P, NT, E])
        gap, expgap, den = (M.sb(n, [P, NT]) for n in ("gap", "expgap", "den"))
        primary, masked, unmasked = (M.sb(n, [P, E]) for n in ("primary", "masked", "unmasked"))
        sim, simw = M.sb("sim", [P, E, E]), M.sb("simw", [P, E, E])
        best, best_j, moved, emap = (M.sb(n, [P, E]) for n in ("best", "best_j", "moved", "emap"))
        target = M.sb("target", [P, SLOTC])
        routed = M.sb("routed", [P, SLOTC, E], BF16)
        big = M.sb("big", [P, SLOTC, E])
        upto = M.sb("upto", [P, SLOTC + 1, E])
        ones = M.sb("ones", [P, SLOTC])
        zeros = M.sb("zeros", [P, MT], F16)
        counts_i, tiles_i = M.sb("counts_i", [P, E], I32), M.sb("tiles_i", [P, E], I32)
        tiles, tiles_end, row0 = (M.sb(n, [P, E]) for n in ("tiles", "tiles_end", "row0"))
        place, place_i = M.sb("place", [P, SLOTC]), M.sb("place_i", [P, SLOTC], I32)
        lane_i, tile_i = M.sb("lane_i", [P, SLOTC], I32), M.sb("tile_i", [P, SLOTC], I32)
        lane, tile = M.sb("lane", [P, SLOTC]), M.sb("tile", [P, SLOTC])
        ended = M.sb("ended", [P, MT, E])
        expert_f = M.sb("expert_f", [P, MT])
        CW = 8
        lane_hot = M.sb("lane_hot", [P, 2, CW, P], F16)
        tile_hot, tile_col, tile_lane = (M.sb(n, [P, 2, CW, MT], F16) for n in ("tile_hot", "tile_col", "tile_lane"))
        empty = M.sb("empty", [P, MT])
        ps_count, ps_before, ps_total, ps_table = (M.ps(n, [P, 512]) for n in ("ps_count", "ps_before", "ps_total", "ps_table"))
        chain_sem, gap_ready, exp_ready, picked_ready, counted, routed_ready, ranked, tile_ready, lane_ready, col_ready, \
            number_ready, hot_used, table_done = (
                M.sem(n) for n in ("chain", "gap_ready", "exp_ready", "picked_ready", "counted", "routed_ready", "ranked",
                                   "tile_ready", "lane_ready", "col_ready", "number_ready", "hot_used", "table_done"))
        block = ctx.enter_context(nc.Block())
        iota_e = T.iota[:, 0:E]

        def table_steps(eng, body):
            for b in range(2):
                body(b, b)
            with eng.Fori(1, SLOTC // CW // 2) as it:
                for b in range(2):
                    body(it * 2 + b, b)

        @block.scalar
        def _(act):
            act.wait_ge(gap_ready, 1)
            nc.scalar.activation(expgap[:], gap[:], ACT.Exp).then_inc(exp_ready, 1)

            def by_lane(r, b):
                act.wait_ge(tile_ready, r + 1)
                wait(act, hot_used, r - 1)
                nc.scalar.activation(tile_lane[:, b], tile_hot[:, b], ACT.Copy, scale=T.lane_number[:]).then_inc(number_ready, 1)
            table_steps(act, by_lane)

        @block.vector
        def _(dve):
            c = Chain(dve, chain_sem)
            v = nc.vector
            c.link(v.memset(ones[:], 1.0))
            c.link(v.memset(zeros[:], 0.0))
            c.link(v.memset(upto[:, 0, :], 0.0))
            src = logits
            for k in range(TOPK):
                c.link(v.tensor_reduce(top[k][:], src[:], AX_X, ALU.max))
                c.link(v.tensor_tensor(work[:], src[:], bc(top[k][:], 2, shape), ALU.not_equal))
                c.link(v.scalar_tensor_tensor(work[:], work[:], float(E), bc(iota_e, 1, shape), ALU.mult, ALU.add))
                c.link(v.tensor_reduce(choice[k][:], work[:], AX_X, ALU.min))
                ins = v.tensor_tensor(picked[:, k], bc(iota_e, 1, shape), bc(choice[k][:], 2, shape), ALU.is_equal)
                ins.then_inc(picked_ready, 1)
                dve.wait_ge(picked_ready, k + 1)
                if k == 0:
                    c.link(v.scalar_tensor_tensor(rest[:], picked[:, 0], -BIG, logits[:], ALU.mult, ALU.add))
                    src = rest
            v.tensor_tensor(gap[:], top[1][:], top[0][:], ALU.subtract).then_inc(gap_ready, 1)
            dve.wait_ge(counted, 1)
            c.link(v.tensor_reduce(primary[:], ps_count[:, 0:NT * E].rearrange("p (n e) -> p e n", e=E), AX_X, ALU.add))
            c.link(v.tensor_scalar(primary[:], primary[:], 1.0, None, ALU.min))
            v.tensor_scalar(unmasked[:], primary[:], -1.0, 1.0, ALU.mult, ALU.add)
            c.link(v.tensor_scalar(masked[:], primary[:], BIG, -BIG, ALU.mult, ALU.add))
            ee = [P, E, E]
            dve.wait_ge(T.w_loaded, T.N_W)
            c.link(v.tensor_tensor(sim[:], T.simb[:], bc(primary[:], 1, ee), ALU.mult))
            c.link(v.tensor_tensor(sim[:], sim[:], bc(masked[:], 1, ee), ALU.add))
            c.link(v.tensor_reduce(best[:], sim[:], AX_X, ALU.max))
            c.link(v.tensor_tensor(simw[:], sim[:], bc(best[:], 2, ee), ALU.not_equal))
            c.link(v.scalar_tensor_tensor(simw[:], simw[:], float(E), bc(iota_e, 1, ee), ALU.mult, ALU.add))
            c.link(v.tensor_reduce(best_j[:], simw[:], AX_X, ALU.min))
            c.link(v.scalar_tensor_tensor(moved[:], best[:], THRESHOLD, unmasked[:], ALU.is_ge, ALU.mult))
            c.link(v.tensor_tensor(best_j[:], best_j[:], iota_e, ALU.subtract))
            c.link(v.tensor_tensor(best_j[:], best_j[:], moved[:], ALU.mult))
            c.link(v.tensor_tensor(emap[:], best_j[:], iota_e, ALU.add))
            full = [P, SLOTC, E]
            c.link(v.tensor_tensor(big[:], picked[:].rearrange("p k n e -> p (k n) e"), bc(emap[:], 1, full), ALU.mult))
            c.link(v.tensor_reduce(target[:], big[:], AX_X, ALU.add))
            v.tensor_tensor(routed[:], bc(iota_e, 1, full), bc(target[:], 2, full), ALU.is_equal).then_inc(routed_ready, 1)
            dve.wait_ge(exp_ready, 1)
            c.link(v.tensor_scalar(den[:], expgap[:], 1.0, None, ALU.add))
            c.link(v.reciprocal(gap[:], den[:]))
            v.tensor_scalar(R.weight[:, 0], gap[:], HALF, None, ALU.mult)
            c.link(v.scalar_tensor_tensor(R.weight[:, 1], expgap[:], HALF, gap[:], ALU.mult, ALU.mult))
            dve.wait_ge(ranked, 1)
            before = ps_before[:].rearrange("p (c e) -> p c e", e=E)
            total = ps_total[:].rearrange("p (c e) -> p c e", e=E)
            for e in range(E):
                ins = v.tensor_tensor_scan(upto[:, 1:, e], ones[:], total[:, :, e], 0.0, ALU.mult, ALU.add)
                c.n += 1
                ins.then_inc(chain_sem, 1)
            dve.wait_ge(chain_sem, c.n)
            c.link(v.tensor_scalar(counts_i[:], upto[:, SLOTC, :], float(P - 1), None, ALU.add))
            c.link(v.tensor_scalar(tiles_i[:], counts_i[:], P.bit_length() - 1, None, ALU.logical_shift_right))
            c.link(v.tensor_copy(tiles[:], tiles_i[:]))
            c.link(v.tensor_tensor_scan(tiles_end[:], ones[:, 0:E], tiles[:], 0.0, ALU.mult, ALU.add))
            c.link(v.tensor_tensor(row0[:], tiles_end[:], tiles[:], ALU.subtract))
            c.link(v.tensor_scalar(row0[:], row0[:], float(P), None, ALU.mult))
            c.link(v.tensor_tensor(big[:], upto[:, 0:SLOTC, :], before, ALU.add))
            c.link(v.tensor_tensor(big[:], big[:], bc(row0[:], 1, full), ALU.add))
            c.link(v.tensor_tensor(big[:], big[:], routed[:], ALU.mult))
            c.link(v.tensor_reduce(place[:], big[:], AX_X, ALU.add))
            c.link(v.tensor_copy(place_i[:], place[:]))
            v.tensor_scalar(lane_i[:], place_i[:], P - 1, None, ALU.bitwise_and)
            c.link(v.tensor_scalar(tile_i[:], place_i[:], P.bit_length() - 1, None, ALU.logical_shift_right))
            v.tensor_copy(lane[:], lane_i[:])
            c.link(v.tensor_copy(tile[:], tile_i[:]))
            def hot(r, b):
                cols = bass.ds(r * CW, CW)
                lanes, tiles_of = [P, CW, P], [P, CW, MT]
                wait(dve, hot_used, r - 1)
                v.tensor_tensor(tile_hot[:, b], bc(T.iota[:, 0:MT], 1, tiles_of), bc(tile[:, cols], 2, tiles_of),
                                ALU.is_equal).then_inc(tile_ready, 1)
                v.tensor_tensor(lane_hot[:, b], bc(T.iota[:], 1, lanes), bc(lane[:, cols], 2, lanes),
                                ALU.is_equal).then_inc(lane_ready, 1)

            table_steps(dve, hot)
            te = [P, MT, E]
            c.link(v.tensor_tensor(ended[:], bc(T.iota[:, 0:MT], 2, te), bc(tiles_end[:], 1, te), ALU.is_ge))
            c.link(v.tensor_reduce(expert_f[:], ended[:], AX_X, ALU.add))
            c.link(v.tensor_scalar(R.expert[:], expert_f[0:1, :], float(E - 1), None, ALU.min))
            dve.wait_ge(table_done, 1)
            found = ps_table[:, 0:MT]
            c.link(v.scalar_tensor_tensor(empty[:], found, 0.0, T.unused_row[:], ALU.is_equal, ALU.mult))
            c.link(v.scalar_tensor_tensor(R.slot[:], found, -1.0, empty[:], ALU.add, ALU.add))
            c.link(v.tensor_scalar(R.token[:], R.slot[:], N - 1, None, ALU.bitwise_and))

        @block.gpsimd
        def _(pool):
            def by_column(r, b):
                cols = bass.ds(r * CW, CW)
                hold(pool, tile_ready, r + 1, T)
                hold(pool, hot_used, r - 1, T)
                nc.gpsimd.tensor_tensor(tile_col[:, b], tile_hot[:, b], bc(T.col_number[:, cols], 2, [P, CW, MT]),
                                        ALU.mult).then_inc(col_ready, 1)
            table_steps(pool, by_column)

        @block.tensor
        def _(pe):
            pe.wait_ge(picked_ready, 1)
            nc.tensor.matmul(ps_count[:, 0:NT * E], T.ones_f[:], picked[:, 0].rearrange("p n e -> p (n e)"),
                             start=True, stop=True).then_inc(counted, 1)
            pe.wait_ge(routed_ready, 1)
            rhs = routed[:].rearrange("p c e -> p (c e)")
            nc.tensor.matmul(ps_before[:], T.lower_bf[:], rhs, start=True, stop=True)
            nc.tensor.matmul(ps_total[:], T.ones_bf[:], rhs, start=True, stop=True).then_inc(ranked, 1)
            pe.wait_ge(lane_ready, 1)
            nc.tensor.matmul(ps_table[:, 0:MT], lane_hot[:, 0, 0, :], zeros[:], start=True, stop=False)

            def add(r, b):
                pe.wait_ge(lane_ready, r + 1)
                pe.wait_ge(col_ready, r + 1)
                pe.wait_ge(number_ready, r + 1)
                for j in range(CW):
                    for number in (tile_col, tile_lane):
                        ins = nc.tensor.matmul(ps_table[:, 0:MT], lane_hot[:, b, j, :], number[:, b, j, :], start=False, stop=False)
                ins.then_inc(hot_used, 1)
            table_steps(pe, add)
            nc.tensor.matmul(ps_table[:, 0:MT], lane_hot[:, 1, 0, :], zeros[:], start=False, stop=True).then_inc(table_done, 1)


def phase_experts(nc, T, tag, R, xn_dram, y_dram):
    with ExitStack() as ctx:
        M = Mem(nc, ctx, tag)
        LAG = 6
        index, target = M.sb("index", [P, U], I32), M.sb("target", [P, U], I32)
        xg = M.sb("xg", [P, U, D])
        xT = M.sb("xT", [P, 2, DC, P])
        sg = M.sb("sg", [P, 2, F])
        hid = M.sb("hid", [P, 2, F])
        hT = M.sb("hT", [P, 2, DC, P])
        y = M.sb("y", [P, U, D])
        psX, psH = M.ps("psX", [P, 512]), M.ps("psH", [P, 512])
        psG = [M.ps(f"psG{i}", [P, 512]) for i in range(2)]
        psY = [M.ps(f"psY{i}", [P, 512]) for i in range(2)]
        x_loaded = [M.sem(f"x_loaded{s}") for s in range(U)]
        y_stored = [M.sem(f"y_stored{s}") for s in range(U)]
        index_ready, target_ready, xt_done, xT_ready, gu_done, sg_ready, hid_ready, ht_done, hT_ready, y_done, y_ready = (
            M.sem(n) for n in ("index_ready", "target_ready", "xt_done", "xT_ready", "gu_done", "sg_ready", "hid_ready", "ht_done",
                               "hT_ready", "y_done", "y_ready"))
        ITS = MT // U
        block = ctx.enter_context(nc.Block())

        def steps(eng, body):
            body(0, False)
            with eng.Fori(1, ITS - 1) as it:
                body(it, False)
            body(ITS - 1, True)

        @block.gpsimd
        def _(pool):
            def gather(it, s):
                t = it * U + s
                hold(pool, xt_done, t + 1 - U, T)
                nc.gpsimd.tensor_copy(index[:, s:s + 1], R.token[:, bass.ds(t, 1)]).then_inc(index_ready, 1)
                hold(pool, index_ready, t + 1, T)
                nc.gpsimd.indirect_dma_start(xg[:, s, :], None, xn_dram,
                                             bass.IndirectOffsetOnAxis(ap=index[:, s:s + 1], axis=0)).then_inc(x_loaded[s], 16)

            def scatter(it, s):
                t = it * U + s
                hold(pool, y_stored[s], it * 16, T)
                nc.gpsimd.tensor_copy(target[:, s:s + 1], R.slot[:, bass.ds(t, 1)]).then_inc(target_ready, 1)
                hold(pool, target_ready, t + 1, T)
                hold(pool, y_ready, t + 1, T)
                nc.gpsimd.indirect_dma_start(y_dram, bass.IndirectOffsetOnAxis(ap=target[:, s:s + 1], axis=0),
                                             y[:, s, :], None).then_inc(y_stored[s], 16)

            def body(it):
                for s in range(U):
                    gather(it, s)
                    if not isinstance(it, int) or it * U + s >= LAG:
                        scatter(it - (LAG + U - 1 - s) // U, (s - LAG) % U)
            for it in range(2):
                body(it)
            with pool.Fori(2, ITS) as it:
                body(it)
            for t in range(MT - LAG, MT):
                scatter(t // U, t % U)
            for s in range(U):
                pool.wait_ge(y_stored[s], 16 * ITS)

        @block.tensor
        def _(pe):
            def transpose_x(it, s):
                t = it * U + s
                pe.wait_ge(x_loaded[s], it * 16 + 16)
                wait(pe, xT_ready, t)
                for c in range(DC):
                    ins = nc.tensor.transpose(psX[:, c * P:(c + 1) * P], xg[:, s, c * P:(c + 1) * P], T.ident[:])
                ins.then_inc(xt_done, 1)

            def transpose_h(t, s):
                pe.wait_ge(hid_ready, t + 1)
                wait(pe, hT_ready, t)
                for c in range(DC):
                    ins = nc.tensor.transpose(psH[:, c * P:(c + 1) * P], hid[:, s % 2, c * P:(c + 1) * P], T.ident[:])
                ins.then_inc(ht_done, 1)

            def gate_up(t, s, e):
                pe.wait_ge(xT_ready, t + 1)
                wait(pe, hid_ready, t - 1)
                for c in range(DC):
                    ins = nc.tensor.matmul(psG[s % 2][:], xT[:, s % 2, c, :], T.wgu[:, c, bass.ds(e, 1), :].rearrange("p a f -> p (a f)"),
                                           start=(c == 0), stop=(c == DC - 1))
                ins.then_inc(gu_done, 1)

            def down(t, s, e):
                pe.wait_ge(hT_ready, t + 1)
                wait(pe, y_ready, t - 1)
                for c in range(DC):
                    ins = nc.tensor.matmul(psY[s % 2][:, 0:D], hT[:, s % 2, c, :], T.wd[:, c, bass.ds(e, 1), :].rearrange("p a f -> p (a f)"),
                                           start=(c == 0), stop=(c == DC - 1))
                ins.then_inc(y_done, 1)

            def expert(t):
                return pe.value_load(R.expert[0:1, bass.ds(t, 1)], min_val=0, max_val=E - 1)

            def body(it, last):
                first = isinstance(it, int) and it == 0
                before = None if first else expert(it * U - 1)
                now = expert(it * U)
                for s in range(U):
                    t = it * U + s
                    if not (last and s == U - 1):
                        transpose_x(it + (s + 1) // U, (s + 1) % U)
                    if before is not None:
                        transpose_h(t - 1, s + 1)
                    gate_up(t, s, now)
                    after = expert(t + 1) if s + 1 < U else None
                    if before is not None:
                        down(t - 1, s + 1, before)
                    before, now = now, after

            transpose_x(0, 0)
            steps(pe, body)
            transpose_h(MT - 1, MT - 1)
            down(MT - 1, MT - 1, expert(MT - 1))

        @block.scalar
        def _(act):
            def copy_x(t, s):
                act.wait_ge(xt_done, t + 1)
                wait(act, gu_done, t - 1)
                nc.scalar.copy(xT[:, s % 2, :, :], psX[:, 0:D].rearrange("p (c t) -> p c t", c=DC)).then_inc(xT_ready, 1)

            def copy_y(it, s, t):
                act.wait_ge(y_done, t + 1)
                wait(act, y_stored[s], it * 16)
                nc.scalar.copy(y[:, s, :], psY[s % 2][:, 0:D]).then_inc(y_ready, 1)

            def body(it, last):
                for s in range(U):
                    t = it * U + s
                    if not (last and s == U - 1):
                        copy_x(t + 1, s + 1)
                    act.wait_ge(gu_done, t + 1)
                    wait(act, hid_ready, t - 1)
                    nc.scalar.activation(sg[:, s % 2, :], psG[s % 2][:, 0:F], ACT.Silu).then_inc(sg_ready, 1)
                    if not (isinstance(t, int) and t == 0):
                        copy_y(it - (s == 0), (s - 1) % U, t - 1)

            copy_x(0, 0)
            steps(act, body)
            copy_y(ITS - 1, U - 1, MT - 1)

        @block.vector
        def _(dve):
            def copy_h(t, s):
                dve.wait_ge(ht_done, t + 1)
                wait(dve, y_done, t - 1)
                nc.vector.tensor_copy(hT[:, s % 2, :, :], psH[:, 0:D].rearrange("p (c t) -> p c t", c=DC)).then_inc(hT_ready, 1)

            def body(it, last):
                for s in range(U):
                    t = it * U + s
                    if not (isinstance(t, int) and t == 0):
                        copy_h(t - 1, s + 1)
                    dve.wait_ge(sg_ready, t + 1)
                    wait(dve, ht_done, t - 1)
                    nc.vector.tensor_tensor(hid[:, s % 2, :], sg[:, s % 2, :], psG[s % 2][:, F:2 * F], ALU.mult).then_inc(hid_ready, 1)

            steps(dve, body)
            copy_h(MT - 1, MT - 1)


def phase_sum(nc, T, tag, R, x, y_dram, out):
    with ExitStack() as ctx:
        M = Mem(nc, ctx, tag)
        yk = M.sb("yk", [P, 2, TOPK, U, D])
        y_loaded = [M.sem(f"y_loaded{b}") for b in range(2)]
        first_added, added, stored = (M.sem(n) for n in ("first_added", "added", "stored"))
        CH = NT // U
        y_view = y_dram[0:TOPK * N, :].rearrange("(k n p) d -> p k n d", p=P, k=TOPK)
        out_view = out.rearrange("(n p) d -> p n d", p=P)
        block = ctx.enter_context(nc.Block())

        @block.sync
        def _(sp):
            def load(c, b):
                for k in range(TOPK):
                    sp.dma_start(yk[:, b, k], y_view[:, k, bass.ds(c * U, U), :]).then_inc(y_loaded[b], 16)

            def store(c, b, more):
                rows = bass.ds(c * U, U)
                hold(sp, added, c * U + U, T)
                if more:
                    load(c + 2, b)
                sp.dma_start(out_view[:, rows, :], x[:, rows, :]).then_inc(stored, 16)

            for b in range(2):
                load(b, b)
            with sp.Fori(0, CH // 2 - 1) as it:
                for b in range(2):
                    store(it * 2 + b, b, True)
            for b in range(2):
                store(CH - 2 + b, b, False)
            sp.wait_ge(stored, 16 * CH)

        @block.vector
        def _(dve):
            with dve.Fori(0, CH // 2) as it:
                for b in range(2):
                    for s in range(U):
                        n = it * (2 * U) + (b * U + s)
                        row = x[:, bass.ds(n, 1), :].rearrange("p a d -> p (a d)")
                        if s == 0:
                            dve.wait_ge(y_loaded[b], it * (16 * TOPK) + 16 * TOPK)
                        nc.vector.scalar_tensor_tensor(row, yk[:, b, 0, s, :], R.weight[:, 0, bass.ds(n, 1)], row,
                                                       ALU.mult, ALU.add).then_inc(first_added, 1)
                    for s in range(U):
                        n = it * (2 * U) + (b * U + s)
                        row = x[:, bass.ds(n, 1), :].rearrange("p a d -> p (a d)")
                        dve.wait_ge(first_added, n + 1)
                        nc.vector.scalar_tensor_tensor(row, yk[:, b, 1, s, :], R.weight[:, 1, bass.ds(n, 1)], row,
                                                       ALU.mult, ALU.add).then_inc(added, 1)


class LayerNorm:

    def __init__(self, nc, T, M):
        self.nc, self.T = nc, T
        self.stats, self.moments = M.sb("stats", [P, U, 6]), M.sb("moments", [P, U, 2])
        self.std, self.rstd = M.sb("std", [P, U]), M.sb("rstd", [P, U])
        self.stats_done, self.var_ready, self.std_ready, self.rstd_ready = (
            M.sem(n) for n in ("stats_done", "var_ready", "std_ready", "rstd_ready"))

    def tile_stats(self, s, rows):
        self.nc.vector.bn_stats(self.stats[:, s:s + 1, :], rows).then_inc(self.stats_done, 1)

    def variance(self, dve, c):
        hold(dve, self.stats_done, c * U + U, self.T)
        for s in range(U):
            self.nc.vector.bn_aggr(self.moments[:, s, :], self.stats[:, s, :]).then_inc(self.var_ready, 1)

    def deviation(self, act, c):
        act.wait_ge(self.var_ready, c * U + U)
        self.nc.scalar.activation(self.std[:], self.moments[:, :, 1], ACT.Sqrt, bias=self.T.eps[:]).then_inc(self.std_ready, 1)

    def reciprocal(self, dve, c):
        dve.wait_ge(self.std_ready, c + 1)
        self.nc.vector.reciprocal(self.rstd[:], self.std[:]).then_inc(self.rstd_ready, 1)
        dve.wait_ge(self.rstd_ready, c + 1)

    def normalised(self, s, out, rows):
        return self.nc.vector.tensor_scalar(out, rows, self.moments[:, s, 0:1], self.rstd[:, s:s + 1], ALU.subtract, ALU.mult)


def phase_qkv(nc, T, tag, R, x, y_dram, qk_dram, v_dram):
    with ExitStack() as ctx:
        M = Mem(nc, ctx, tag)
        ln = LayerNorm(nc, T, M)
        W = U * P
        CH = N // W
        NU = 4
        yk = M.sb("yk", [P, 2, TOPK, U, D])
        xn = M.sb("xn", [P, 2, U, D])
        xT = M.sb("xT", [P, DC, W])
        cT = M.sb("cT", [P, W])
        parts = M.sb("parts", [P, NU, PARTS, W], BF16)
        left = M.sb("left", [P, 2, W])
        vx = M.sb("vx", [P, U, H, VW])
        psT = [M.ps(f"psT{i}", [P, 512]) for i in range(DC)]
        psC = M.ps("psC", [P, 512])
        psU = [M.ps(f"psU{i}", [P, 512]) for i in range(2)]
        psV = [M.ps(f"psV{i}", [P, 512]) for i in range(2)]
        y_loaded = [M.sem(f"y_loaded{b}") for b in range(2)]
        parts_stored = [M.sem(f"parts_stored{u}") for u in range(NU)]
        wset, first_added, added, xn_ready, t_done, xT_ready, c_done, cT_ready, u_done, high_ready, left_ready, mid_ready, \
            low_ready, v_done, v_ready, v_stored = (
                M.sem(n) for n in ("vset", "first_added", "added", "xn_ready", "t_done", "xT_ready", "c_done", "cT_ready",
                                   "u_done", "high_ready", "left_ready", "mid_ready", "low_ready", "v_done", "v_ready", "v_stored"))
        y_view = y_dram[0:TOPK * N, :].rearrange("(k n p) d -> p k n d", p=P, k=TOPK)
        v_view = v_dram.rearrange("(n p) w -> p n w", p=P)
        block = ctx.enter_context(nc.Block())

        def row(c, s):
            return x[:, bass.ds(c * U + s, 1), :].rearrange("p a d -> p (a d)")

        def steps(eng, step):
            for c in range(-2, 2):
                step(c, c % 2, c >= 0, True)
            with eng.Fori(1, CH // 2 - 1) as it:
                for b in range(2):
                    step(it * 2 + b, b, True, True)
            for c in (CH - 2, CH - 1):
                step(c, c % 2, True, False)

        @block.sync
        def _(sp):
            def load(c, b):
                for k in range(TOPK):
                    sp.dma_start(yk[:, b, k], y_view[:, k, bass.ds(c * U, U), :]).then_inc(y_loaded[b], 16)

            def store(c, b, more):
                if more:
                    hold(sp, added, c * U + (2 * U), T)
                    load(c + 3, 1 - b)
                for u in range(NU):
                    hold(sp, low_ready, c * NU + u + 1, T)
                    rows = slice((u % 2) * P, (u % 2) * P + P)
                    sp.dma_start(qk_dram[u // 2, :, rows, bass.ds(c * W, W)].rearrange("a p t -> p a t"),
                                 parts[:, u]).then_inc(parts_stored[u], 16)
                hold(sp, v_ready, c * 2 + 2, T)
                sp.dma_start(v_view[:, bass.ds(c * U, U), :], vx[:].rearrange("p n h w -> p n (h w)")).then_inc(v_stored, 16)

            for c in range(3):
                if c == 2:
                    hold(sp, added, U, T)
                load(c, c % 2)
            with sp.Fori(0, CH // 2 - 2) as it:
                for b in range(2):
                    store(it * 2 + b, b, True)
            for c in range(CH - 4, CH):
                store(c, c % 2, c + 3 < CH)
            for u in range(NU):
                sp.wait_ge(parts_stored[u], 16 * CH)
            sp.wait_ge(v_stored, 16 * CH)

        @block.gpsimd
        def _(pool):
            nc.gpsimd.memset(vx[:], 0.0).then_inc(wset, 1)
            hold(pool, wset, 1, T)
            nc.gpsimd.memset(vx[:, :, :, DK:DK + 1], 1.0).then_inc(wset, 1)

            def step(c, b, now, ahead):
                for u in range(NU if now else 0):
                    hold(pool, mid_ready, c * NU + u + 1, T)
                    nc.gpsimd.tensor_tensor(parts[:, u, 2, :], left[:, u % 2, :], parts[:, u, 1, :],
                                            ALU.subtract).then_inc(low_ready, 1)
            steps(pool, step)

        @block.vector
        def _(dve):
            def step(c, b, now, ahead):
                a = c + 2
                if ahead:
                    dve.wait_ge(y_loaded[b], (a // 2) * (16 * TOPK) + 16 * TOPK)
                    for s in range(U):
                        nc.vector.scalar_tensor_tensor(row(a, s), yk[:, b, 0, s, :], R.weight[:, 0, bass.ds(a * U + s, 1)], row(a, s),
                                                       ALU.mult, ALU.add).then_inc(first_added, 1)
                for s in range(U):
                    if ahead:
                        dve.wait_ge(first_added, a * U + s + 1)
                        nc.vector.scalar_tensor_tensor(row(a, s), yk[:, b, 1, s, :], R.weight[:, 1, bass.ds(a * U + s, 1)], row(a, s),
                                                       ALU.mult, ALU.add).then_inc(added, 1)
                    if now:
                        r = c * NU + s
                        dve.wait_ge(high_ready, r + 1)
                        wait(dve, low_ready, r - 1)
                        nc.vector.tensor_tensor(left[:, s % 2, :], psU[s % 2][:], parts[:, s, 0, :], ALU.subtract).then_inc(left_ready, 1)
                    if ahead:
                        hold(dve, added, a * U + s + 1, T)
                        ln.tile_stats(s, x[:, bass.ds(a * U + s, 1), :])
                if ahead:
                    ln.variance(dve, a)
                    ln.reciprocal(dve, a)
                    for s in range(U):
                        if s == 0:
                            wait(dve, t_done, c + 1)
                        ln.normalised(s, xn[:, b, s, :], row(a, s)).then_inc(xn_ready, 1)
            steps(dve, step)

        @block.tensor
        def _(pe):
            def turn(c, b):
                pe.wait_ge(xn_ready, c * U + U)
                wait(pe, xT_ready, c * DC)
                for k in range(DC):
                    for s in range(U):
                        ins = nc.tensor.transpose(psT[k][:, s * P:(s + 1) * P], xn[:, b, s, k * P:(k + 1) * P], T.ident[:])
                ins.then_inc(t_done, 1)

            def step(c, b, now, ahead):
                if not now:
                    if c == -1:
                        turn(0, 0)
                    return
                pe.wait_ge(xT_ready, c * DC + DC)
                wait(pe, cT_ready, c)
                for k in range(DC):
                    ins = nc.tensor.matmul(psC[:], T.wdown[:, k, :], xT[:, k, :], start=(k == 0), stop=(k == DC - 1))
                ins.then_inc(c_done, 1)
                if not isinstance(c, int) or c + 1 < CH:
                    turn(c + 1, 1 - b)
                pe.wait_ge(cT_ready, c + 1)
                for u in range(NU):
                    wait(pe, left_ready, c * NU + u - 1)
                    rows = slice(0, DL) if u < 2 else slice(DL, 2 * DL)
                    nc.tensor.matmul(psU[u % 2][:], T.wup[rows, (u % 2) * P:(u % 2 + 1) * P], cT[rows, :],
                                     start=True, stop=True).then_inc(u_done, 1)
                    if u % 2 == 0:
                        continue
                    i = u // 2
                    wait(pe, v_ready, c * 2 + i - 1)
                    for s in range(2):
                        ins = nc.tensor.matmul(psV[i][:, s * D:(s + 1) * D], cT[DL:2 * DL, (2 * i + s) * P:(2 * i + s + 1) * P],
                                               T.wuv[DL:2 * DL, :], start=True, stop=True)
                    ins.then_inc(v_done, 1)
            steps(pe, step)

        @block.scalar
        def _(act):
            act.wait_ge(wset, 2)

            def copy_turned(c):
                act.wait_ge(t_done, c + 1)
                wait(act, c_done, c)
                for k in range(DC):
                    nc.scalar.copy(xT[:, k, :], psT[k][:]).then_inc(xT_ready, 1)

            def step(c, b, now, ahead):
                if now:
                    act.wait_ge(c_done, c + 1)
                    wait(act, v_done, c * 2)
                    nc.scalar.copy(cT[:], psC[:]).then_inc(cT_ready, 1)
                    if not isinstance(c, int) or c + 1 < CH:
                        copy_turned(c + 1)
                    for u in range(NU + 1):
                        r = c * NU + u
                        if u < NU:
                            act.wait_ge(u_done, r + 1)
                            wait(act, parts_stored[u], c * 16)
                            nc.scalar.copy(parts[:, u, 0, :], psU[u % 2][:]).then_inc(high_ready, 1)
                        if u:
                            act.wait_ge(left_ready, r)
                            nc.scalar.copy(parts[:, u - 1, 1, :], left[:, (u - 1) % 2, :]).then_inc(mid_ready, 1)
                elif c == -1:
                    copy_turned(0)
                if ahead:
                    ln.deviation(act, c + 2)
                for i in range(2 if now else 0):
                    act.wait_ge(v_done, c * 2 + i + 1)
                    wait(act, v_stored, c * 16)
                    nc.scalar.copy(vx[:, 2 * i:2 * i + 2, :, 0:DK],
                                   psV[i][:].rearrange("p (s h d) -> p s h d", s=2, h=H)).then_inc(v_ready, 1)
            steps(act, step)


def score_units():
    units = []
    for h in range(HG):
        for i in range(QT):
            end = (i + 1) * P
            units.append((h, i, 0, min(end, 512), i))
            if end > 512:
                units.append((h, i, 512, end - 512, i + QT // 2))
    return units


def plan_step(units, later, with_before):
    width = lambda j, c: min((c + 1) * 512, S) - max(c * 512, j * P)
    diag = lambda i, k0, w: k0 + w == (i + 1) * P
    ring = [("s", u, 1) for u in range(AHEAD, len(units))] + [("m", 1)] if later else []
    if later > 1:
        ring += [("s", u, 2) for u in range(AHEAD)]
    if with_before:
        at = 6 if later else 0
        ring[at:at] = [("o", c) for c in range(2)]
    st = [("st", j, c, h) for j in range(QT) for c in range(2) for h in range(HG) if width(j, c) > 0]
    pv = [("pv", j, c) for j in range(QT) for c in range(2) if width(j, c) > 0]
    need_s = sum(units[x[1]][3] for x in ring if x[0] == "s") or 1
    need_t = sum(width(x[1], x[2]) for x in st)
    order, ring_free, st_free = [], [0.0] * RING_BANKS, [0.0] * ST_BANKS
    exp_end, pv_end = {}, {}
    t = dve = act = had_s = had_t = 0.0
    n_ring = n_st = n_pv = 0
    while n_ring < len(ring) or n_st < len(st) or n_pv < len(pv):
        can = []
        if n_ring < len(ring):
            can.append((max(t, ring_free[n_ring % RING_BANKS]), had_s / need_s, "r"))
        if n_st < len(st):
            _, j, c, h = st[n_st]
            slot_free = pv_end.get((j - 2, c), 0.0 if j < 2 else float("inf"))
            can.append((max(t, st_free[n_st % ST_BANKS], slot_free - 300), had_t / need_t, "t"))
        if n_pv < len(pv):
            _, j, c = pv[n_pv]
            ready = max(exp_end.get((j, c, h), float("inf")) for h in range(HG))
            can.append((max(t, ready), 0.0, "p"))
        start, _, what = min(can)
        if what == "r":
            kind, u = ring[n_ring][:2]
            w = units[u][3] + P * diag(*units[u][1:4]) if kind == "s" else 512
            t = start + w / 2.4
            dve = max(dve, t + 200) + 64 + (w if kind == "s" else 900) * 1.04
            ring_free[n_ring % RING_BANKS] = dve + 60
            had_s += units[u][3] if kind == "s" else 0
            order.append(ring[n_ring])
            n_ring += 1
        elif what == "t":
            _, j, c, h = st[n_st]
            w = width(j, c)
            t = start + (w + P * (max(c * 512, j * P) == j * P)) / 2.4
            act = max(act, t + 200) + 100 + w * 0.833
            st_free[n_st % ST_BANKS] = act + 60
            exp_end[j, c, h] = act + 100
            had_t += w
            order.append(st[n_st])
            n_st += 1
        else:
            _, j, c = pv[n_pv]
            t = start + width(j, c) * 4 / 2.4
            pv_end[j, c] = t + 150
            order.append(pv[n_pv])
            n_pv += 1
    return order, [x for x in order if x[0] in "smo"]


def phase_attention(nc, T, tag, qk_dram, v_dram, o_dram):
    with ExitStack() as ctx:
        M = Mem(nc, ctx, tag)
        units = score_units()
        NS = len(units)
        QHALF = QT // 2
        GB = H // HG
        MROW = HG * QT
        n_pv = {(j, c): n for n, (j, c) in enumerate((j, c) for j in range(QT) for c in range(2) if j < QHALF * (c + 1))}
        n_st = {(j, c, h): n * HG + h for (j, c), n in n_pv.items() for h in range(HG)}
        PV, ST = len(n_pv), len(n_st)
        qst = [M.sb(f"qst{s}", [P, HG, S], BF16) for s in range(SLOTS)]
        kst = [M.sb(f"kst{s}", [P, HG, S], BF16) for s in range(SLOTS)]
        vst = [M.sb(f"vst{s}", [P, QT, HG * VW]) for s in range(SLOTS)]
        prob = [M.sb(f"prob{i}", [P, HG, S]) for i in range(2)]
        maxp = M.sb("maxp", [P, HG, QT + QHALF])
        maxq = M.sb("maxq", [P, HG, QT])
        neg, mid = M.sb("neg", [MROW, P]), M.sb("mid", [MROW, P])
        mparts = M.sb("mparts", [MROW, PARTS, P], BF16)
        oT = M.sb("oT", [P, 2, 512])
        orow = M.sb("orow", [P, 2, 512])
        psR = [M.ps(f"psR{i}", [P, 512]) for i in range(RING_BANKS)]
        psS = [M.ps(f"psS{i}", [P, 512]) for i in range(ST_BANKS)]
        psO = [M.ps(f"psO{i}", [P, 512]) for i in range(2)]
        loaded = [M.sem(f"loaded{s}") for s in range(SLOTS)]
        o_stored = [M.sem(f"o_stored{c}") for c in range(2)]
        m_loaded, filled, drained, max_ready, m_ready, st_done, exp_done, pv_done, o_copied, ones_set, chain = (
            M.sem(n) for n in ("m_loaded", "filled", "drained", "max_ready", "m_ready", "st_done", "exp_done", "pv_done",
                               "o_copied", "ones_set", "chain"))
        N_LOADS = 2 * len(Q_PARTS) + 1
        RING0 = NS + 1 + AHEAD
        RING = NS + 3
        CHAIN = 4
        assert RING % RING_BANKS == 0 and ST % ST_BANKS == 0
        block = ctx.enter_context(nc.Block())

        def steps(step):
            def run(eng):
                last = (NG - 1) // SLOTS - 1
                for k in range(SLOTS):
                    step(k, k, 2, k > 0)
                with eng.Fori(1, last) as it:
                    for k in range(SLOTS):
                        step(it * SLOTS + k, k, 2, True)
                for g in range(last * SLOTS, NG):
                    step(g, g % SLOTS, min(2, NG - 1 - g), True)
            return run

        def ring_base(g):
            if isinstance(g, int) and g == 0:
                return RING0
            return g * RING + (RING0 - 2 - (AHEAD if isinstance(g, int) and g == NG - 1 else 0))

        def ring_bank(g, idx):
            return (idx + (ring_base(g) if isinstance(g, int) else RING0 - 2)) % RING_BANKS

        def out_at(g, c):
            if isinstance(g, int) and g == NG - 1:
                return ring_base(g) + 2 + c + 1
            later = min(2, NG - 2 - g) if isinstance(g, int) else 2
            return ring_base(g + 1) + (plan_step(units, later, True)[1].index(("o", c)) + 1)

        @block.sync
        def _(sp):
            def load(g, slot):
                b, hg = g // GB, g % GB
                for kind, st, which in ((0, qst, Q_PARTS), (1, kst, K_PARTS)):
                    for r, part in enumerate(which):
                        src = qk_dram[kind, part, bass.ds(hg * (HG * DK), HG * DK), bass.ds(b * S, S)]
                        sp.dma_start(st[slot][r * DK:(r + 1) * DK, :, :],
                                     src.rearrange("(h d) t -> d h t", d=DK)).then_inc(loaded[slot], 16)
                src = v_dram[bass.ds(b * S, S), bass.ds(hg * (HG * VW), HG * VW)]
                sp.dma_start(vst[slot][:], src.rearrange("(j p) w -> p j w", p=P)).then_inc(loaded[slot], 16)

            def store_out(g):
                b, hg = g // GB, g % GB
                for c in range(2):
                    hold(sp, drained, out_at(g, c), T)
                    dst = o_dram[bass.ds(b * S + c * 512, 512), bass.ds(hg * (HG * VW), HG * VW)]
                    sp.dma_start(dst.rearrange("(i p) w -> p i w", p=P),
                                 orow[:, c, :].rearrange("p (i w) -> p i w", w=HG * VW)).then_inc(o_stored[c], 16)

            def load_max(g, slot):
                hold(sp, m_ready, g + 1, T)
                for part in range(PARTS):
                    sp.dma_start(qst[slot][KROWS + part:KROWS + part + 1, :, :], mparts[:, part, :]).then_inc(m_loaded, 16)

            def step(g, k, later, with_before):
                if with_before:
                    store_out(g - 1)
                if later:
                    load_max(g + 1, (k + 1) % SLOTS)
                if not isinstance(g, int) or g + SLOTS < NG:
                    hold(sp, pv_done, g * PV + PV, T)
                    load(g + SLOTS, k)

            for g in range(SLOTS):
                load(g, g)
            load_max(0, 0)
            steps(step)(sp)
            store_out(NG - 1)
            for c in range(2):
                sp.wait_ge(o_stored[c], 16 * NG)

        @block.gpsimd
        def _(pool):
            for s in range(SLOTS):
                nc.gpsimd.memset(kst[s][KROWS:MROWS, :, :], 1.0).then_inc(ones_set, 1)

        @block.tensor
        def _(pe):
            def score(u, slot, r, bank):
                h, i, k0, w, _ = units[u]
                wait(pe, drained, r + 1 - RING_BANKS)
                diag = k0 + w == (i + 1) * P
                ins = nc.tensor.matmul(psR[bank][:, 0:w], qst[slot][0:KROWS, h, i * P:(i + 1) * P],
                                       kst[slot][0:KROWS, h, k0:k0 + w], start=True, stop=not diag)
                if diag:
                    ins = nc.tensor.matmul(psR[bank][:, w - P:w], T.ident_bf[:], T.causal[:], start=False, stop=True)
                ins.then_inc(filled, 1)

            def turn_max(g, r, bank):
                wait(pe, drained, r + 1 - RING_BANKS)
                pe.wait_ge(max_ready, g + 1)
                nc.tensor.transpose(psR[bank][0:MROW, 0:P], maxq[:].rearrange("p h i -> p (h i)"), T.ident[:]).then_inc(filled, 1)

            def turn_out(g, c, r, bank):
                wait(pe, drained, r + 1 - RING_BANKS)
                pe.wait_ge(o_copied, g * 2 + c + 1)
                for i in range(512 // P):
                    ins = nc.tensor.transpose(psR[bank][:, i * P:(i + 1) * P], oT[:, c, i * P:(i + 1) * P], T.ident[:])
                ins.then_inc(filled, 1)

            def score_t(g, k, j, c, h):
                n, a = n_st[j, c, h], max(c * 512, j * P)
                ps = psS[n % ST_BANKS][:, a - c * 512:512]
                wait(pe, exp_done, g * ST + n + 1 - ST_BANKS)
                ins = nc.tensor.matmul(ps, kst[k][0:MROWS, h, j * P:(j + 1) * P], qst[k][0:MROWS, h, a:(c + 1) * 512],
                                       start=True, stop=a > j * P)
                if a == j * P:
                    ins = nc.tensor.matmul(ps[:, 0:P], T.ident_bf[:], T.causal_t[:], start=False, stop=True)
                ins.then_inc(st_done, 1)

            def pv(g, k, j, c):
                a = max(c * 512, j * P)
                pe.wait_ge(exp_done, g * ST + n_st[j, c, HG - 1] + 1)
                if j == 0:
                    wait(pe, o_copied, g * 2 + c - 1)
                for h in range(HG):
                    ins = nc.tensor.matmul(psO[c][h * VW:(h + 1) * VW, a - c * 512:512],
                                           vst[k][:, j, h * VW:(h + 1) * VW], prob[j % 2][:, h, a:(c + 1) * 512],
                                           start=(j == 0), stop=(j == QHALF * (c + 1) - 1))
                ins.then_inc(pv_done, 1)

            def step(g, k, later, with_before):
                base, idx, asked = ring_base(g), 0, False
                pe.wait_ge(m_loaded, g * (16 * PARTS) + 16 * PARTS)
                for what, *at in plan_step(units, later, with_before)[0]:
                    if what == "st":
                        score_t(g, k, *at)
                        continue
                    if what == "pv":
                        pv(g, k, *at)
                        continue
                    r, bank = base + idx, ring_bank(g, idx)
                    if what == "s":
                        u, ahead = at
                        if ahead == 2 and not asked:
                            pe.wait_ge(loaded[(k + 2) % SLOTS],
                                       ((g - k) // SLOTS) * (16 * N_LOADS) + 16 * N_LOADS * ((k + 2) // SLOTS + 1))
                            asked = True
                        score(u, (k + ahead) % SLOTS, r, bank)
                    elif what == "m":
                        turn_max(g + 1, r, bank)
                    else:
                        turn_out(g - 1, at[0], r, bank)
                    idx += 1

            pe.wait_ge(loaded[0], 16 * N_LOADS)
            for u in range(NS):
                score(u, 0, u, u % RING_BANKS)
            turn_max(0, NS, NS % RING_BANKS)
            pe.wait_ge(loaded[1], 16 * N_LOADS)
            for u in range(AHEAD):
                score(u, 1, NS + 1 + u, (NS + 1 + u) % RING_BANKS)
            pe.wait_ge(ones_set, SLOTS)
            steps(step)(pe)
            for c in range(2):
                turn_out(NG - 1, c, out_at(NG - 1, c) - 1, ring_bank(NG - 1, 2 + c))

        @block.scalar
        def _(act):
            def copy_out(g, c):
                act.wait_ge(pv_done, g * PV + n_pv[QHALF * (c + 1) - 1, c] + 1)
                nc.scalar.copy(oT[:, c, :], psO[c][:]).then_inc(o_copied, 1)

            def step(g, k, later, with_before):
                for (j, c), n in n_pv.items():
                    if j > 1:
                        act.wait_ge(pv_done, g * PV + n_pv[j - 2, c] + 1)
                    else:
                        wait(act, pv_done, (g - 1) * PV + n_pv[j + QHALF * (c + 1) - 2, c] + 1)
                    for h in range(HG):
                        n, a = n_st[j, c, h], max(c * 512, j * P)
                        act.wait_ge(st_done, g * ST + n + 1)
                        nc.scalar.activation(prob[j % 2][:, h, a:(c + 1) * 512], psS[n % ST_BANKS][:, a - c * 512:512], ACT.Exp,
                                             scale=DK ** -0.5).then_inc(exp_done, 1)
                    if j == QHALF + 1:
                        copy_out(g, 0)
                copy_out(g, 1)
            steps(step)(act)

        @block.vector
        def _(dve):
            def link(ins, g, n):
                ins.then_inc(chain, 1)
                dve.wait_ge(chain, g * CHAIN + n)

            def row_max(u, r, bank):
                h, _, _, w, col = units[u]
                dve.wait_ge(filled, r + 1)
                nc.vector.tensor_reduce(maxp[:, h, col:col + 1], psR[bank][:, 0:w], AX_X, ALU.max).then_inc(drained, 1)

            def join_max(g, r):
                dve.wait_ge(drained, r)
                link(nc.vector.tensor_copy(maxq[:, :, 0:QHALF], maxp[:, :, 0:QHALF]), g, 1)
                nc.vector.tensor_tensor(maxq[:, :, QHALF:QT], maxp[:, :, QHALF:QT], maxp[:, :, QT:QT + QHALF],
                                        ALU.max).then_inc(max_ready, 1)

            def split_max(g, r, bank):
                dve.wait_ge(filled, r + 1)
                wait(dve, m_loaded, g * (16 * PARTS))
                nc.vector.tensor_scalar(neg[:], psR[bank][0:MROW, 0:P], -1.0, None, ALU.mult).then_inc(drained, 1)
                dve.wait_ge(drained, r + 1)
                link(nc.vector.tensor_copy(mparts[:, 0], neg[:]), g, 2)
                link(nc.vector.tensor_tensor(mid[:], neg[:], mparts[:, 0], ALU.subtract), g, 3)
                link(nc.vector.tensor_copy(mparts[:, 1], mid[:]), g, 4)
                nc.vector.tensor_tensor(mparts[:, 2], mid[:], mparts[:, 1], ALU.subtract).then_inc(m_ready, 1)

            def copy_rows(g, c, r, bank):
                dve.wait_ge(filled, r + 1)
                wait(dve, o_stored[c], g * 16)
                nc.vector.tensor_copy(orow[:, c, :], psR[bank][:]).then_inc(drained, 1)

            def step(g, k, later, with_before):
                base = ring_base(g)
                for idx, (what, at, *_) in enumerate(plan_step(units, later, with_before)[1]):
                    r, bank = base + idx, ring_bank(g, idx)
                    if what == "s":
                        row_max(at, r, bank)
                    elif what == "m":
                        join_max(g + 1, r)
                        split_max(g + 1, r, bank)
                    else:
                        copy_rows(g - 1, at, r, bank)

            for u in range(NS):
                row_max(u, u, u % RING_BANKS)
            join_max(0, NS)
            split_max(0, NS, NS % RING_BANKS)
            for u in range(AHEAD):
                row_max(u, NS + 1 + u, (NS + 1 + u) % RING_BANKS)
            steps(step)(dve)
            for c in range(2):
                copy_rows(NG - 1, c, out_at(NG - 1, c) - 1, ring_bank(NG - 1, 2 + c))


class Tables:
    pass


def phase_constants(nc, T, M):
    T.ident, T.ident_bf = M.sb("ident", [P, P]), M.sb("ident_bf", [P, P], BF16)
    T.causal, T.causal_t = M.sb("causal", [P, P], BF16), M.sb("causal_t", [P, P], BF16)
    T.lower_bf, T.ones_bf, T.ones_f = M.sb("lower_bf", [P, P], BF16), M.sb("ones_bf", [P, P], BF16), M.sb("ones_f", [P, P])
    iota_i, col_i = M.sb("iota_i", [P, P], I32), M.sb("col_i", [P, SLOTC], I32)
    row_i, lane_i = M.sb("row_i", [P, MT], I32), M.sb("lane_i", [P, 1], I32)
    T.iota, T.eps = M.sb("iota", [P, P]), M.sb("eps", [P, 1])
    T.col_number, T.lane_number = M.sb("col_number", [P, SLOTC]), M.sb("lane_number", [P, 1])
    T.unused_row = M.sb("unused_row", [P, MT])
    made = M.sem("made")
    T.const_ready = M.sem("const_ready")
    T.N_CONST = 1
    with nc.Block() as block:
        @block.gpsimd
        def _(pool):
            g = nc.gpsimd
            c = Chain(pool, made)
            c.link(g.memset(T.ones_f[:], 1.0))
            c.link(g.memset(T.ones_bf[:], 1.0))
            c.link(g.memset(T.causal[:], 0.0))
            c.link(g.memset(T.causal_t[:], 0.0))
            square = [[1, P]]
            c.link(g.affine_select(out=T.ident[:], in_=T.ones_f[:], compare_op=ALU.is_equal, fill=0.0, base=0,
                                   pattern=square, channel_multiplier=-1))
            c.link(g.affine_select(out=T.ident_bf[:], in_=T.ones_bf[:], compare_op=ALU.is_equal, fill=0.0, base=0,
                                   pattern=square, channel_multiplier=-1))
            c.link(g.affine_select(out=T.lower_bf[:], in_=T.ones_bf[:], compare_op=ALU.is_gt, fill=0.0, base=0,
                                   pattern=square, channel_multiplier=-1))
            c.link(g.affine_select(out=T.causal[:], in_=T.causal[:], compare_op=ALU.is_ge, fill=NEG, base=0,
                                   pattern=[[-1, P]], channel_multiplier=1))
            c.link(g.affine_select(out=T.causal_t[:], in_=T.causal_t[:], compare_op=ALU.is_ge, fill=NEG, base=0,
                                   pattern=square, channel_multiplier=-1))
            c.link(g.iota(iota_i[:], [[1, P]], base=0, channel_multiplier=0))
            c.link(g.iota(col_i[:], [[P, SLOTC]], base=0, channel_multiplier=0))
            c.link(g.iota(lane_i[:], [[0, 1]], base=1, channel_multiplier=1))
            c.link(g.iota(row_i[:], [[P, MT]], base=TOPK * N + 1, channel_multiplier=1))
            c.link(g.memset(T.eps[:], EPS))
            c.link(g.tensor_copy(T.iota[:], iota_i[:]))
            c.link(g.tensor_copy(T.col_number[:], col_i[:]))
            c.link(g.tensor_copy(T.lane_number[:], lane_i[:]))
            g.tensor_copy(T.unused_row[:], row_i[:]).then_inc(T.const_ready, 1)



class Routing:

    def __init__(self, M, k):
        self.weight = M.sb(f"weight{k}", [P, TOPK, NT])
        self.token = M.sb(f"token{k}", [P, MT], I32)
        self.slot = M.sb(f"slot{k}", [P, MT], I32)
        self.expert = M.sb(f"expert{k}", [1, MT], I32)


def program(nc, x, W_dq, W_uq, W_dkv, W_uk, W_uv, W_o, gate, gate_up, down, similarity, out):
    with ExitStack() as ctx:
        M = Mem(nc, ctx, "all")
        T = Tables()
        xs = M.sb("x", [P, NT, D])
        logits = M.sb("logits", [P, NT, E])
        R = Routing(M, 0)
        T.gateT, T.simb = M.sb("gateT", [P, DC, E]), M.sb("simb", [P, E, E])
        T.wgu, T.wd = M.sb("wgu", [P, DC, E, 2 * F]), M.sb("wd", [P, DC, E, D])
        T.wdown = M.sb("wdown", [P, DC, 2 * DL])
        T.wup, T.wuv = M.sb("wup", [P, D]), M.sb("wuv", [P, D])
        T.wo = M.sb("wo", [P, DC, D])
        T.w_loaded, T.gate_loaded = M.sem("w_loaded"), M.sem("gate_loaded")
        T.x_loaded = [M.sem(f"x_loaded{i}") for i in range(3)]
        T.holds_passed = {e.engine: M.sem(n) for e, n in ((nc.gpsimd, "pool_holds"), (nc.sync, "sp_holds"), (nc.vector, "dve_holds"))}
        xn_dram = nc.dram_tensor("xn_rows", (N, D), F32).ap()
        y_dram = nc.dram_tensor("y_rows", (TOPK * N + MT * P, D), F32).ap()
        qk_dram = nc.dram_tensor("qk_parts", (2, PARTS, D, N), BF16).ap()
        v_dram = nc.dram_tensor("v_rows", (N, H * VW), F32).ap()
        o_dram = nc.dram_tensor("o_rows", (N, H * VW), F32).ap()
        phase_constants(nc, T, M)
        x_view = x.rearrange("(n p) d -> p n d", p=P)
        split = lambda w: w.rearrange("(c p) n -> p c n", p=P)
        weights = [(T.simb[:].rearrange("p a b -> p (a b)"), similarity.partition_broadcast(P)),
                   (T.wdown[:, :, 0:DL], split(W_dq)), (T.wdown[:, :, DL:2 * DL], split(W_dkv)),
                   (T.wup[0:DL, :], W_uq), (T.wup[DL:2 * DL, :], W_uk), (T.wuv[DL:2 * DL, :], W_uv), (T.wo[:], split(W_o))]
        T.N_W = 16 * (len(weights) + 2 * DC * E)
        assert E == NT // U

        def loads(sp):
            half = NT // 2 + U
            for i, n in ((0, slice(0, U)), (1, slice(U, 2 * U)), (2, slice(2 * U, half)), (2, slice(half, NT))):
                sp.dma_start(xs[:, n, :], x_view[:, n, :]).then_inc(T.x_loaded[i], 16)
                if n.start == 0:
                    sp.dma_start(T.gateT[:], split(gate)).then_inc(T.gate_loaded, 16)
            for dst, src in weights:
                sp.dma_start(dst, src).then_inc(T.w_loaded, 16)

        def load_expert(sp, e):
            for dst, src in ((T.wgu, gate_up), (T.wd, down)):
                for c in range(DC):
                    sp.dma_start(dst[:, c, bass.ds(e, 1), :].rearrange("p a f -> p (a f)"),
                                 src[bass.ds(e, 1), c * P:(c + 1) * P, :].rearrange("a p f -> (a p) f")).then_inc(T.w_loaded, 16)

        def moe(tag, o_rows, first):
            phase_logits(nc, T, tag + "l", xs, xn_dram, logits, o_rows, first)
            phase_route(nc, T, tag + "r", logits, R)
            phase_experts(nc, T, tag + "e", R, xn_dram, y_dram)

        moe("a", None, (loads, load_expert))
        phase_qkv(nc, T, "q", R, xs, y_dram, qk_dram, v_dram)
        phase_attention(nc, T, "t", qk_dram, v_dram, o_dram)
        moe("b", o_dram, None)
        phase_sum(nc, T, "s", R, xs, y_dram, out)


def kernel(L0_attn_x, L0_attn_W_dq, L0_attn_W_uq, L0_attn_W_dkv, L0_attn_W_uk, L0_attn_W_uv, L0_attn_W_o, L0_ffn_gate_weight,
           L0_ffn_gate_up_proj, L0_ffn_down_proj, L0_ffn_similarity_matrix):
    import concourse.bacc as bacc
    import numpy as np
    from concourse.bass_utils import run_bass_kernel_spmd

    rows = np.ascontiguousarray
    arrays = {
        "x": rows(L0_attn_x).reshape(N, D),
        "w_dq": rows(L0_attn_W_dq), "w_uq": rows(L0_attn_W_uq), "w_dkv": rows(L0_attn_W_dkv),
        "w_uk": rows(L0_attn_W_uk), "w_uv": rows(L0_attn_W_uv), "w_o": rows(L0_attn_W_o),
        "gate": rows(np.transpose(L0_ffn_gate_weight)),
        "gate_up": rows(np.transpose(L0_ffn_gate_up_proj, (0, 2, 1))),
        "down": rows(np.transpose(L0_ffn_down_proj, (0, 2, 1))),
        "similarity": rows(L0_ffn_similarity_matrix).reshape(E * E),
    }
    nc = bacc.Bacc("TRN2", target_bir_lowering=False, num_devices=1)
    args = [nc.dram_tensor(f"in_{k}", a.shape, mybir.dt.from_np(a.dtype), kind="ExternalInput").ap() for k, a in arrays.items()]
    out = nc.dram_tensor("out_rows", (N, D), F32, kind="ExternalOutput").ap()
    program(nc, *args, out)
    result = run_bass_kernel_spmd(nc, [{f"in_{k}": a for k, a in arrays.items()}], core_ids=[0])
    return result.results[0]["out_rows"].reshape(B, S, D)
```

```python
from contextlib import ExitStack

import concourse.bass as bass
from concourse import mybir

F32 = mybir.dt.float32
F32R = mybir.dt.float32r
BF16 = mybir.dt.bfloat16
F16 = mybir.dt.float16
I32 = mybir.dt.int32
ALU = mybir.AluOpType
ACT = mybir.ActivationFunctionType
AX_X = mybir.AxisListType.X

P = 128
B, S, D = 4, 1024, 256
N = B * S
NT = N // P
DC = D // P
E = 8
EP = P // 4
F = 256
EW = 2 * F + D
TOPK = 2
SLOTC = TOPK * NT
U = 4
MT = TOPK * N // P + E
H, DK, DL = 16, 16, 64
HG = 4
NG = B * H // HG
QT = S // P
BIG = 3.0e38
NEG = -1.0e30
EPS = 1e-5
THRESHOLD = 0.7
HALF = 0.5
PARTS = 3
Q_PARTS = (0, 0, 0, 1, 1, 2)
K_PARTS = (0, 1, 2, 0, 1, 0)
KROWS = len(Q_PARTS) * DK
MROWS = KROWS + PARTS
VW = 32
OW = DK + 1
SLOTS = 3
RING_BANKS = 3
ST_BANKS = 3
AHEAD = 11
READER_LATENCY = 1000


def wait(eng, sem, value):
    if not isinstance(value, int) or value > 0:
        eng.wait_ge(sem, value)


def hold(eng, sem, value, T):
    wait(eng, sem, value)
    if not isinstance(value, int):
        eng.sem_inc(T.holds_passed[eng.engine], 1)


class Chain:

    def __init__(self, eng, sem):
        self.eng, self.sem, self.n = eng, sem, 0

    def link(self, ins):
        self.n += 1
        ins.then_inc(self.sem, 1)
        self.eng.wait_ge(self.sem, self.n)


class Mem:

    def __init__(self, nc, ctx, tag):
        self.nc, self.ctx, self.tag = nc, ctx, tag

    def sb(self, name, shape, dt=F32):
        return self.ctx.enter_context(self.nc.sbuf_tensor(f"{self.tag}_{name}", shape, dt))

    def ps(self, name, shape, dt=F32):
        return self.ctx.enter_context(self.nc.psum_tensor(f"{self.tag}_{name}", shape, dt))

    def sem(self, name):
        return self.ctx.enter_context(self.nc.semaphore(f"{self.tag}_{name}"))


def bc(ap, axis, shape):
    return ap.unsqueeze(axis).to_broadcast(shape)


class Weights:

    ROUTED = 2

    def __init__(self, nc, T, M, gate_up, down):
        self.nc, self.T = nc, T
        self.sources = ((slice(0, 2 * F), gate_up), (slice(2 * F, EW), down))
        self.parts = [M.sb(f"w{part}", [P, DC, E, EW], F32R) for part in range(2)]
        self.loaded = [M.sem(f"w_loaded{b}") for b in range(2)]
        self.high_ready, self.low_ready = M.sem("w_high"), M.sem("w_low")

    def whole(self, e):
        return self.parts[1][:, :, bass.ds(e, 1), :].bitcast(F32)

    def load(self, sp, e, b):
        hold(sp, self.loaded[b], (e // 2) * 32, self.T)
        for cols, src in self.sources:
            sp.dma_start(self.parts[1][:, :, bass.ds(e, 1), cols].bitcast(F32).rearrange("p c a f -> p (c a) f"),
                         src[bass.ds(e, 1), :, :].rearrange("a (c p) f -> p (a c) f", p=P)).then_inc(self.loaded[b], 16)

    def high(self, act, e, b):
        act.wait_ge(self.loaded[b], (e // 2) * 32 + 32)
        self.nc.scalar.copy(self.parts[0][:, :, bass.ds(e, 1), :], self.whole(e)).then_inc(self.high_ready, 1)

    def low(self, pool, e):
        hold(pool, self.high_ready, e + 1, self.T)
        one = bass.ds(e, 1)
        for k in range(DC):
            self.nc.gpsimd.tensor_tensor(self.parts[1][:, k, one, :], self.parts[1][:, k, one, :].bitcast(F32),
                                         self.parts[0][:, k, one, :], ALU.subtract).then_inc(self.low_ready, 1)


def phase_logits(nc, T, tag, x, xn_dram, logits, W, o_dram=None, loads=None, load_others=None):
    with ExitStack() as ctx:
        M = Mem(nc, ctx, tag)
        ln = LayerNorm(nc, T, M)
        CH = NT // U
        raw, inv = M.sb("raw", [P, 2, U, H, OW]), M.sb("inv", [P, 2, U, H])
        att = M.sb("att", [P, 2, U, H, DK])
        aT = M.sb("aT", [P, U, DC, P])
        xn = M.sb("xn", [P, 2, U, D])
        xT = M.sb("xT", [P, DC, U, P])
        lT = M.sb("lT", [P, P])
        psA, psW, psT, psL = ([M.ps(f"{n}{i}", [P, 512]) for i in range(2)] for n in ("psA", "psW", "psT", "psL"))
        xn_stored = [M.sem(f"xn_stored{b}") for b in range(2)]
        xn_ready, t_done, xT_ready, l_done, l_copied = (M.sem(n) for n in ("xn_ready", "t_done", "xT_ready", "l_done", "l_copied"))
        xn_view = xn_dram.rearrange("(n p) d -> p n d", p=P)
        attended = o_dram is not None
        if attended:
            raw_loaded = [M.sem(f"raw_loaded{b}") for b in range(2)]
            inv_ready, att_ready, at_done, aT_ready, w_done, added = (
                M.sem(n) for n in ("inv_ready", "att_ready", "at_done", "aT_ready", "w_done", "added"))
            o_view = o_dram.rearrange("(n p) w -> p n w", p=P)
        block = ctx.enter_context(nc.Block())

        def row(c, s):
            return x[:, bass.ds(c * U + s, 1), :].rearrange("p a d -> p (a d)")

        def steps(eng, step):
            def has(c):
                return lambda d: not isinstance(c, int) or 0 <= c + d < CH
            for c in range(-2, 2):
                step(c, c % 2, has(c))
            with eng.Fori(1, CH // 2 - 1) as it:
                for b in range(2):
                    step(it * 2 + b, b, has(it))
            for c in range(CH - 2, CH + 2):
                step(c, c % 2, has(c))

        @block.sync
        def _(sp):
            def load(c, b):
                sp.dma_start(raw[:, b].rearrange("p n h w -> p n (h w)"), o_view[:, bass.ds(c * U, U), :]).then_inc(raw_loaded[b], 16)

            def step(c, b, has):
                if attended and has(4):
                    hold(sp, att_ready, c * U + (2 * U + U), T)
                    load(c + 4, b)
                if has(0):
                    hold(sp, xn_ready, c * U + U, T)
                    sp.dma_start(xn_view[:, bass.ds(c * U, U), :], xn[:, b]).then_inc(xn_stored[b], 16)
                    if loads and b == 0 and has(4):
                        loads(sp, c // 2 + 2)
                    W.load(sp, c, b)
                    if loads and isinstance(c, int) and c == CH - 2:
                        load_others(sp)

            for pair in range(2 if loads else 0):
                loads(sp, pair)
            if attended:
                for b in range(2):
                    load(b, b)
            for c in range(-2, 2):
                step(c, c % 2, lambda d: 0 <= c + d < CH)
            with sp.Fori(1, CH // 2 - 2) as it:
                for b in range(2):
                    step(it * 2 + b, b, lambda d: True)
            for c in range(CH - 4, CH):
                step(c, c % 2, lambda d: 0 <= c + d < CH)
            for b in range(2):
                sp.wait_ge(xn_stored[b], 16 * (CH // 2))

        @block.gpsimd
        def _(pool):
            def step(c, b, has):
                if attended and has(2):
                    a = c + 2
                    hold(pool, inv_ready, a + 1, T)
                    hold(pool, at_done, c * U + U, T)
                    for s in range(U):
                        nc.gpsimd.tensor_tensor(att[:, b, s], raw[:, b, s, :, 0:DK], bc(inv[:, b, s, :], 2, [P, H, DK]),
                                                ALU.mult).then_inc(att_ready, 1)
                if has(-2) and has(W.ROUTED - 2):
                    W.low(pool, c - 2)
            steps(pool, step)

        @block.vector
        def _(dve):
            def step(c, b, has):
                if attended and has(2):
                    dve.wait_ge(raw_loaded[b], (c // 2) * 16 + 32)
                    wait(dve, att_ready, c * U + U)
                    nc.vector.reciprocal(inv[:, b], raw[:, b, :, :, DK]).then_inc(inv_ready, 1)
                if not has(0):
                    return
                for s in range(U):
                    if attended:
                        n = c * U + s
                        dve.wait_ge(w_done, n + 1)
                        nc.vector.tensor_tensor(row(c, s), row(c, s), psW[s % 2][:, 0:D], ALU.add).then_inc(added, 1)
                        if s:
                            hold(dve, added, n, T)
                            ln.tile_stats(s - 1, x[:, bass.ds(n - 1, 1), :])
                    else:
                        if s == 0:
                            first = isinstance(c, int) and c < 2
                            dve.wait_ge(T.x_loaded[c if first else 2], 16 if first else (c // 2) * 16)
                        ln.tile_stats(s, x[:, bass.ds(c * U + s, 1), :])
                if attended:
                    hold(dve, added, c * U + U, T)
                    ln.tile_stats(U - 1, x[:, bass.ds(c * U + U - 1, 1), :])
                ln.variance(dve, c)
                ln.reciprocal(dve, c)
                for s in range(U):
                    if s == 0 and (not isinstance(c, int) or c > 1):
                        dve.wait_ge(xn_stored[b], (c // 2) * 16)
                        dve.wait_ge(t_done, c * U - U)
                    ln.normalised(s, xn[:, b, s, :], row(c, s)).then_inc(xn_ready, 1)
            steps(dve, step)

        @block.tensor
        def _(pe):
            pe.wait_ge(T.const_ready, T.N_CONST)
            if loads:
                pe.wait_ge(T.gate_loaded, 16)

            def project(c, s):
                n = c * U + s
                pe.wait_ge(aT_ready, n + 1)
                wait(pe, added, n - 1)
                for k in range(DC):
                    ins = nc.tensor.matmul(psW[s % 2][:, 0:D], aT[:, s, k, :], T.wo[:, k, :], start=(k == 0), stop=(k == DC - 1))
                ins.then_inc(w_done, 1)

            def turn_att(c, b, s):
                n = c * U + s
                pe.wait_ge(att_ready, n + 1)
                wait(pe, aT_ready, n - 1)
                for k in range(DC):
                    ins = nc.tensor.transpose(psA[s % 2][:, k * P:(k + 1) * P],
                                              att[:, b, s].rearrange("p h d -> p (h d)")[:, k * P:(k + 1) * P], T.ident[:])
                ins.then_inc(at_done, 1)

            def turn(c, b, s):
                n = c * U + s
                pe.wait_ge(xn_ready, n + 1)
                wait(pe, xT_ready, n - 1)
                for k in range(DC):
                    ins = nc.tensor.transpose(psT[s % 2][:, k * P:(k + 1) * P], xn[:, b, s, k * P:(k + 1) * P], T.ident[:])
                ins.then_inc(t_done, 1)

            def scores(c):
                pe.wait_ge(xT_ready, c * U + U)
                for k in range(DC):
                    for s in range(U):
                        ins = nc.tensor.matmul(psL[0][s * EP:(s + 1) * EP, 0:P], T.gateT[:, k, :], xT[:, k, s, :],
                                               start=(k == 0), stop=(k == DC - 1))
                ins.then_inc(l_done, 1)

            def turn_scores(c):
                pe.wait_ge(l_copied, c * 2 + 1)
                nc.tensor.transpose(psL[1][:, 0:P], lT[:], T.ident[:]).then_inc(l_done, 1)

            def step(c, b, has):
                if has(-2):
                    scores(c - 2)
                for s in range(U):
                    if attended and has(0):
                        project(c, s)
                    if attended and has(1):
                        turn_att(c + 1, 1 - b, s)
                    if has(-1):
                        turn(c - 1, 1 - b, s)
                    if has(-2) and s == 1:
                        turn_scores(c - 2)
            steps(pe, step)

        @block.scalar
        def _(act):
            def step(c, b, has):
                if has(-2):
                    act.wait_ge(l_done, c * 2 - 3)
                    nc.scalar.copy(lT[:], psL[0][:, 0:P]).then_inc(l_copied, 1)
                for s in range(U):
                    if attended and has(1):
                        n = (c + 1) * U + s
                        act.wait_ge(at_done, n + 1)
                        wait(act, w_done, n + 1 - U)
                        nc.scalar.copy(aT[:, s], psA[s % 2][:, 0:D].rearrange("p (k t) -> p k t", k=DC)).then_inc(aT_ready, 1)
                    if has(-1):
                        n = (c - 1) * U + s
                        act.wait_ge(t_done, n + 1)
                        wait(act, l_done, c * 2 - 3)
                        nc.scalar.copy(xT[:, :, s, :], psT[s % 2][:, 0:D].rearrange("p (k t) -> p k t", k=DC)).then_inc(xT_ready, 1)
                    if has(-2) and s == 1:
                        act.wait_ge(l_done, c * 2 - 2)
                        nc.scalar.copy(logits[:, bass.ds((c - 2) * U, U), :],
                                       psL[1][:, 0:P].rearrange("p (s e) -> p s e", s=U)[:, :, 0:E]).then_inc(l_copied, 1)
                if has(0):
                    ln.deviation(act, c)
                if has(-2) and has(W.ROUTED - 2):
                    W.high(act, c - 2, b)
            steps(act, step)


def phase_route(nc, T, tag, logits, R, W):
    with ExitStack() as ctx:
        M = Mem(nc, ctx, tag)
        shape = [P, NT, E]
        top = [M.sb(f"top{k}", [P, NT]) for k in range(TOPK)]
        choice = [M.sb(f"choice{k}", [P, NT]) for k in range(TOPK)]
        picked = M.sb("picked", [P, TOPK, NT, E])
        work = M.sb("work", [P, NT, E])
        rest = M.sb("rest", [P, NT, E])
        gap, expgap, den = (M.sb(n, [P, NT]) for n in ("gap", "expgap", "den"))
        primary, masked, unmasked = (M.sb(n, [P, E]) for n in ("primary", "masked", "unmasked"))
        sim, simw = M.sb("sim", [P, E, E]), M.sb("simw", [P, E, E])
        best, best_j, moved, emap = (M.sb(n, [P, E]) for n in ("best", "best_j", "moved", "emap"))
        target = M.sb("target", [P, SLOTC])
        routed = M.sb("routed", [P, SLOTC, E], BF16)
        big = M.sb("big", [P, SLOTC, E])
        upto = M.sb("upto", [P, SLOTC + 1, E])
        ones = M.sb("ones", [P, SLOTC])
        zeros = M.sb("zeros", [P, MT], F16)
        counts_i, tiles_i = M.sb("counts_i", [P, E], I32), M.sb("tiles_i", [P, E], I32)
        tiles, tiles_end, row0 = (M.sb(n, [P, E]) for n in ("tiles", "tiles_end", "row0"))
        place, place_i = M.sb("place", [P, SLOTC]), M.sb("place_i", [P, SLOTC], I32)
        lane_i, tile_i = M.sb("lane_i", [P, SLOTC], I32), M.sb("tile_i", [P, SLOTC], I32)
        lane, tile = M.sb("lane", [P, SLOTC], F16), M.sb("tile", [P, SLOTC], F16)
        ended = M.sb("ended", [P, MT, E])
        expert_f = M.sb("expert_f", [P, MT])
        CW = 8
        number16 = M.sb("number16", [P, P, CW], F16)
        lane_hot = M.sb("lane_hot", [P, 2, P, CW], F16)
        tile_hot, tile_col, tile_lane = (M.sb(n, [P, 2, MT, CW], F16) for n in ("tile_hot", "tile_col", "tile_lane"))
        empty = M.sb("empty", [P, MT])
        ps_count, ps_before, ps_total, ps_table = (M.ps(n, [P, 512]) for n in ("ps_count", "ps_before", "ps_total", "ps_table"))
        chain_sem, gap_ready, exp_ready, picked_ready, counted, routed_ready, ranked, hot_ready, col_ready, \
            number_ready, hot_used, table_done = (
                M.sem(n) for n in ("chain", "gap_ready", "exp_ready", "picked_ready", "counted", "routed_ready", "ranked",
                                   "hot_ready", "col_ready", "number_ready", "hot_used", "table_done"))
        block = ctx.enter_context(nc.Block())
        iota_e = T.iota[:, 0:E]

        def table_steps(eng, body):
            for b in range(2):
                body(b, b)
            with eng.Fori(1, SLOTC // CW // 2) as it:
                for b in range(2):
                    body(it * 2 + b, b)

        @block.scalar
        def _(act):
            for e in range(E - W.ROUTED, E):
                W.high(act, e, e % 2)
            act.wait_ge(gap_ready, 1)
            nc.scalar.activation(expgap[:], gap[:], ACT.Exp).then_inc(exp_ready, 1)
            nc.scalar.copy(number16[:], bc(T.iota[:], 2, [P, P, CW])).then_inc(exp_ready, 1)

            def by_lane(r, b):
                act.wait_ge(hot_ready, r * 2 + 1)
                wait(act, hot_used, r - 1)
                nc.scalar.activation(tile_lane[:, b], tile_hot[:, b], ACT.Copy, scale=T.lane_number[:]).then_inc(number_ready, 1)
            table_steps(act, by_lane)

        @block.vector
        def _(dve):
            c = Chain(dve, chain_sem)
            v = nc.vector
            c.link(v.memset(ones[:], 1.0))
            c.link(v.memset(zeros[:], 0.0))
            c.link(v.memset(upto[:, 0, :], 0.0))
            src = logits
            for k in range(TOPK):
                c.link(v.tensor_reduce(top[k][:], src[:], AX_X, ALU.max))
                c.link(v.tensor_tensor(work[:], src[:], bc(top[k][:], 2, shape), ALU.not_equal))
                c.link(v.scalar_tensor_tensor(work[:], work[:], float(E), bc(iota_e, 1, shape), ALU.mult, ALU.add))
                c.link(v.tensor_reduce(choice[k][:], work[:], AX_X, ALU.min))
                ins = v.tensor_tensor(picked[:, k], bc(iota_e, 1, shape), bc(choice[k][:], 2, shape), ALU.is_equal)
                ins.then_inc(picked_ready, 1)
                dve.wait_ge(picked_ready, k + 1)
                if k == 0:
                    c.link(v.scalar_tensor_tensor(rest[:], picked[:, 0], -BIG, logits[:], ALU.mult, ALU.add))
                    src = rest
            v.tensor_tensor(gap[:], top[1][:], top[0][:], ALU.subtract).then_inc(gap_ready, 1)
            dve.wait_ge(counted, 1)
            c.link(v.tensor_reduce(primary[:], ps_count[:, 0:NT * E].rearrange("p (n e) -> p e n", e=E), AX_X, ALU.add))
            c.link(v.tensor_scalar(primary[:], primary[:], 1.0, None, ALU.min))
            v.tensor_scalar(unmasked[:], primary[:], -1.0, 1.0, ALU.mult, ALU.add)
            c.link(v.tensor_scalar(masked[:], primary[:], BIG, -BIG, ALU.mult, ALU.add))
            ee = [P, E, E]
            dve.wait_ge(T.w_loaded, T.N_W)
            c.link(v.tensor_tensor(sim[:], T.simb[:], bc(primary[:], 1, ee), ALU.mult))
            c.link(v.tensor_tensor(sim[:], sim[:], bc(masked[:], 1, ee), ALU.add))
            c.link(v.tensor_reduce(best[:], sim[:], AX_X, ALU.max))
            c.link(v.tensor_tensor(simw[:], sim[:], bc(best[:], 2, ee), ALU.not_equal))
            c.link(v.scalar_tensor_tensor(simw[:], simw[:], float(E), bc(iota_e, 1, ee), ALU.mult, ALU.add))
            c.link(v.tensor_reduce(best_j[:], simw[:], AX_X, ALU.min))
            c.link(v.scalar_tensor_tensor(moved[:], best[:], THRESHOLD, unmasked[:], ALU.is_ge, ALU.mult))
            c.link(v.tensor_tensor(best_j[:], best_j[:], iota_e, ALU.subtract))
            c.link(v.tensor_tensor(best_j[:], best_j[:], moved[:], ALU.mult))
            c.link(v.tensor_tensor(emap[:], best_j[:], iota_e, ALU.add))
            full = [P, SLOTC, E]
            c.link(v.tensor_tensor(big[:], picked[:].rearrange("p k n e -> p (k n) e"), bc(emap[:], 1, full), ALU.mult))
            c.link(v.tensor_reduce(target[:], big[:], AX_X, ALU.add))
            v.tensor_tensor(routed[:], bc(iota_e, 1, full), bc(target[:], 2, full), ALU.is_equal).then_inc(routed_ready, 1)
            dve.wait_ge(exp_ready, 1)
            c.link(v.tensor_scalar(den[:], expgap[:], 1.0, None, ALU.add))
            c.link(v.reciprocal(gap[:], den[:]))
            v.tensor_scalar(R.weight[:, 0], gap[:], HALF, None, ALU.mult)
            c.link(v.scalar_tensor_tensor(R.weight[:, 1], expgap[:], HALF, gap[:], ALU.mult, ALU.mult))
            dve.wait_ge(ranked, 1)
            before = ps_before[:].rearrange("p (c e) -> p c e", e=E)
            total = ps_total[:].rearrange("p (c e) -> p c e", e=E)
            for e in range(E):
                ins = v.tensor_tensor_scan(upto[:, 1:, e], ones[:], total[:, :, e], 0.0, ALU.mult, ALU.add)
                c.n += 1
                ins.then_inc(chain_sem, 1)
            dve.wait_ge(chain_sem, c.n)
            c.link(v.tensor_scalar(counts_i[:], upto[:, SLOTC, :], float(P - 1), None, ALU.add))
            c.link(v.tensor_scalar(tiles_i[:], counts_i[:], P.bit_length() - 1, None, ALU.logical_shift_right))
            c.link(v.tensor_copy(tiles[:], tiles_i[:]))
            c.link(v.tensor_tensor_scan(tiles_end[:], ones[:, 0:E], tiles[:], 0.0, ALU.mult, ALU.add))
            c.link(v.tensor_tensor(row0[:], tiles_end[:], tiles[:], ALU.subtract))
            c.link(v.tensor_scalar(row0[:], row0[:], float(P), None, ALU.mult))
            c.link(v.tensor_tensor(big[:], upto[:, 0:SLOTC, :], before, ALU.add))
            c.link(v.tensor_tensor(big[:], big[:], bc(row0[:], 1, full), ALU.add))
            c.link(v.tensor_tensor(big[:], big[:], routed[:], ALU.mult))
            c.link(v.tensor_reduce(place[:], big[:], AX_X, ALU.add))
            c.link(v.tensor_copy(place_i[:], place[:]))
            v.tensor_scalar(lane_i[:], place_i[:], P - 1, None, ALU.bitwise_and)
            c.link(v.tensor_scalar(tile_i[:], place_i[:], P.bit_length() - 1, None, ALU.logical_shift_right))
            v.tensor_copy(lane[:], lane_i[:])
            c.link(v.tensor_copy(tile[:], tile_i[:]))
            def hot(r, b):
                cols = bass.ds(r * CW, CW)
                lanes, tiles_of = [P, P, CW], [P, MT, CW]
                wait(dve, hot_used, r - 1)
                v.tensor_tensor(tile_hot[:, b], number16[:, 0:MT], bc(tile[:, cols], 1, tiles_of),
                                ALU.is_equal).then_inc(hot_ready, 1)
                v.tensor_tensor(lane_hot[:, b], number16[:], bc(lane[:, cols], 1, lanes),
                                ALU.is_equal).then_inc(hot_ready, 1)

            dve.wait_ge(exp_ready, 2)
            table_steps(dve, hot)
            te = [P, MT, E]
            c.link(v.tensor_tensor(ended[:], bc(T.iota[:, 0:MT], 2, te), bc(tiles_end[:], 1, te), ALU.is_ge))
            c.link(v.tensor_reduce(expert_f[:], ended[:], AX_X, ALU.add))
            c.link(v.tensor_scalar(R.expert[:], expert_f[0:1, :], float(E - 1), None, ALU.min))
            dve.wait_ge(table_done, 1)
            found = ps_table[:, 0:MT]
            c.link(v.scalar_tensor_tensor(empty[:], found, 0.0, T.unused_row[:], ALU.is_equal, ALU.mult))
            c.link(v.scalar_tensor_tensor(R.slot[:], found, -1.0, empty[:], ALU.add, ALU.add))
            c.link(v.tensor_scalar(R.token[:], R.slot[:], N - 1, None, ALU.bitwise_and))

        @block.gpsimd
        def _(pool):
            def by_column(r, b):
                cols = bass.ds(r * CW, CW)
                hold(pool, hot_ready, r * 2 + 1, T)
                hold(pool, hot_used, r - 1, T)
                nc.gpsimd.tensor_tensor(tile_col[:, b], tile_hot[:, b], bc(T.col_number[:, cols], 1, [P, MT, CW]),
                                        ALU.mult).then_inc(col_ready, 1)
            for e in range(E - W.ROUTED, E):
                W.low(pool, e)
            table_steps(pool, by_column)

        @block.tensor
        def _(pe):
            pe.wait_ge(picked_ready, 1)
            nc.tensor.matmul(ps_count[:, 0:NT * E], T.ones_f[:], picked[:, 0].rearrange("p n e -> p (n e)"),
                             start=True, stop=True).then_inc(counted, 1)
            pe.wait_ge(routed_ready, 1)
            rhs = routed[:].rearrange("p c e -> p (c e)")
            nc.tensor.matmul(ps_before[:], T.lower_bf[:], rhs, start=True, stop=True)
            nc.tensor.matmul(ps_total[:], T.ones_bf[:], rhs, start=True, stop=True).then_inc(ranked, 1)
            pe.wait_ge(hot_ready, 2)
            nc.tensor.matmul(ps_table[:, 0:MT], lane_hot[:, 0, :, 0], zeros[:], start=True, stop=False)

            def add(r, b):
                pe.wait_ge(hot_ready, r * 2 + 2)
                pe.wait_ge(col_ready, r + 1)
                pe.wait_ge(number_ready, r + 1)
                for j in range(CW):
                    for number in (tile_col, tile_lane):
                        ins = nc.tensor.matmul(ps_table[:, 0:MT], lane_hot[:, b, :, j], number[:, b, :, j], start=False, stop=False)
                ins.then_inc(hot_used, 1)
            table_steps(pe, add)
            nc.tensor.matmul(ps_table[:, 0:MT], lane_hot[:, 1, :, 0], zeros[:], start=False, stop=True).then_inc(table_done, 1)


def phase_experts(nc, T, tag, R, W, xn_dram, y_dram):
    with ExitStack() as ctx:
        M = Mem(nc, ctx, tag)
        UT = 8
        ITS = MT // UT
        RING = 4
        index, target = M.sb("index", [P, UT], I32), M.sb("target", [P, UT], I32)
        xg = M.sb("xg", [P, RING, D])
        xT = [M.sb(f"xT{part}", [P, 2, DC, P], F32R) for part in range(2)]
        hT = [M.sb(f"hT{part}", [P, 2, DC, P], F32R) for part in range(2)]
        sg = M.sb("sg", [P, 2, F])
        hid = M.sb("hid", [P, 2, F])
        y = M.sb("y", [P, RING, D])
        psX, psH, psG, psY = ([M.ps(f"{n}{i}", [P, 512]) for i in range(2)] for n in ("psX", "psH", "psG", "psY"))
        x_loaded, y_stored = ([M.sem(f"{n}{i}") for i in range(RING)] for n in ("x_loaded", "y_stored"))
        index_ready, xt_done, xhigh_ready, xlow_ready, gu_done, sg_ready, hid_ready, ht_done, hhigh_ready, hlow_ready, y_done, \
            y_ready = (
                M.sem(n) for n in ("index_ready", "xt_done", "xhigh_ready", "xlow_ready", "gu_done", "sg_ready", "hid_ready",
                                   "ht_done", "hhigh_ready", "hlow_ready", "y_done", "y_ready"))
        block = ctx.enter_context(nc.Block())

        def steps(body, eng):
            body(0)
            with eng.Fori(1, ITS - 1) as it:
                body(it)
            body(ITS - 1)

        def some(t):
            return not isinstance(t, int) or 0 <= t < MT

        def chunks(ps):
            return ps[:, 0:D].rearrange("p (c t) -> p c t", c=DC)

        @block.gpsimd
        def _(pool):
            def indices(it, s):
                t, cols = it * UT + s, slice(s, s + RING)
                first = isinstance(it, int) and it == 0
                hold(pool, xt_done, t + 1 - RING, T)
                nc.gpsimd.tensor_copy(index[:, cols], R.token[:, bass.ds(t, RING)]).then_inc(index_ready, 1)
                if not first:
                    places(it, s)
                hold(pool, index_ready, UT // RING + (it - 1) * (2 * UT // RING) + 2 * (s // RING) + 2 if not first else s // RING + 1, T)

            def places(it, s):
                for i in range(RING):
                    hold(pool, y_stored[i], (it - 2) * (16 * UT // RING) + 16 * (s // RING) + 16, T)
                nc.gpsimd.tensor_copy(target[:, s:s + RING], R.slot[:, bass.ds(it * UT + s - UT, RING)]).then_inc(index_ready, 1)

            def gather(it, s):
                i = s % RING
                hold(pool, xt_done, it * UT + s + 1 - RING, T)
                nc.gpsimd.indirect_dma_start(xg[:, i, :], None, xn_dram,
                                             bass.IndirectOffsetOnAxis(ap=index[:, s:s + 1], axis=0)).then_inc(x_loaded[i], 16)

            def scatter(it, s):
                i = s % RING
                hold(pool, y_ready, it * UT + s + 1, T)
                nc.gpsimd.indirect_dma_start(y_dram, bass.IndirectOffsetOnAxis(ap=target[:, s:s + 1], axis=0),
                                             y[:, i, :], None).then_inc(y_stored[i], 16)

            def body(it):
                for s in range(UT):
                    if s % RING == 0:
                        indices(it, s)
                    gather(it, s)
                    if not isinstance(it, int) or it > 0:
                        scatter(it - 1, s)

            body(0)
            body(1)
            with pool.Fori(2, ITS) as it:
                body(it)
            for s in range(UT):
                if s % RING == 0:
                    places(ITS, s)
                    pool.wait_ge(index_ready, UT // RING + (ITS - 1) * (2 * UT // RING) + s // RING + 1)
                scatter(ITS - 1, s)
            for i in range(RING):
                pool.wait_ge(y_stored[i], 16 * (MT // RING))

        @block.tensor
        def _(pe):
            def transpose_x(it, s):
                t = it * UT + s
                pe.wait_ge(x_loaded[s % RING], it * (16 * UT // RING) + 16 * (s // RING) + 16)
                wait(pe, xlow_ready, t - 1)
                for c in range(DC):
                    ins = nc.tensor.transpose(psX[s % 2][:, c * P:(c + 1) * P], xg[:, s % RING, c * P:(c + 1) * P], T.ident[:])
                ins.then_inc(xt_done, 1)

            def transpose_h(t, s):
                pe.wait_ge(hid_ready, t + 1)
                wait(pe, hlow_ready, t - 1)
                for c in range(DC):
                    ins = nc.tensor.transpose(psH[s % 2][:, c * P:(c + 1) * P], hid[:, s % 2, c * P:(c + 1) * P], T.ident[:])
                ins.then_inc(ht_done, 1)

            def product(out, lhsT, s, e, cols):
                passes = [(a, b, c) for c in range(DC) for a, b in ((0, 0), (0, 1), (1, 0))]
                for n, (a, b, c) in enumerate(passes):
                    ins = nc.tensor.matmul(out, lhsT[a][:, s % 2, c, :], W.parts[b][:, c, bass.ds(e, 1), cols].rearrange("p a f -> p (a f)"),
                                           start=(n == 0), stop=(n == len(passes) - 1))
                return ins

            def gate_up(t, s, e):
                pe.wait_ge(xlow_ready, t + 1)
                wait(pe, hid_ready, t - 1)
                product(psG[s % 2][:], xT, s, e, slice(0, 2 * F)).then_inc(gu_done, 1)

            def down(t, s, e):
                pe.wait_ge(hlow_ready, t + 1)
                wait(pe, y_ready, t - 1)
                product(psY[s % 2][:, 0:D], hT, s, e, slice(2 * F, EW)).then_inc(y_done, 1)

            def expert(t):
                return pe.value_load(R.expert[0:1, bass.ds(t, 1)], min_val=0, max_val=E - 1)

            def body(it):
                t0 = it * UT
                experts = [expert(t0 + d) if some(t0 + d) else None for d in (-2, -1, 0)]
                for s in range(UT):
                    t = t0 + s
                    gate_up(t, s, experts[s + 2])
                    if s + 1 < UT:
                        experts.append(expert(t + 1))
                    if some(t - 1):
                        transpose_h(t - 1, s + 1)
                    if some(t + 2):
                        transpose_x(it + (s + 2) // UT, (s + 2) % UT)
                    if some(t - 2):
                        down(t - 2, s, experts[s])

            for s in range(2):
                transpose_x(0, s)
            steps(body, pe)
            transpose_h(MT - 1, MT - 1)
            for t in (MT - 2, MT - 1):
                down(t, t, expert(t))

        @block.scalar
        def _(act):
            def high_x(t, s):
                act.wait_ge(xt_done, t + 1)
                wait(act, gu_done, t - 1)
                nc.scalar.copy(xT[0][:, s % 2], chunks(psX[s % 2])).then_inc(xhigh_ready, 1)

            def high_h(t, s):
                act.wait_ge(ht_done, t + 1)
                wait(act, y_done, t - 1)
                nc.scalar.copy(hT[0][:, s % 2], chunks(psH[s % 2])).then_inc(hhigh_ready, 1)

            def copy_y(it, s):
                t = it * UT + s
                act.wait_ge(y_done, t + 1)
                wait(act, y_stored[s % RING], it * (16 * UT // RING) + 16 * (s // RING))
                nc.scalar.copy(y[:, s % RING, :], psY[s % 2][:, 0:D]).then_inc(y_ready, 1)

            def body(it):
                for s in range(UT):
                    t = it * UT + s
                    act.wait_ge(gu_done, t + 1)
                    wait(act, hid_ready, t - 1)
                    nc.scalar.activation(sg[:, s % 2, :], psG[s % 2][:, 0:F], ACT.Silu).then_inc(sg_ready, 1)
                    if some(t - 1):
                        high_h(t - 1, s + 1)
                    if some(t + 2):
                        high_x(t + 2, s)
                    if some(t - 2):
                        copy_y(it - (s < 2), (s - 2) % UT)

            for s in range(2):
                high_x(s, s)
            steps(body, act)
            high_h(MT - 1, MT - 1)
            for s in (UT - 2, UT - 1):
                copy_y(ITS - 1, s)

        @block.vector
        def _(dve):
            def low_x(t, s):
                dve.wait_ge(xhigh_ready, t + 1)
                nc.vector.tensor_tensor(xT[1][:, s % 2], chunks(psX[s % 2]), xT[0][:, s % 2], ALU.subtract).then_inc(xlow_ready, 1)

            def low_h(t, s):
                dve.wait_ge(hhigh_ready, t + 1)
                nc.vector.tensor_tensor(hT[1][:, s % 2], chunks(psH[s % 2]), hT[0][:, s % 2], ALU.subtract).then_inc(hlow_ready, 1)

            def body(it):
                for s in range(UT):
                    t = it * UT + s
                    dve.wait_ge(sg_ready, t + 1)
                    wait(dve, ht_done, t - 1)
                    nc.vector.tensor_tensor(hid[:, s % 2, :], sg[:, s % 2, :], psG[s % 2][:, F:2 * F], ALU.mult).then_inc(hid_ready, 1)
                    if some(t - 1):
                        low_h(t - 1, s + 1)
                    if some(t + 2):
                        low_x(t + 2, s)

            for s in range(2):
                low_x(s, s)
            steps(body, dve)
            low_h(MT - 1, MT - 1)


def phase_sum(nc, T, tag, R, x, y_dram, out):
    with ExitStack() as ctx:
        M = Mem(nc, ctx, tag)
        yk = M.sb("yk", [P, 2, TOPK, U, D])
        y_loaded = [M.sem(f"y_loaded{b}") for b in range(2)]
        first_added, added, stored = (M.sem(n) for n in ("first_added", "added", "stored"))
        CH = NT // U
        y_view = y_dram[0:TOPK * N, :].rearrange("(k n p) d -> p k n d", p=P, k=TOPK)
        out_view = out.rearrange("(n p) d -> p n d", p=P)
        block = ctx.enter_context(nc.Block())

        @block.sync
        def _(sp):
            def load(c, b):
                for k in range(TOPK):
                    sp.dma_start(yk[:, b, k], y_view[:, k, bass.ds(c * U, U), :]).then_inc(y_loaded[b], 16)

            def store(c, b, more):
                rows = bass.ds(c * U, U)
                hold(sp, added, c * U + U, T)
                if more:
                    load(c + 2, b)
                sp.dma_start(out_view[:, rows, :], x[:, rows, :]).then_inc(stored, 16)

            for b in range(2):
                load(b, b)
            with sp.Fori(0, CH // 2 - 1) as it:
                for b in range(2):
                    store(it * 2 + b, b, True)
            for b in range(2):
                store(CH - 2 + b, b, False)
            sp.wait_ge(stored, 16 * CH)

        @block.vector
        def _(dve):
            with dve.Fori(0, CH // 2) as it:
                for b in range(2):
                    for s in range(U):
                        n = it * (2 * U) + (b * U + s)
                        row = x[:, bass.ds(n, 1), :].rearrange("p a d -> p (a d)")
                        if s == 0:
                            dve.wait_ge(y_loaded[b], it * (16 * TOPK) + 16 * TOPK)
                        nc.vector.scalar_tensor_tensor(row, yk[:, b, 0, s, :], R.weight[:, 0, bass.ds(n, 1)], row,
                                                       ALU.mult, ALU.add).then_inc(first_added, 1)
                    for s in range(U):
                        n = it * (2 * U) + (b * U + s)
                        row = x[:, bass.ds(n, 1), :].rearrange("p a d -> p (a d)")
                        dve.wait_ge(first_added, n + 1)
                        nc.vector.scalar_tensor_tensor(row, yk[:, b, 1, s, :], R.weight[:, 1, bass.ds(n, 1)], row,
                                                       ALU.mult, ALU.add).then_inc(added, 1)


class LayerNorm:

    def __init__(self, nc, T, M):
        self.nc, self.T = nc, T
        self.stats, self.moments = M.sb("stats", [P, U, 6]), M.sb("moments", [P, U, 2])
        self.std, self.rstd = M.sb("std", [P, U]), M.sb("rstd", [P, U])
        self.stats_done, self.var_ready, self.std_ready = (M.sem(n) for n in ("stats_done", "var_ready", "std_ready"))

    def tile_stats(self, s, rows):
        self.nc.vector.bn_stats(self.stats[:, s:s + 1, :], rows).then_inc(self.stats_done, 1)

    def variance(self, dve, c):
        hold(dve, self.stats_done, c * U + U, self.T)
        for s in range(U):
            self.nc.vector.bn_aggr(self.moments[:, s, :], self.stats[:, s, :]).then_inc(self.var_ready, 1)

    def deviation(self, act, c):
        act.wait_ge(self.var_ready, c * U + U)
        self.nc.scalar.activation(self.std[:], self.moments[:, :, 1], ACT.Sqrt, bias=self.T.eps[:]).then_inc(self.std_ready, 1)

    def reciprocal(self, dve, c):
        dve.wait_ge(self.std_ready, c * 2 + 1)
        self.nc.vector.reciprocal(self.rstd[:], self.std[:]).then_inc(self.std_ready, 1)
        dve.wait_ge(self.std_ready, c * 2 + 2)

    def normalised(self, s, out, rows):
        return self.nc.vector.tensor_scalar(out, rows, self.moments[:, s, 0:1], self.rstd[:, s:s + 1], ALU.subtract, ALU.mult)


class Stacks:
    GB = H // HG
    N_LOADS = len(Q_PARTS) + len(K_PARTS) + 1

    def __init__(self, M, qk_dram, v_dram):
        self.qk_dram, self.v_dram = qk_dram, v_dram
        self.qst = [M.sb(f"qst{s}", [P, HG, S], BF16) for s in range(SLOTS)]
        self.kst = [M.sb(f"kst{s}", [P, HG, S], BF16) for s in range(SLOTS)]
        self.v_rows = [M.sb(f"v_rows{s}", [P, QT, HG * DK]) for s in range(SLOTS)]
        self.loaded = [M.sem(f"loaded{s}") for s in range(SLOTS)]

    def load(self, sp, g, slot):
        b, hg = g // self.GB, g % self.GB
        for kind, st, which in ((0, self.qst, Q_PARTS), (1, self.kst, K_PARTS)):
            for r, part in enumerate(which):
                src = self.qk_dram[kind, part, bass.ds(hg * (HG * DK), HG * DK), bass.ds(b * S, S)]
                sp.dma_start(st[slot][r * DK:(r + 1) * DK, :, :],
                             src.rearrange("(h d) t -> d h t", d=DK)).then_inc(self.loaded[slot], 16)
        src = self.v_dram[bass.ds(b * S, S), bass.ds(hg * (HG * DK), HG * DK)]
        sp.dma_start(self.v_rows[slot][:], src.rearrange("(j p) w -> p j w", p=P)).then_inc(self.loaded[slot], 16)


def phase_qkv(nc, T, tag, R, x, y_dram, A):
    with ExitStack() as ctx:
        M = Mem(nc, ctx, tag)
        ln = LayerNorm(nc, T, M)
        W = U * P
        CH = N // W
        NU = 4
        yk = M.sb("yk", [P, 2, TOPK, U, D])
        xn = M.sb("xn", [P, 2, U, D])
        xT = M.sb("xT", [P, DC, W])
        cT = M.sb("cT", [P, 2, W])
        parts = M.sb("parts", [P, NU, PARTS, W], BF16)
        left = M.sb("left", [P, 2, W])
        vx = M.sb("vx", [P, 2, U, D])
        psT = [M.ps(f"psT{i}", [P, 512]) for i in range(DC)]
        psC = M.ps("psC", [P, 512])
        psU = [M.ps(f"psU{i}", [P, 512]) for i in range(2)]
        psV = [M.ps(f"psV{i}", [P, 512]) for i in range(2)]
        y_loaded = [M.sem(f"y_loaded{b}") for b in range(2)]
        parts_stored = [M.sem(f"parts_stored{u}") for u in range(NU)]
        first_added, added, xn_ready, t_done, xT_ready, c_done, cT_ready, u_done, high_ready, left_ready, mid_ready, \
            low_ready, v_done, v_ready = (
                M.sem(n) for n in ("first_added", "added", "xn_ready", "t_done", "xT_ready", "c_done", "cT_ready",
                                   "u_done", "high_ready", "left_ready", "mid_ready", "low_ready", "v_done", "v_ready"))
        v_stored = [M.sem(f"v_stored{b}") for b in range(2)]
        y_view = y_dram[0:TOPK * N, :].rearrange("(k n p) d -> p k n d", p=P, k=TOPK)
        qk_dram, v_dram = A.qk_dram, A.v_dram
        v_view = v_dram.rearrange("(n p) w -> p n w", p=P)
        block = ctx.enter_context(nc.Block())

        def row(c, s):
            return x[:, bass.ds(c * U + s, 1), :].rearrange("p a d -> p (a d)")

        def steps(eng, step):
            for c in range(-2, 2):
                step(c, c % 2, c >= 0, True)
            with eng.Fori(1, CH // 2 - 1) as it:
                for b in range(2):
                    step(it * 2 + b, b, True, True)
            for c in (CH - 2, CH - 1):
                step(c, c % 2, True, False)

        @block.sync
        def _(sp):
            def load(c, b):
                for k in range(TOPK):
                    sp.dma_start(yk[:, b, k], y_view[:, k, bass.ds(c * U, U), :]).then_inc(y_loaded[b], 16)

            def store(c, b, more):
                if more:
                    hold(sp, added, c * U + (2 * U), T)
                    load(c + 3, 1 - b)
                for u in range(NU):
                    hold(sp, low_ready, c * NU + u + 1, T)
                    rows = slice((u % 2) * P, (u % 2) * P + P)
                    sp.dma_start(qk_dram[u // 2, :, rows, bass.ds(c * W, W)].rearrange("a p t -> p a t"),
                                 parts[:, u]).then_inc(parts_stored[u], 16)
                hold(sp, v_ready, c * 2 + 2, T)
                sp.dma_start(v_view[:, bass.ds(c * U, U), :], vx[:, b]).then_inc(v_stored[b], 16)

            for c in range(3):
                if c == 2:
                    hold(sp, added, U, T)
                load(c, c % 2)
            with sp.Fori(0, CH // 2 - 2) as it:
                for b in range(2):
                    store(it * 2 + b, b, True)
            for c in range(CH - 4, CH):
                store(c, c % 2, c + 3 < CH)
                if c == CH - 2:
                    A.load(sp, 0, 0)
            for u in range(NU):
                sp.wait_ge(parts_stored[u], 16 * CH)
            for b in range(2):
                sp.wait_ge(v_stored[b], 16 * (CH // 2))

        @block.gpsimd
        def _(pool):
            def step(c, b, now, ahead):
                for u in range(NU if now else 0):
                    hold(pool, mid_ready, c * NU + u + 1, T)
                    nc.gpsimd.tensor_tensor(parts[:, u, 2, :], left[:, u % 2, :], parts[:, u, 1, :],
                                            ALU.subtract).then_inc(low_ready, 1)
            steps(pool, step)

        @block.vector
        def _(dve):
            def step(c, b, now, ahead):
                a = c + 2

                def stats(s):
                    hold(dve, added, a * U + s + 1, T)
                    ln.tile_stats(s, x[:, bass.ds(a * U + s, 1), :])

                for s in range(U):
                    if now:
                        r = c * NU + s
                        dve.wait_ge(high_ready, r + 1)
                        wait(dve, low_ready, r - 1)
                        nc.vector.tensor_tensor(left[:, s % 2, :], psU[s % 2][:], parts[:, s, 0, :], ALU.subtract).then_inc(left_ready, 1)
                    if ahead:
                        weight = [R.weight[:, k, bass.ds(a * U + s, 1)] for k in range(TOPK)]
                        if s == 0:
                            dve.wait_ge(y_loaded[b], (a // 2) * (16 * TOPK) + 16 * TOPK)
                        nc.vector.scalar_tensor_tensor(row(a, s), yk[:, b, 0, s, :], weight[0], row(a, s),
                                                       ALU.mult, ALU.add).then_inc(first_added, 1)
                        if s:
                            stats(s - 1)
                        dve.wait_ge(first_added, a * U + s + 1)
                        nc.vector.scalar_tensor_tensor(row(a, s), yk[:, b, 1, s, :], weight[1], row(a, s),
                                                       ALU.mult, ALU.add).then_inc(added, 1)
                if ahead:
                    stats(U - 1)
                if ahead:
                    ln.variance(dve, a)
                    ln.reciprocal(dve, a)
                    for s in range(U):
                        if s == 0:
                            wait(dve, t_done, c + 1)
                        ln.normalised(s, xn[:, b, s, :], row(a, s)).then_inc(xn_ready, 1)
            steps(dve, step)

        @block.tensor
        def _(pe):
            def turn(c, b):
                pe.wait_ge(xn_ready, c * U + U)
                wait(pe, xT_ready, c * DC)
                for k in range(DC):
                    for s in range(U):
                        ins = nc.tensor.transpose(psT[k][:, s * P:(s + 1) * P], xn[:, b, s, k * P:(k + 1) * P], T.ident[:])
                ins.then_inc(t_done, 1)

            def latents(c, b):
                pe.wait_ge(xT_ready, c * DC + DC)
                wait(pe, cT_ready, c)
                for k in range(DC):
                    ins = nc.tensor.matmul(psC[:], T.wdown[:, k, :], xT[:, k, :], start=(k == 0), stop=(k == DC - 1))
                ins.then_inc(c_done, 1)

            def up(c, b, u):
                pe.wait_ge(cT_ready, c + 1)
                wait(pe, left_ready, c * NU + u - 1)
                rows = slice(0, DL) if u < 2 else slice(DL, 2 * DL)
                nc.tensor.matmul(psU[u % 2][:], T.wup[rows, (u % 2) * P:(u % 2 + 1) * P], cT[rows, b, :],
                                 start=True, stop=True).then_inc(u_done, 1)

            def values(c, b, i):
                wait(pe, v_ready, c * 2 + i - 1)
                for s in range(2):
                    ins = nc.tensor.matmul(psV[i][:, s * D:(s + 1) * D], cT[DL:2 * DL, b, (2 * i + s) * P:(2 * i + s + 1) * P],
                                           T.wuv[DL:2 * DL, :], start=True, stop=True)
                ins.then_inc(v_done, 1)

            def step(c, b, now, ahead):
                more = not isinstance(c, int) or c + 1 < CH
                if not now:
                    if c == -1:
                        turn(0, 0)
                        latents(0, 0)
                    return
                up(c, b, 0)
                up(c, b, 1)
                values(c, b, 0)
                if more:
                    turn(c + 1, 1 - b)
                up(c, b, 2)
                up(c, b, 3)
                if more:
                    latents(c + 1, 1 - b)
                values(c, b, 1)
            steps(pe, step)

        @block.scalar
        def _(act):
            def copy_turned(c):
                act.wait_ge(t_done, c + 1)
                wait(act, c_done, c)
                for k in range(DC):
                    nc.scalar.copy(xT[:, k, :], psT[k][:]).then_inc(xT_ready, 1)

            def copy_latents(c, b):
                act.wait_ge(c_done, c + 1)
                wait(act, v_done, (c - 1) * 2)
                nc.scalar.copy(cT[:, b], psC[:]).then_inc(cT_ready, 1)

            def high(c, u):
                r = c * NU + u
                act.wait_ge(u_done, r + 1)
                wait(act, parts_stored[u], c * 16)
                nc.scalar.copy(parts[:, u, 0, :], psU[u % 2][:]).then_inc(high_ready, 1)

            def middle(c, u):
                act.wait_ge(left_ready, c * NU + u + 1)
                nc.scalar.copy(parts[:, u, 1, :], left[:, u % 2, :]).then_inc(mid_ready, 1)

            def copy_values(c, b, i):
                act.wait_ge(v_done, c * 2 + i + 1)
                wait(act, v_stored[b], (c // 2) * 16)
                nc.scalar.copy(vx[:, b, 2 * i:2 * i + 2, :], psV[i][:].rearrange("p (s d) -> p s d", s=2)).then_inc(v_ready, 1)

            def step(c, b, now, ahead):
                more = not isinstance(c, int) or c + 1 < CH
                if now:
                    high(c, 0)
                    high(c, 1)
                    middle(c, 0)
                    copy_values(c, b, 0)
                    if more:
                        copy_turned(c + 1)
                    high(c, 2)
                    middle(c, 1)
                    high(c, 3)
                    middle(c, 2)
                    if more:
                        copy_latents(c + 1, 1 - b)
                    middle(c, 3)
                    copy_values(c, b, 1)
                elif c == -1:
                    copy_turned(0)
                    copy_latents(0, 0)
                if ahead:
                    ln.deviation(act, c + 2)
            steps(act, step)


def score_units():
    units = []
    for h in range(HG):
        for i in range(QT):
            end = (i + 1) * P
            units.append((h, i, 0, min(end, 512), i))
            if end > 512:
                units.append((h, i, 512, end - 512, i + QT // 2))
    return units


def plan_step(units, later, with_before):
    width = lambda j, c: min((c + 1) * 512, S) - max(c * 512, j * P)
    ring = [("s", u, 1) for u in range(AHEAD, len(units))] + [("m", 1)] if later else []
    if later > 1:
        ring += [("s", u, 2) for u in range(AHEAD)]
    if with_before:
        at = 4 if later else 0
        ring[at:at] = [("o", c) for c in range(2)]
    st = [("st", j, c, h) for j in range(QT) for c in range(2) for h in range(HG) if width(j, c) > 0]
    pv = [("pv", j, c) for j in range(QT) for c in range(2) if width(j, c) > 0]
    need_s = sum(units[x[1]][3] for x in ring if x[0] == "s") or 1
    need_t = sum(width(x[1], x[2]) for x in st)
    order, ring_free, st_free = [], [0.0] * RING_BANKS, [0.0] * ST_BANKS
    exp_end, pv_end = {}, {}
    t = dve = act = had_s = had_t = 0.0
    n_ring = n_st = n_pv = 0
    while n_ring < len(ring) or n_st < len(st) or n_pv < len(pv):
        can = []
        if n_ring < len(ring):
            can.append((max(t, ring_free[n_ring % RING_BANKS]), had_s / need_s, "r"))
        if n_st < len(st):
            _, j, c, h = st[n_st]
            slot_free = pv_end.get((j - 2, c), 0.0 if j < 2 else float("inf"))
            can.append((max(t, st_free[n_st % ST_BANKS], slot_free - 300), had_t / need_t, "t"))
        if n_pv < len(pv):
            _, j, c = pv[n_pv]
            ready = max(exp_end.get((j, c, h), float("inf")) for h in range(HG))
            can.append((max(t, ready), 0.0, "p"))
        start, _, what = min(can)
        if what == "r":
            kind, u = ring[n_ring][:2]
            w = units[u][3] if kind == "s" else 512
            t = start + w / 2.4
            dve = max(dve, t + READER_LATENCY) + 64 + (w if kind == "s" else 900) * 1.04
            ring_free[n_ring % RING_BANKS] = dve + 60
            had_s += units[u][3] if kind == "s" else 0
            order.append(ring[n_ring])
            n_ring += 1
        elif what == "t":
            _, j, c, h = st[n_st]
            w = width(j, c)
            t = start + (w + P * (max(c * 512, j * P) == j * P)) / 2.4
            act = max(act, t + READER_LATENCY) + 100 + w * 0.833
            st_free[n_st % ST_BANKS] = act + 60
            exp_end[j, c, h] = act + 100
            had_t += w
            order.append(st[n_st])
            n_st += 1
        else:
            _, j, c = pv[n_pv]
            t = start + width(j, c) * 4 / 2.4
            pv_end[j, c] = t + 150
            order.append(pv[n_pv])
            n_pv += 1
    return order, [x for x in order if x[0] in "smo"]


def phase_attention(nc, T, tag, A, o_dram):
    with ExitStack() as ctx:
        M = Mem(nc, ctx, tag)
        units = score_units()
        NS = len(units)
        QHALF = QT // 2
        MROW = HG * QT
        n_pv = {(j, c): n for n, (j, c) in enumerate((j, c) for j in range(QT) for c in range(2) if j < QHALF * (c + 1))}
        n_st = {(j, c, h): n * HG + h for (j, c), n in n_pv.items() for h in range(HG)}
        PV, ST = len(n_pv), len(n_st)
        qst, kst, v_rows, loaded, N_LOADS = A.qst, A.kst, A.v_rows, A.loaded, A.N_LOADS
        vst = [M.sb(f"vst{s}", [P, QT, HG * VW]) for s in range(SLOTS)]
        prob = [M.sb(f"prob{i}", [P, HG, S]) for i in range(2)]
        maxp = M.sb("maxp", [P, HG, QT + QHALF])
        maxq = M.sb("maxq", [P, HG, QT])
        neg, mid = M.sb("neg", [MROW, P]), M.sb("mid", [MROW, P])
        mparts = M.sb("mparts", [MROW, PARTS, P], BF16)
        oT = M.sb("oT", [P, 2, 512])
        orow = M.sb("orow", [P, 2, 512 // VW, OW])
        psR = [M.ps(f"psR{i}", [P, 512]) for i in range(RING_BANKS)]
        psS = [M.ps(f"psS{i}", [P, 512]) for i in range(ST_BANKS)]
        psO = [M.ps(f"psO{i}", [P, 512]) for i in range(2)]
        o_stored = [M.sem(f"o_stored{c}") for c in range(2)]
        m_loaded, filled, drained, max_ready, m_ready, st_done, exp_done, pv_done, o_copied, pool_done, chain = (
            M.sem(n) for n in ("m_loaded", "filled", "drained", "max_ready", "m_ready", "st_done", "exp_done", "pv_done",
                               "o_copied", "pool_done", "chain"))
        RING0 = NS + 1 + AHEAD
        RING = NS + 3
        POOL0 = 3 * SLOTS
        CHAIN = 4
        assert RING % RING_BANKS == 0 and ST % ST_BANKS == 0
        block = ctx.enter_context(nc.Block())

        def steps(step):
            def run(eng):
                last = (NG - 1) // SLOTS - 1
                for k in range(SLOTS):
                    step(k, k, 2, k > 0)
                with eng.Fori(1, last) as it:
                    for k in range(SLOTS):
                        step(it * SLOTS + k, k, 2, True)
                for g in range(last * SLOTS, NG):
                    step(g, g % SLOTS, min(2, NG - 1 - g), True)
            return run

        def ring_base(g):
            if isinstance(g, int) and g == 0:
                return RING0
            return g * RING + (RING0 - 2 - (AHEAD if isinstance(g, int) and g == NG - 1 else 0))

        def ring_bank(g, idx):
            return (idx + (ring_base(g) if isinstance(g, int) else RING0 - 2)) % RING_BANKS

        def out_at(g, c):
            if isinstance(g, int) and g == NG - 1:
                return ring_base(g) + 2 + c + 1
            later = min(2, NG - 2 - g) if isinstance(g, int) else 2
            return ring_base(g + 1) + (plan_step(units, later, True)[1].index(("o", c)) + 1)

        @block.sync
        def _(sp):
            def store_out(g):
                b, hg = g // A.GB, g % A.GB
                for c in range(2):
                    hold(sp, drained, out_at(g, c), T)
                    dst = o_dram[bass.ds(b * S + c * 512, 512), bass.ds(hg * (HG * OW), HG * OW)]
                    sp.dma_start(dst.rearrange("(i p) w -> p i w", p=P),
                                 orow[:, c].rearrange("p (i h) w -> p i (h w)", h=HG)).then_inc(o_stored[c], 16)

            def load_max(g, slot):
                hold(sp, m_ready, g + 1, T)
                for part in range(PARTS):
                    sp.dma_start(qst[slot][KROWS + part:KROWS + part + 1, :, :], mparts[:, part, :]).then_inc(m_loaded, 16)

            def step(g, k, later, with_before):
                if with_before:
                    store_out(g - 1)
                if later:
                    load_max(g + 1, (k + 1) % SLOTS)
                if not isinstance(g, int) or g + SLOTS < NG:
                    hold(sp, pv_done, g * PV + PV, T)
                    A.load(sp, g + SLOTS, k)

            for g in range(1, SLOTS):
                A.load(sp, g, g)
            load_max(0, 0)
            steps(step)(sp)
            store_out(NG - 1)
            for c in range(2):
                sp.wait_ge(o_stored[c], 16 * NG)

        def heads(rows, width):
            return rows[:].rearrange("p j (h w) -> p (j h) w", w=width)

        @block.gpsimd
        def _(pool):
            first = Chain(pool, pool_done)
            for s in range(SLOTS):
                first.link(nc.gpsimd.memset(kst[s][KROWS:MROWS, :, :], 1.0))
                first.link(nc.gpsimd.memset(vst[s][:], 0.0))
                first.link(nc.gpsimd.memset(heads(vst[s], VW)[:, :, DK:DK + 1], 1.0))

            def step(g, k, later, with_before):
                hold(pool, loaded[k], ((g - k) // SLOTS) * (16 * N_LOADS) + 16 * N_LOADS, T)
                hold(pool, pool_done, g + POOL0, T)
                nc.gpsimd.tensor_copy(heads(vst[k], VW)[:, :, 0:DK], heads(v_rows[k], DK)).then_inc(pool_done, 1)

            steps(step)(pool)

        @block.tensor
        def _(pe):
            def score(u, slot, r, bank):
                h, i, k0, w, _ = units[u]
                wait(pe, drained, r + 1 - RING_BANKS)
                nc.tensor.matmul(psR[bank][:, 0:w], qst[slot][0:KROWS, h, i * P:(i + 1) * P],
                                 kst[slot][0:KROWS, h, k0:k0 + w], start=True, stop=True).then_inc(filled, 1)

            def turn_max(g, r, bank):
                wait(pe, drained, r + 1 - RING_BANKS)
                pe.wait_ge(max_ready, g + 1)
                nc.tensor.transpose(psR[bank][0:MROW, 0:P], maxq[:].rearrange("p h i -> p (h i)"), T.ident[:]).then_inc(filled, 1)

            def turn_out(g, c, r, bank):
                wait(pe, drained, r + 1 - RING_BANKS)
                pe.wait_ge(o_copied, g * 2 + c + 1)
                for i in range(512 // P):
                    ins = nc.tensor.transpose(psR[bank][:, i * P:(i + 1) * P], oT[:, c, i * P:(i + 1) * P], T.ident[:])
                ins.then_inc(filled, 1)

            def score_t(g, k, j, c, h):
                n, a = n_st[j, c, h], max(c * 512, j * P)
                ps = psS[n % ST_BANKS][:, a - c * 512:512]
                wait(pe, exp_done, g * ST + n + 1 - ST_BANKS)
                ins = nc.tensor.matmul(ps, kst[k][0:MROWS, h, j * P:(j + 1) * P], qst[k][0:MROWS, h, a:(c + 1) * 512],
                                       start=True, stop=a > j * P)
                if a == j * P:
                    ins = nc.tensor.matmul(ps[:, 0:P], T.ident_bf[:], T.causal_t[:], start=False, stop=True)
                ins.then_inc(st_done, 1)

            def pv(g, k, j, c):
                a = max(c * 512, j * P)
                pe.wait_ge(exp_done, g * ST + n_st[j, c, HG - 1] + 1)
                if j == 0 and c == 0:
                    pe.wait_ge(pool_done, g + (POOL0 + 1))
                if j == 0:
                    wait(pe, o_copied, g * 2 + c - 1)
                for h in range(HG):
                    ins = nc.tensor.matmul(psO[c][h * VW:(h + 1) * VW, a - c * 512:512],
                                           vst[k][:, j, h * VW:(h + 1) * VW], prob[j % 2][:, h, a:(c + 1) * 512],
                                           start=(j == 0), stop=(j == QHALF * (c + 1) - 1))
                ins.then_inc(pv_done, 1)

            def step(g, k, later, with_before):
                base, idx, asked = ring_base(g), 0, False
                pe.wait_ge(m_loaded, g * (16 * PARTS) + 16 * PARTS)
                for what, *at in plan_step(units, later, with_before)[0]:
                    if what == "st":
                        score_t(g, k, *at)
                        continue
                    if what == "pv":
                        pv(g, k, *at)
                        continue
                    r, bank = base + idx, ring_bank(g, idx)
                    if what == "s":
                        u, ahead = at
                        if ahead == 2 and not asked:
                            pe.wait_ge(loaded[(k + 2) % SLOTS],
                                       ((g - k) // SLOTS) * (16 * N_LOADS) + 16 * N_LOADS * ((k + 2) // SLOTS + 1))
                            asked = True
                        score(u, (k + ahead) % SLOTS, r, bank)
                    elif what == "m":
                        turn_max(g + 1, r, bank)
                    else:
                        turn_out(g - 1, at[0], r, bank)
                    idx += 1

            pe.wait_ge(loaded[0], 16 * N_LOADS)
            for u in range(NS):
                score(u, 0, u, u % RING_BANKS)
            turn_max(0, NS, NS % RING_BANKS)
            pe.wait_ge(loaded[1], 16 * N_LOADS)
            for u in range(AHEAD):
                score(u, 1, NS + 1 + u, (NS + 1 + u) % RING_BANKS)
            pe.wait_ge(pool_done, POOL0)
            steps(step)(pe)
            for c in range(2):
                turn_out(NG - 1, c, out_at(NG - 1, c) - 1, ring_bank(NG - 1, 2 + c))

        @block.scalar
        def _(act):
            def copy_out(g, c):
                act.wait_ge(pv_done, g * PV + n_pv[QHALF * (c + 1) - 1, c] + 1)
                nc.scalar.copy(oT[:, c, :], psO[c][:]).then_inc(o_copied, 1)

            def step(g, k, later, with_before):
                for (j, c), n in n_pv.items():
                    if j > 1:
                        act.wait_ge(pv_done, g * PV + n_pv[j - 2, c] + 1)
                    else:
                        wait(act, pv_done, (g - 1) * PV + n_pv[j + QHALF * (c + 1) - 2, c] + 1)
                    for h in range(HG):
                        n, a = n_st[j, c, h], max(c * 512, j * P)
                        act.wait_ge(st_done, g * ST + n + 1)
                        nc.scalar.activation(prob[j % 2][:, h, a:(c + 1) * 512], psS[n % ST_BANKS][:, a - c * 512:512], ACT.Exp,
                                             scale=DK ** -0.5).then_inc(exp_done, 1)
                    if j == QHALF + 1:
                        copy_out(g, 0)
                copy_out(g, 1)

            steps(step)(act)

        @block.vector
        def _(dve):
            def link(ins, g, n):
                ins.then_inc(chain, 1)
                dve.wait_ge(chain, g * CHAIN + n)

            def row_max(u, r, bank):
                h, i, k0, w, col = units[u]
                if k0 + w == (i + 1) * P:
                    hold(dve, filled, r + 1, T)
                    ins = nc.vector.tensor_tensor_reduce(psR[bank][:, 0:w], psR[bank][:, 0:w], T.causal[:, 512 - w:512], 1.0, -BIG,
                                                         ALU.add, ALU.max, maxp[:, h, col:col + 1])
                else:
                    dve.wait_ge(filled, r + 1)
                    ins = nc.vector.tensor_reduce(maxp[:, h, col:col + 1], psR[bank][:, 0:w], AX_X, ALU.max)
                ins.then_inc(drained, 1)

            def join_max(g, r):
                dve.wait_ge(drained, r)
                link(nc.vector.tensor_copy(maxq[:, :, 0:QHALF], maxp[:, :, 0:QHALF]), g, 1)
                nc.vector.tensor_tensor(maxq[:, :, QHALF:QT], maxp[:, :, QHALF:QT], maxp[:, :, QT:QT + QHALF],
                                        ALU.max).then_inc(max_ready, 1)

            def split_max(g, r, bank):
                dve.wait_ge(filled, r + 1)
                wait(dve, m_loaded, g * (16 * PARTS))
                nc.vector.tensor_scalar(neg[:], psR[bank][0:MROW, 0:P], -1.0, None, ALU.mult).then_inc(drained, 1)
                dve.wait_ge(drained, r + 1)
                link(nc.vector.tensor_copy(mparts[:, 0], neg[:]), g, 2)
                link(nc.vector.tensor_tensor(mid[:], neg[:], mparts[:, 0], ALU.subtract), g, 3)
                link(nc.vector.tensor_copy(mparts[:, 1], mid[:]), g, 4)
                nc.vector.tensor_tensor(mparts[:, 2], mid[:], mparts[:, 1], ALU.subtract).then_inc(m_ready, 1)

            def copy_rows(g, c, r, bank):
                dve.wait_ge(filled, r + 1)
                wait(dve, o_stored[c], g * 16)
                nc.vector.tensor_copy(orow[:, c], psR[bank][:].rearrange("p (x w) -> p x w", w=VW)[:, :, 0:OW]).then_inc(drained, 1)

            def step(g, k, later, with_before):
                base = ring_base(g)
                for idx, (what, at, *_) in enumerate(plan_step(units, later, with_before)[1]):
                    r, bank = base + idx, ring_bank(g, idx)
                    if what == "s":
                        row_max(at, r, bank)
                    elif what == "m":
                        join_max(g + 1, r)
                        split_max(g + 1, r, bank)
                    else:
                        copy_rows(g - 1, at, r, bank)

            for u in range(NS):
                row_max(u, u, u % RING_BANKS)
            join_max(0, NS)
            split_max(0, NS, NS % RING_BANKS)
            for u in range(AHEAD):
                row_max(u, NS + 1 + u, (NS + 1 + u) % RING_BANKS)
            steps(step)(dve)
            for c in range(2):
                copy_rows(NG - 1, c, out_at(NG - 1, c) - 1, ring_bank(NG - 1, 2 + c))


class Tables:
    pass


def phase_constants(nc, T, M):
    T.ident, T.ident_bf = M.sb("ident", [P, P]), M.sb("ident_bf", [P, P], BF16)
    T.causal, T.causal_t = M.sb("causal", [P, 512]), M.sb("causal_t", [P, P], BF16)
    T.lower_bf, T.ones_bf, T.ones_f = M.sb("lower_bf", [P, P], BF16), M.sb("ones_bf", [P, P], BF16), M.sb("ones_f", [P, P])
    iota_i, col_i = M.sb("iota_i", [P, P], I32), M.sb("col_i", [P, SLOTC], I32)
    row_i, lane_i = M.sb("row_i", [P, MT], I32), M.sb("lane_i", [P, 1], I32)
    T.iota, T.eps = M.sb("iota", [P, P]), M.sb("eps", [P, 1])
    T.col_number, T.lane_number = M.sb("col_number", [P, SLOTC]), M.sb("lane_number", [P, 1])
    T.unused_row = M.sb("unused_row", [P, MT])
    made = M.sem("made")
    T.const_ready = M.sem("const_ready")
    T.N_CONST = 1
    with nc.Block() as block:
        @block.gpsimd
        def _(pool):
            g = nc.gpsimd
            c = Chain(pool, made)
            c.link(g.memset(T.ones_f[:], 1.0))
            c.link(g.memset(T.ones_bf[:], 1.0))
            c.link(g.memset(T.gateT[:], 0.0))
            c.link(g.memset(T.causal[:], 0.0))
            c.link(g.memset(T.causal_t[:], 0.0))
            square = [[1, P]]
            c.link(g.affine_select(out=T.ident[:], in_=T.ones_f[:], compare_op=ALU.is_equal, fill=0.0, base=0,
                                   pattern=square, channel_multiplier=-1))
            c.link(g.affine_select(out=T.ident_bf[:], in_=T.ones_bf[:], compare_op=ALU.is_equal, fill=0.0, base=0,
                                   pattern=square, channel_multiplier=-1))
            c.link(g.affine_select(out=T.lower_bf[:], in_=T.ones_bf[:], compare_op=ALU.is_gt, fill=0.0, base=0,
                                   pattern=square, channel_multiplier=-1))
            c.link(g.affine_select(out=T.causal[:, 512 - P:], in_=T.causal[:, 512 - P:], compare_op=ALU.is_ge, fill=NEG, base=0,
                                   pattern=[[-1, P]], channel_multiplier=1))
            c.link(g.affine_select(out=T.causal_t[:], in_=T.causal_t[:], compare_op=ALU.is_ge, fill=NEG, base=0,
                                   pattern=square, channel_multiplier=-1))
            c.link(g.iota(iota_i[:], [[1, P]], base=0, channel_multiplier=0))
            c.link(g.iota(col_i[:], [[P, SLOTC]], base=0, channel_multiplier=0))
            c.link(g.iota(lane_i[:], [[0, 1]], base=1, channel_multiplier=1))
            c.link(g.iota(row_i[:], [[P, MT]], base=TOPK * N + 1, channel_multiplier=1))
            c.link(g.memset(T.eps[:], EPS))
            c.link(g.tensor_copy(T.iota[:], iota_i[:]))
            c.link(g.tensor_copy(T.col_number[:], col_i[:]))
            c.link(g.tensor_copy(T.lane_number[:], lane_i[:]))
            g.tensor_copy(T.unused_row[:], row_i[:]).then_inc(T.const_ready, 1)



class Routing:

    def __init__(self, M, k):
        self.weight = M.sb(f"weight{k}", [P, TOPK, NT])
        self.token = M.sb(f"token{k}", [P, MT], I32)
        self.slot = M.sb(f"slot{k}", [P, MT], I32)
        self.expert = M.sb(f"expert{k}", [1, MT], I32)


def program(nc, x, W_dq, W_uq, W_dkv, W_uk, W_uv, W_o, gate, gate_up, down, similarity, out):
    with ExitStack() as ctx:
        M = Mem(nc, ctx, "all")
        T = Tables()
        xs = M.sb("x", [P, NT, D])
        logits = M.sb("logits", [P, NT, E])
        R = Routing(M, 0)
        T.gateT, T.simb = M.sb("gateT", [P, DC, EP]), M.sb("simb", [P, E, E])
        T.wdown = M.sb("wdown", [P, DC, 2 * DL])
        T.wup, T.wuv = M.sb("wup", [P, D]), M.sb("wuv", [P, D])
        T.wo = M.sb("wo", [P, DC, D])
        T.w_loaded, T.gate_loaded = M.sem("w_loaded"), M.sem("gate_loaded")
        T.x_loaded = [M.sem(f"x_loaded{i}") for i in range(3)]
        T.holds_passed = {e.engine: M.sem(n) for e, n in ((nc.gpsimd, "pool_holds"), (nc.sync, "sp_holds"), (nc.vector, "dve_holds"))}
        xn_dram = nc.dram_tensor("xn_rows", (N, D), F32).ap()
        y_dram = nc.dram_tensor("y_rows", (TOPK * N + MT * P, D), F32).ap()
        qk_dram = nc.dram_tensor("qk_parts", (2, PARTS, D, N), BF16).ap()
        v_dram = nc.dram_tensor("v_rows", (N, D), F32).ap()
        o_dram = nc.dram_tensor("o_rows", (N, H * OW), F32).ap()
        phase_constants(nc, T, M)
        x_view = x.rearrange("(n p) d -> p n d", p=P)
        split = lambda w: w.rearrange("(c p) n -> p c n", p=P)
        weights = [(T.simb[:].rearrange("p a b -> p (a b)"), similarity.partition_broadcast(P)),
                   (T.wdown[:, :, 0:DL], split(W_dq)), (T.wdown[:, :, DL:2 * DL], split(W_dkv)),
                   (T.wup[0:DL, :], W_uq), (T.wup[DL:2 * DL, :], W_uk), (T.wuv[DL:2 * DL, :], W_uv), (T.wo[:], split(W_o))]
        T.N_W = 16 * len(weights)
        assert E == NT // U and D == F and U * EP == P

        def load_x(sp, pair):
            if isinstance(pair, int) and pair == 0:
                sp.dma_start(T.gateT[:, :, 0:E], split(gate)).then_inc(T.gate_loaded, 16)
                for c in range(2):
                    n = slice(c * U, (c + 1) * U)
                    sp.dma_start(xs[:, n, :], x_view[:, n, :]).then_inc(T.x_loaded[c], 16)
                return
            hold(sp, T.x_loaded[2], (pair - 1) * 16, T)
            n = bass.ds(pair * (2 * U), 2 * U)
            sp.dma_start(xs[:, n, :], x_view[:, n, :]).then_inc(T.x_loaded[2], 16)

        def load_others(sp):
            for dst, src in weights:
                sp.dma_start(dst, src).then_inc(T.w_loaded, 16)

        def moe(tag, o_rows, *loads):
            with ExitStack() as layer:
                W = Weights(nc, T, Mem(nc, layer, tag), gate_up, down)
                phase_logits(nc, T, tag + "l", xs, xn_dram, logits, W, o_rows, *loads)
                phase_route(nc, T, tag + "r", logits, R, W)
                phase_experts(nc, T, tag + "e", R, W, xn_dram, y_dram)

        moe("a", None, load_x, load_others)
        with ExitStack() as both:
            A = Stacks(Mem(nc, both, "stacks"), qk_dram, v_dram)
            phase_qkv(nc, T, "q", R, xs, y_dram, A)
            phase_attention(nc, T, "t", A, o_dram)
        moe("b", o_dram)
        phase_sum(nc, T, "s", R, xs, y_dram, out)


def kernel(L0_attn_x, L0_attn_W_dq, L0_attn_W_uq, L0_attn_W_dkv, L0_attn_W_uk, L0_attn_W_uv, L0_attn_W_o, L0_ffn_gate_weight,
           L0_ffn_gate_up_proj, L0_ffn_down_proj, L0_ffn_similarity_matrix):
    import concourse.bacc as bacc
    import numpy as np
    from concourse.bass_utils import run_bass_kernel_spmd

    rows = np.ascontiguousarray
    arrays = {
        "x": rows(L0_attn_x).reshape(N, D),
        "w_dq": rows(L0_attn_W_dq), "w_uq": rows(L0_attn_W_uq), "w_dkv": rows(L0_attn_W_dkv),
        "w_uk": rows(L0_attn_W_uk), "w_uv": rows(L0_attn_W_uv), "w_o": rows(L0_attn_W_o),
        "gate": rows(np.transpose(L0_ffn_gate_weight)),
        "gate_up": rows(np.transpose(L0_ffn_gate_up_proj, (0, 2, 1))),
        "down": rows(np.transpose(L0_ffn_down_proj, (0, 2, 1))),
        "similarity": rows(L0_ffn_similarity_matrix).reshape(E * E),
    }
    nc = bacc.Bacc("TRN2", target_bir_lowering=False, num_devices=1)
    args = [nc.dram_tensor(f"in_{k}", a.shape, mybir.dt.from_np(a.dtype), kind="ExternalInput").ap() for k, a in arrays.items()]
    out = nc.dram_tensor("out_rows", (N, D), F32, kind="ExternalOutput").ap()
    program(nc, *args, out)
    result = run_bass_kernel_spmd(nc, [{f"in_{k}": a for k, a in arrays.items()}], core_ids=[0])
    return result.results[0]["out_rows"].reshape(B, S, D)
```
